# Optimizing a Trainium2 kernel written in Bass

```python
import numpy as np
import jax
import jax.numpy as jnp

def _softmax(x, axis=-1):
    return jax.nn.softmax(x, axis=axis)

def _gelu(x):
    return jax.nn.gelu(x, approximate=True)

def _silu(x):
    return jax.nn.silu(x)

def _sigmoid(x):
    return jax.nn.sigmoid(x)

def _layernorm(x, axis=-1, eps=1e-05):
    m = jnp.mean(x, axis=axis, keepdims=True)
    v = jnp.var(x, axis=axis, keepdims=True)
    return (x - m) / jnp.sqrt(v + eps)

def _scatter_add(tgt, idx, src, axis=0):
    return tgt.at[idx].add(src)

def _segment_sum(src, seg, n):
    return jax.ops.segment_sum(src, seg, n)
kernel_name = 'mk_flamingo_gated_d2_seqx_r4_86c827'

def setup_inputs(seed: int=0):
    np.random.seed(seed)
    _w = jnp.asarray

    def _rec_inputs():
        import jax
        import jax.numpy as jnp
        _rk = jax.random.key(seed)
        x = 7.22e-05 + 1 * jax.random.normal(jax.random.fold_in(_rk, 1), (16, 256, 512), jnp.float32)
        _lenS = 256 - jax.random.randint(jax.random.fold_in(_rk, 7), (16,), 0, max(1, 256 // 4) + 1, jnp.int32)
        _lenS2 = 256 - jax.random.randint(jax.random.fold_in(_rk, 8), (16,), 0, max(1, 256 // 4) + 1, jnp.int32)
        _ctx_2048P = jax.random.normal(jax.random.fold_in(_rk, 11), (16, 16, 512), jnp.float32)
        _ctx_2048c = jax.random.dirichlet(jax.random.fold_in(_rk, 511), 0.3 * jnp.ones((16,), jnp.float32), (16, 256))
        _ctx_2048t = jnp.einsum('bsk,bkd->bsd', _ctx_2048c, _ctx_2048P)
        _ctx_2048t = _ctx_2048t * jax.lax.rsqrt(jnp.mean(jnp.square(_ctx_2048t)) + 1e-12) * 0.953939
        ctx_2048 = 4.13588e-05 + 0.999923 * (_ctx_2048t + 0.3 * jax.random.normal(jax.random.fold_in(_rk, 611), (16, 256, 512), jnp.float32))
        _g = jax.random.normal(jax.random.fold_in(_rk, 9001), (2, 2), jnp.float32)
        _g = jnp.sign(_g) * jnp.maximum(jnp.abs(_g), 1.0) + (_g == 0) * 1.0
        g_xattn = _g[0]
        g_ffn = _g[1]
        return (x, ctx_2048, g_xattn, g_ffn)
    x, ctx_2048, g_xattn, g_ffn = _rec_inputs()

    def _L0_xattn_setup():
        import jax, jax.numpy as jnp
        import numpy as np
        B, S, DIM, HD = (4, 256, 512, 128)
        H = DIM // HD
        GN_EPS = 0.001

        def _decay_masks(n_heads, seq_len):
            gam = 1.0 - 2.0 ** (-5.0 - jnp.arange(n_heads, dtype=jnp.float32))
            idx = jnp.arange(seq_len, dtype=jnp.float32)
            expo = idx[None, :] - idx[:, None]
            D = jnp.where(expo[None, :, :] <= 0, gam[:, None, None] ** expo[None, :, :], 0.0)
            return D / jnp.sqrt(D.sum(axis=-1))[:, None, :]
        key = jax.random.key(seed)
        ks = jax.random.split(key, 8)
        x = jax.random.normal(ks[0], (B, S, DIM), dtype=jnp.float32)
        k = jax.random.normal(ks[1], (B, S, DIM), dtype=jnp.float32)
        v = jax.random.normal(ks[2], (B, S, DIM), dtype=jnp.float32)
        Wh = jax.random.normal(ks[3], (H, HD, HD), dtype=jnp.float32) / np.sqrt(HD)
        wg_w = jax.random.normal(ks[4], (DIM, DIM), dtype=jnp.float32) / np.sqrt(DIM)
        wo_w = jax.random.normal(ks[5], (DIM, DIM), dtype=jnp.float32) / np.sqrt(DIM)
        gn_gamma = jnp.ones((DIM,), dtype=jnp.float32)
        gn_beta = jnp.zeros((DIM,), dtype=jnp.float32)
        return {'x': x, 'k': k, 'v': v, 'Wh': Wh, 'wg_w': wg_w, 'wo_w': wo_w, 'gn_gamma': gn_gamma, 'gn_beta': gn_beta}
    _L0_xattn_all = _L0_xattn_setup()
    _L0_xattn_in = {k: v for k, v in _L0_xattn_all.items() if k in ('Wh', 'wg_w', 'wo_w', 'gn_gamma', 'gn_beta')}
    del _L0_xattn_all

    def _L0_ffn_setup():
        import jax, jax.numpy as jnp
        import numpy as np
        DIM = 512
        HIDDEN = 2048
        EPS = 1e-06

        def rms_norm(x, gamma):
            var = jnp.mean(x * x, axis=-1, keepdims=True)
            return x * jax.lax.rsqrt(var + EPS) * gamma

        def activation_quant(x):
            scale = 127.0 / jnp.maximum(jnp.max(jnp.abs(x), axis=-1, keepdims=True), 1e-05)
            return jnp.clip(jnp.round(x * scale), -128.0, 127.0) / scale

        def weight_quant(w):
            scale = 1.0 / jnp.maximum(jnp.mean(jnp.abs(w)), 1e-05)
            return jnp.clip(jnp.round(w * scale), -1.0, 1.0) / scale

        def bit_linear(x, w):
            xq = x + jax.lax.stop_gradient(activation_quant(x) - x)
            wq = w + jax.lax.stop_gradient(weight_quant(w) - w)
            return jnp.einsum('bsi,oi->bso', xq, wq)
        key = jax.random.key(seed)
        k_x, k_w1, k_w2 = jax.random.split(key, 3)
        x = jax.random.normal(k_x, (4, 512, DIM), dtype=jnp.float32)
        b1 = 1.0 / np.sqrt(DIM)
        b2 = 1.0 / np.sqrt(HIDDEN)
        w1 = jax.random.uniform(k_w1, (HIDDEN, DIM), dtype=jnp.float32, minval=-b1, maxval=b1)
        w2 = jax.random.uniform(k_w2, (DIM, HIDDEN), dtype=jnp.float32, minval=-b2, maxval=b2)
        gamma = jnp.ones((DIM,), dtype=jnp.float32)
        return {'x': x, 'w1': w1, 'w2': w2, 'gamma': gamma}
    _L0_ffn_all = _L0_ffn_setup()
    _L0_ffn_in = {k: v for k, v in _L0_ffn_all.items() if k in ('w1', 'w2', 'gamma')}
    del _L0_ffn_all

    def _L1_xattn_setup():
        import jax, jax.numpy as jnp
        import numpy as np
        key = jax.random.key(seed)
        k1, k2, k3, k4, k5 = jax.random.split(key, 5)
        B, D_MODEL, L = (2, 256, 512)
        HEAD_DIM = 8
        H = D_MODEL // HEAD_DIM
        return {'k': jax.random.normal(k1, (B, D_MODEL, L), dtype=jnp.float32), 'v': jax.random.normal(k2, (B, D_MODEL, L), dtype=jnp.float32), 'q': jax.random.normal(k3, (B, D_MODEL, L), dtype=jnp.float32), 'ssm_kernel': jax.random.normal(k4, (H, L), dtype=jnp.float32), 'D': jax.random.normal(k5, (H,), dtype=jnp.float32), 'head_dim': HEAD_DIM}
    _L1_xattn_all = _L1_xattn_setup()
    _L1_xattn_in = {k: v for k, v in _L1_xattn_all.items() if k in ('ssm_kernel', 'D')}
    del _L1_xattn_all

    def _L1_ffn_setup():
        import jax, jax.numpy as jnp
        import numpy as np
        B, S, D = (4, 512, 512)
        E = 8
        N_SHARE = 2
        N_ROUTED = E - N_SHARE
        H = 2048 // E
        key = jax.random.key(seed)
        ks = jax.random.split(key, 12)
        s = 0.02
        return {'x': jax.random.normal(ks[0], (B, S, D), jnp.float32), 'Wg': jax.random.normal(ks[1], (D, E), jnp.float32) * s, 'bg': jnp.zeros((E,), jnp.float32), 'Wgate': jax.random.normal(ks[2], (N_ROUTED, D, H), jnp.float32) * s, 'bgate': jnp.zeros((N_ROUTED, H), jnp.float32), 'Wup': jax.random.normal(ks[3], (N_ROUTED, D, H), jnp.float32) * s, 'bup': jnp.zeros((N_ROUTED, H), jnp.float32), 'Wdown': jax.random.normal(ks[4], (N_ROUTED, H, D), jnp.float32) * s, 'bdown': jnp.zeros((N_ROUTED, D), jnp.float32), 'Ws_up': jax.random.normal(ks[5], (D, N_SHARE * H), jnp.float32) * s, 'bs_up': jnp.zeros((N_SHARE * H,), jnp.float32), 'Ws_down': jax.random.normal(ks[6], (N_SHARE * H, D), jnp.float32) * s, 'bs_down': jnp.zeros((D,), jnp.float32)}
    _L1_ffn_all = _L1_ffn_setup()
    _L1_ffn_in = {k: v for k, v in _L1_ffn_all.items() if k in ('Wg', 'bg', 'Wgate', 'bgate', 'Wup', 'bup', 'Wdown', 'bdown', 'Ws_up', 'bs_up', 'Ws_down', 'bs_down')}
    del _L1_ffn_all
    return {'x': x, 'ctx_2048': ctx_2048, 'g_xattn': g_xattn, 'g_ffn': g_ffn, 'L0_xattn_Wh': _L0_xattn_in['Wh'], 'L0_xattn_wg_w': _L0_xattn_in['wg_w'], 'L0_xattn_wo_w': _L0_xattn_in['wo_w'], 'L0_xattn_gn_gamma': _L0_xattn_in['gn_gamma'], 'L0_xattn_gn_beta': _L0_xattn_in['gn_beta'], 'L0_ffn_w1': _L0_ffn_in['w1'], 'L0_ffn_w2': _L0_ffn_in['w2'], 'L0_ffn_gamma': _L0_ffn_in['gamma'], 'L1_xattn_ssm_kernel': _L1_xattn_in['ssm_kernel'], 'L1_xattn_D': _L1_xattn_in['D'], 'L1_ffn_Wg': _L1_ffn_in['Wg'], 'L1_ffn_bg': _L1_ffn_in['bg'], 'L1_ffn_Wgate': _L1_ffn_in['Wgate'], 'L1_ffn_bgate': _L1_ffn_in['bgate'], 'L1_ffn_Wup': _L1_ffn_in['Wup'], 'L1_ffn_bup': _L1_ffn_in['bup'], 'L1_ffn_Wdown': _L1_ffn_in['Wdown'], 'L1_ffn_bdown': _L1_ffn_in['bdown'], 'L1_ffn_Ws_up': _L1_ffn_in['Ws_up'], 'L1_ffn_bs_up': _L1_ffn_in['bs_up'], 'L1_ffn_Ws_down': _L1_ffn_in['Ws_down'], 'L1_ffn_bs_down': _L1_ffn_in['bs_down']}

def reference(x, ctx_2048, g_xattn, g_ffn, L0_xattn_Wh, L0_xattn_wg_w, L0_xattn_wo_w, L0_xattn_gn_gamma, L0_xattn_gn_beta, L0_ffn_w1, L0_ffn_w2, L0_ffn_gamma, L1_xattn_ssm_kernel, L1_xattn_D, L1_ffn_Wg, L1_ffn_bg, L1_ffn_Wgate, L1_ffn_bgate, L1_ffn_Wup, L1_ffn_bup, L1_ffn_Wdown, L1_ffn_bdown, L1_ffn_Ws_up, L1_ffn_bs_up, L1_ffn_Ws_down, L1_ffn_bs_down):
    import jax
    import jax.numpy as jnp

    def _L0_xattn_ref(x, k, v, Wh, wg_w, wo_w, gn_gamma, gn_beta):
        import jax, jax.numpy as jnp
        import numpy as np
        B, S, DIM, HD = (4, 256, 512, 128)
        H = DIM // HD
        GN_EPS = 0.001

        def _decay_masks(n_heads, seq_len):
            gam = 1.0 - 2.0 ** (-5.0 - jnp.arange(n_heads, dtype=jnp.float32))
            idx = jnp.arange(seq_len, dtype=jnp.float32)
            expo = idx[None, :] - idx[:, None]
            D = jnp.where(expo[None, :, :] <= 0, gam[:, None, None] ** expo[None, :, :], 0.0)
            return D / jnp.sqrt(D.sum(axis=-1))[:, None, :]
        b, s, dim = x.shape
        h, hd, _ = Wh.shape
        xh = x.reshape(b, s, h, hd)
        kh = k.reshape(b, s, h, hd)
        vh = v.reshape(b, s, h, hd)
        Q = jnp.einsum('bshd,hde->bshe', xh, Wh)
        K = jnp.einsum('bshd,hde->bshe', kh, Wh)
        V = jnp.einsum('bshd,hde->bshe', vh, Wh)
        scores = jnp.einsum('bshe,bthe->bhst', Q, K) / jnp.sqrt(jnp.float32(hd))
        Dn = _decay_masks(h, s)
        masked = scores * Dn[None, :, :, :]
        A = jnp.maximum(jnp.abs(masked.sum(axis=0)), 1.0)
        O = jnp.einsum('hst,bthe->bshe', A, V).reshape(b, s, dim)
        mu = O.mean(axis=-1, keepdims=True)
        var = O.var(axis=-1, keepdims=True)
        Y = (O - mu) / jnp.sqrt(var + GN_EPS) * gn_gamma + gn_beta
        W = jax.nn.relu(x @ wg_w)
        return W * Y @ wo_w

    def _L0_ffn_ref(x, w1, w2, gamma):
        import jax, jax.numpy as jnp
        import numpy as np
        DIM = 512
        HIDDEN = 2048
        EPS = 1e-06

        def rms_norm(x, gamma):
            var = jnp.mean(x * x, axis=-1, keepdims=True)
            return x * jax.lax.rsqrt(var + EPS) * gamma

        def activation_quant(x):
            scale = 127.0 / jnp.maximum(jnp.max(jnp.abs(x), axis=-1, keepdims=True), 1e-05)
            return jnp.clip(jnp.round(x * scale), -128.0, 127.0) / scale

        def weight_quant(w):
            scale = 1.0 / jnp.maximum(jnp.mean(jnp.abs(w)), 1e-05)
            return jnp.clip(jnp.round(w * scale), -1.0, 1.0) / scale

        def bit_linear(x, w):
            xq = x + jax.lax.stop_gradient(activation_quant(x) - x)
            wq = w + jax.lax.stop_gradient(weight_quant(w) - w)
            return jnp.einsum('bsi,oi->bso', xq, wq)
        h = bit_linear(rms_norm(x, gamma), w1)
        h = jax.nn.gelu(h, approximate=False)
        return bit_linear(h, w2)

    def _L1_xattn_ref(k, v, q, ssm_kernel, D, head_dim):
        import jax, jax.numpy as jnp
        import numpy as np
        B, HD, L = k.shape
        H = HD // head_dim
        fft_size = 2 * L
        k_ = k.reshape(B, H, head_dim, L)
        v_ = v.reshape(B, H, head_dim, L)
        q_ = q.reshape(B, H, head_dim, L)
        kv = jnp.einsum('bhil,bhjl->bijhl', k_, v_)
        kv_f = jnp.fft.rfft(kv, n=fft_size)
        kernel_f = jnp.fft.rfft(ssm_kernel, n=fft_size)
        y = jnp.fft.irfft(kv_f * kernel_f, n=fft_size)[..., :L]
        out = y + kv * D[None, None, None, :, None]
        out = jnp.einsum('bijhl,bhil->bjhl', out, q_)
        out = jnp.transpose(out, (0, 2, 1, 3)).reshape(B, H * head_dim, L)
        return out.astype(k.dtype)

    def _L1_ffn_ref(x, Wg, bg, Wgate, bgate, Wup, bup, Wdown, bdown, Ws_up, bs_up, Ws_down, bs_down):
        import jax, jax.numpy as jnp
        import numpy as np
        B, S, D = (4, 512, 512)
        E = 8
        N_SHARE = 2
        N_ROUTED = E - N_SHARE
        H = 2048 // E
        b, s, d = x.shape
        T = b * s
        n = Wgate.shape[0]
        xf = x.reshape(T, d)
        gate = xf @ Wg + bg
        vals, ids = jax.lax.top_k(gate, n)
        rows = jnp.arange(T)[:, None]
        masked = jnp.full_like(gate, -jnp.inf).at[rows, ids].set(vals)
        probs = jax.nn.softmax(masked, axis=-1)
        routed_mask = (ids[:, :, None] == jnp.arange(n)).any(axis=1)
        w = probs[:, :n] * routed_mask
        g = jnp.einsum('td,ndh->tnh', xf, Wgate) + bgate
        u = jnp.einsum('td,ndh->tnh', xf, Wup) + bup
        h = jax.nn.silu(g) * u
        eo = jnp.einsum('tnh,nhd->tnd', h, Wdown) + bdown
        routed_out = jnp.einsum('tnd,tn->td', eo, w)
        share = jax.nn.silu(xf @ Ws_up + bs_up) @ Ws_down + bs_down
        return (routed_out + share).reshape(b, s, d)
    x = x + jnp.tanh(g_xattn[0]) * _L0_xattn_ref(_layernorm(x, axis=-1), ctx_2048, ctx_2048, L0_xattn_Wh, L0_xattn_wg_w, L0_xattn_wo_w, L0_xattn_gn_gamma, L0_xattn_gn_beta)
    x = x + jnp.tanh(g_ffn[0]) * _L0_ffn_ref(_layernorm(x, axis=-1), L0_ffn_w1, L0_ffn_w2, L0_ffn_gamma)
    x = x + jnp.tanh(g_xattn[1]) * _L1_xattn_ref(ctx_2048, ctx_2048, _layernorm(x, axis=-1), L1_xattn_ssm_kernel, L1_xattn_D, 8)
    x = x + jnp.tanh(g_ffn[1]) * _L1_ffn_ref(_layernorm(x, axis=-1), L1_ffn_Wg, L1_ffn_bg, L1_ffn_Wgate, L1_ffn_bgate, L1_ffn_Wup, L1_ffn_bup, L1_ffn_Wdown, L1_ffn_bdown, L1_ffn_Ws_up, L1_ffn_bs_up, L1_ffn_Ws_down, L1_ffn_bs_down)
    return x

_drawn_inputs = setup_inputs


def setup_inputs(seed=0):
    import zlib

    import numpy as np

    out = dict(_drawn_inputs(seed))
    spreads = {'g_ffn': (-1.0, 0.6),
     'L0_xattn_gn_gamma': (1.0, 0.2),
     'L0_xattn_gn_beta': (0.0, 0.1),
     'L0_ffn_gamma': (1.0, 0.6),
     'L1_ffn_bg': (0.0, 0.8),
     'L1_ffn_bgate': (0.0, 0.8),
     'L1_ffn_bup': (0.0, 0.8),
     'L1_ffn_bdown': (0.0, 0.8),
     'L1_ffn_bs_up': (0.0, 0.8),
     'L1_ffn_bs_down': (0.0, 0.8)}
    factors = {'L1_ffn_Wg': 8.0,
     'L1_ffn_Wgate': 8.0,
     'L1_ffn_Wup': 8.0,
     'L1_ffn_Wdown': 8.0,
     'L1_ffn_Ws_up': 8.0,
     'L1_ffn_Ws_down': 8.0}
    for name, (base, spread) in spreads.items():
        noise = np.random.default_rng([zlib.crc32(name.encode()), seed]).standard_normal(out[name].shape)
        drawn = base * np.exp(spread * noise) if base else spread * noise
        out[name] = jnp.asarray(drawn.astype(out[name].dtype))
    for name, factor in factors.items():
        out[name] = (out[name] * factor).astype(out[name].dtype)
    return out
```

```python
from contextlib import ExitStack

import concourse.bass as bass
from concourse import mybir

F32 = mybir.dt.float32
F32R = mybir.dt.float32r
BF16 = mybir.dt.bfloat16
ACT = mybir.ActivationFunctionType
ALU = mybir.AluOpType
AX = mybir.AxisListType

P = 128
B, S, D = 16, 256, 512
KT = D // P
HEADS = 4
CH = 512
NCH = B * S // CH
TJ = CH // P
HID = 2048
HT = HID // P
START = 1
ROUND = 1.5 * 2.0 ** 23
LN_EPS, GN_EPS, RMS_EPS = 1e-5, 1e-3, 1e-6
QMAX = 127.0
NE, EH = 6, 256
SH = 512
CD = 8
CHD = 4
PAIRS = 36
EXT = 12
STEPS = (NE * EH + SH) // P
RSTEPS = NE * EH // P
V_GAIN, V_GAMMA, V_BETA, V_BG, V_BU, V_BSU, V_BSD, V_BGATE = 0, 4, 8, 12, 24, 36, 40, 44
V_COLS = 52


def f32(ap):
    return ap.bitcast(F32)


def products(nc, out, w_hi, w_lo, x_hi, x_lo, first, last, skip=False):
    nc.tensor.matmul(out, w_hi, x_hi, start=first, stop=False, skip_group_check=skip)
    nc.tensor.matmul(out, w_hi, x_lo, start=False, stop=False, skip_group_check=skip)
    return nc.tensor.matmul(out, w_lo, x_hi, start=False, stop=last, skip_group_check=skip)


def variance(nc, dve, stats, mom, var, eps, step, done):
    nc.vector.tensor_tensor(mom[:, 0], stats[:, :, 1], stats[:, :, 4], ALU.add).then_inc(step, 1)
    nc.vector.tensor_tensor(mom[:, 1], stats[:, :, 1], stats[:, :, 4], ALU.subtract).then_inc(step, 1)
    nc.vector.tensor_tensor(mom[:, 2], stats[:, :, 2], stats[:, :, 5], ALU.add).then_inc(step, 1)
    dve.wait_ge(step, done + 3)
    nc.vector.scalar_tensor_tensor(out=mom[:, 3], in0=mom[:, 1], scalar=0.25, in1=mom[:, 1], op0=ALU.mult,
                                   op1=ALU.mult).then_inc(step, 1)
    nc.vector.tensor_scalar(mom[:, 4], mom[:, 2], 1.0 / D, eps, ALU.mult, ALU.add).then_inc(step, 1)
    dve.wait_ge(step, done + 5)
    nc.vector.tensor_tensor(var, mom[:, 3], mom[:, 4], ALU.add).then_inc(step, 1)


def setup_block(nc, ctx, dram, keep):
    st = ctx.enter_context(ExitStack())
    sb = lambda n, s, d=F32: st.enter_context(nc.sbuf_tensor(n, s, d))
    sem = lambda n: ctx.enter_context(nc.semaphore(n))
    raw1 = sb("raw1", [P, KT, HID])
    raw2 = sb("raw2", [P, HT, D])
    raw_wo = sb("raw_wo", [P, KT, D])
    raw_wg = sb("raw_wg", [P, KT, D])
    raw_wh = sb("raw_wh", [P, HEADS, P])
    raw_wht = sb("raw_wht", [P, HEADS, P])
    wht_hi, wht_lo = sb("wht_hi", [P, HEADS, P], F32R), sb("wht_lo", [P, HEADS, P], F32R)
    ones = sb("ones_f32", [P, P])
    wsum = sb("wsum", [P, 2])
    wrec = sb("wrec", [P, 2])
    ps_mean = st.enter_context(nc.psum_tensor("ps_mean", [P, 512], F32))
    ps_g = st.enter_context(nc.psum_tensor("ps_g", [P, 512], F32))
    vecs_in, ident_in, gam_in, wo_in, wg_in, wh_in, w1_in, w2_in, mask_in = (
        sem(n) for n in ("vecs_in", "ident_in", "gam_in", "wo_in", "wg_in", "wh_in", "w1_in", "w2_in", "mask_in"))
    gains_done, hi_done, lo_done, g_done, ghi_done, glo_done, ones_done, sum_done, mean_done, scale_done, clip_done = (
        sem(n) for n in ("gains_done", "hi_done", "lo_done", "g_done", "ghi_done", "glo_done", "ones_done", "sum_done",
                         "mean_done", "scale_done", "clip_done"))
    identb_done = sem("identb_done")
    cuts = [(raw_wht, wht_hi, wht_lo, wh_in, 32), (raw_wh, keep["wh_hi"], keep["wh_lo"], wh_in, 32),
            (raw_wg, keep["wg_hi"], keep["wg_lo"], wg_in, 16), (raw_wo, keep["wo_hi"], keep["wo_lo"], wo_in, 16)]
    block = st.enter_context(nc.Block())

    @block.sync
    def _(sp):
        sp.dma_start(raw_wht[:], dram["whT"].rearrange("h e d -> e h d")).then_inc(wh_in, 16)
        sp.dma_start(raw_wh[:], dram["wh"].rearrange("h d e -> d h e")).then_inc(wh_in, 16)
        sp.dma_start(raw_wg[:], dram["wg"].rearrange("(k p) n -> p k n", p=P)).then_inc(wg_in, 16)
        sp.dma_start(raw1[:], dram["w1T"].rearrange("(k p) n -> p k n", p=P)).then_inc(w1_in, 16)
        sp.dma_start(raw2[:], dram["w2T"].rearrange("(k p) n -> p k n", p=P)).then_inc(w2_in, 16)

    @block.scalar
    def _(act):
        act.dma_start(keep["vecs"][:], dram["vecs"]).then_inc(vecs_in, 16)
        act.dma_start(keep["ident"][:], dram["ident"]).then_inc(ident_in, 16)
        act.dma_start(raw_wo[:], dram["wo"].rearrange("(k p) n -> p k n", p=P)).then_inc(wo_in, 16)
        act.dma_start(keep["mask"][:], dram["mask"]).then_inc(mask_in, 16)
        act.dma_start(keep["gam"][:], dram["gam"]).then_inc(gam_in, 16)
        act.wait_ge(vecs_in, 16)
        nc.scalar.activation(keep["gains"][:], keep["vecs"][:, V_GAIN:V_GAIN + 4], ACT.Tanh).then_inc(gains_done, 1)
        for raw, hi, lo, arrived, n in cuts:
            act.wait_ge(arrived, n)
            nc.scalar.activation(hi[:], raw[:], ACT.Copy).then_inc(hi_done, 1)
        act.wait_ge(g_done, 1)
        nc.scalar.activation(keep["g_hi"][:], ps_g[:].rearrange("p (h d) -> p h d", h=HEADS), ACT.Copy).then_inc(ghi_done, 1)
        act.wait_ge(mask_in, 16)
        act.wait_ge(gam_in, 16)

    @block.gpsimd
    def _(pool):
        nc.gpsimd.memset(ones[:], 1.0).then_inc(ones_done, 1)
        pool.wait_ge(ident_in, 16)
        nc.gpsimd.tensor_copy(keep["identb"][:], keep["ident"][:]).then_inc(identb_done, 1)

    @block.vector
    def _(dve):
        for n, (raw, hi, lo, arrived, _) in enumerate(cuts):
            dve.wait_ge(hi_done, n + 1)
            nc.vector.tensor_tensor(lo[:], raw[:], f32(hi[:]), ALU.subtract).then_inc(lo_done, 1)
        dve.wait_ge(ghi_done, 1)
        nc.vector.tensor_tensor(keep["g_lo"][:], ps_g[:].rearrange("p (h d) -> p h d", h=HEADS), f32(keep["g_hi"][:]),
                                ALU.subtract).then_inc(glo_done, 1)
        for n, (raw, arrived) in enumerate(((raw1, w1_in), (raw2, w2_in))):
            dve.wait_ge(arrived, 16)
            nc.vector.tensor_reduce(wsum[:, n:n + 1], raw[:].rearrange("p a b -> p (a b)"), AX.X, ALU.add,
                                    apply_absolute_value=True).then_inc(sum_done, 1)
        dve.wait_ge(mean_done, 1)
        nc.vector.tensor_scalar(keep["wmean"][:], ps_mean[:, 0:2], 1.0 / (D * HID), 1e-5, ALU.mult, ALU.max).then_inc(scale_done, 1)
        dve.wait_ge(scale_done, 1)
        nc.vector.reciprocal(wrec[:], keep["wmean"][:]).then_inc(scale_done, 1)
        dve.wait_ge(scale_done, 2)
        for n, (raw, out) in enumerate(((raw1, keep["w1q"]), (raw2, keep["w2q"]))):
            nc.vector.tensor_scalar(raw[:], raw[:], wrec[:, n:n + 1], 1.0, ALU.mult, ALU.min).then_inc(clip_done, 1)
            dve.wait_ge(clip_done, 3 * n + 1)
            nc.vector.tensor_scalar(raw[:], raw[:], -1.0, ROUND, ALU.max, ALU.add).then_inc(clip_done, 1)
            dve.wait_ge(clip_done, 3 * n + 2)
            nc.vector.tensor_scalar(out[:], raw[:], ROUND, None, ALU.subtract).then_inc(clip_done, 1)

    @block.tensor
    def _(pe):
        pe.wait_ge(lo_done, 1)
        for h in range(HEADS):
            last = products(nc, ps_g[:, h * P:(h + 1) * P], wht_hi[:, h], wht_lo[:, h], wht_hi[:, h], wht_lo[:, h], True, True)
        last.then_inc(g_done, 1)
        pe.wait_ge(ones_done, 1)
        pe.wait_ge(sum_done, 2)
        nc.tensor.matmul(ps_mean[:, 0:2], ones[:], wsum[:], start=True, stop=True).then_inc(mean_done, 1)

    st.close()


def scores_block(nc, ctx, dram, keep):
    st = ctx.enter_context(ExitStack())
    sb = lambda n, s, d=F32: st.enter_context(nc.sbuf_tensor(n, s, d))
    sem = lambda n: ctx.enter_context(nc.semaphore(n))
    x = sb("x", [P, TJ, D])
    xn = sb("xn", [P, TJ, D])
    xnT_hi, xnT_lo = sb("xnT_hi", [P, KT, CH], F32R), sb("xnT_lo", [P, KT, CH], F32R)
    c = sb("c", [P, KT, CH])
    c_hi, c_lo = sb("c_hi", [P, KT, CH], F32R), sb("c_lo", [P, KT, CH], F32R)
    q_hi, q_lo = sb("q_hi", [P, HEADS, CH], F32R), sb("q_lo", [P, HEADS, CH], F32R)
    gate = sb("gate", [P, KT, CH])
    val = sb("val", [P, TJ, D])
    zeros = sb("zeros", [P, CH], F32R)
    stats = sb("stats", [P, TJ, 6])
    mom = sb("mom", [P, 5, TJ])
    ve, rstd, shift, mhalf = (sb(n, [P, TJ]) for n in ("ve", "rstd", "shift", "mhalf"))
    acc = st.enter_context(nc.psum_tensor("acc", [P, HEADS, CH], F32))
    bank = [st.enter_context(nc.psum_tensor(f"bank{n}", [P, CH], F32)) for n in range(4)]
    USES = 4 + 4 + 4 + 4
    (x_in, c_in, stats_done, mom_done, rstd_done, shift_done, xn_done, chi_done, clo_done,
     filled, hi_done, freed, xnT_done, val_done, gate_done, q_done, scores_done, consts_done, val_out,
     gate_out, mask_done, abs_done, a_done, ahi_done, alo_done) = (sem("s_" + n) for n in (
         "x_in c_in stats_done mom_done rstd_done shift_done xn_done chi_done clo_done "
         "filled hi_done freed xnT_done val_done gate_done q_done scores_done consts_done val_out "
         "gate_out mask_done abs_done a_done ahi_done alo_done").split())
    x_v = dram["x"].rearrange("(i j p) d -> i p j d", j=TJ, p=P)
    c_v = dram["ctxT"].rearrange("(k p) (i n) -> i p k n", p=P, n=CH)
    block = st.enter_context(nc.Block())

    @block.sync
    def _(sp):
        def load(i):
            sp.wait_ge(xn_done, START + 4 * i)
            sp.dma_start(x[:], x_v[i]).then_inc(x_in, 16)
            sp.wait_ge(clo_done, START + i)
            sp.dma_start(c[:], c_v[i]).then_inc(c_in, 16)

        def store(i):
            sp.wait_ge(gate_done, 4 * (i + 1))
            sp.dma_start(dram["gates"][i], gate[:]).then_inc(gate_out, 16)
            sp.wait_ge(val_done, START + 4 * (i + 1))
            sp.dma_start(dram["vals"][i], val[:]).then_inc(val_out, 16)

        sp.sem_inc(gate_out, START)
        sp.sem_inc(val_out, START)
        load(0)
        with sp.Fori(0, NCH - 1) as i:
            load(i + 1)
            store(i)
        store(NCH - 1)
        sp.wait_ge(gate_out, START + 16 * NCH)
        sp.wait_ge(val_out, START + 16 * NCH)

    @block.gpsimd
    def _(pool):
        nc.gpsimd.memset(mhalf[:], -0.5).then_inc(consts_done, 1)
        nc.gpsimd.memset(f32(zeros[:]), 0.0).then_inc(consts_done, 1)
        pool.wait_ge(consts_done, 1)
        with pool.Fori(0, NCH) as i:
            pool.wait_ge(mom_done, 6 * i + 6)
            nc.gpsimd.tensor_tensor(rstd[:], ve[:], mhalf[:], ALU.pow).then_inc(rstd_done, 1)

    @block.scalar
    def _(act):
        act.sem_inc(xn_done, START)
        with act.Fori(0, NCH) as i:
            act.wait_ge(shift_done, i + 1)
            for j in range(TJ):
                nc.scalar.activation(xn[:, j], x[:, j], ACT.Identity, bias=shift[:, j:j + 1],
                                     scale=rstd[:, j:j + 1]).then_inc(xn_done, 1)
            act.wait_ge(c_in, 16 * (i + 1))
            act.wait_ge(scores_done, START + i)
            nc.scalar.activation(c_hi[:], c[:], ACT.Copy).then_inc(chi_done, 1)
            for k in range(KT):
                act.wait_ge(filled, USES * i + k + 1)
                nc.scalar.activation(xnT_hi[:, k], bank[k][:], ACT.Copy).then_inc(hi_done, 1)
            for h in range(HEADS):
                act.wait_ge(filled, USES * i + 11 + h)
                nc.scalar.activation(q_hi[:, h], bank[(10 + h) % 4][:], ACT.Copy).then_inc(hi_done, 1)

    @block.vector
    def _(dve):
        def evac(i, use, k, hi, lo, done):
            dve.wait_ge(hi_done, 8 * i + k + 1)
            nc.vector.tensor_tensor(lo, bank[use % 4][:], f32(hi), ALU.subtract).then_inc(done, 1)

        for s in (clo_done, q_done, val_done):
            dve.sem_inc(s, START)
        with dve.Fori(0, NCH) as i:
            dve.wait_ge(x_in, 16 * (i + 1))
            for j in range(TJ):
                nc.vector.bn_stats(stats[:, j], x[:, j]).then_inc(stats_done, 1)
            dve.wait_ge(stats_done, 4 * (i + 1))
            variance(nc, dve, stats, mom, ve[:], LN_EPS, mom_done, 6 * i)
            dve.wait_ge(rstd_done, i + 1)
            nc.vector.scalar_tensor_tensor(out=shift[:], in0=mom[:, 0], scalar=-0.5, in1=rstd[:], op0=ALU.mult,
                                           op1=ALU.mult).then_inc(shift_done, 1)
            dve.wait_ge(chi_done, i + 1)
            nc.vector.tensor_tensor(c_lo[:], c[:], f32(c_hi[:]), ALU.subtract).then_inc(clo_done, 1)
            for k in range(KT):
                evac(i, k, k, xnT_hi[:, k], xnT_lo[:, k], xnT_done)
            dve.wait_ge(val_out, START + 16 * i)
            for j in range(2):
                dve.wait_ge(filled, USES * i + 5 + j)
                nc.vector.tensor_copy(val[:, j], bank[j][:]).then_inc(val_done, 1)
            dve.wait_ge(gate_out, START + 16 * i)
            for m in range(KT):
                dve.wait_ge(filled, USES * i + 7 + m)
                nc.vector.tensor_scalar(gate[:, m], bank[(6 + m) % 4][:], 0.0, None, ALU.max).then_inc(gate_done, 1)
            for h in range(HEADS):
                evac(i, 10 + h, 4 + h, q_hi[:, h], q_lo[:, h], q_done)
            for j in range(2, 4):
                dve.wait_ge(filled, USES * i + 13 + j)
                nc.vector.tensor_copy(val[:, j], bank[j][:]).then_inc(val_done, 1)
        dve.wait_ge(scores_done, START + NCH)
        dve.wait_ge(gate_out, START + 16 * NCH)
        dve.wait_ge(val_out, START + 16 * NCH)
        for h in range(HEADS):
            nc.vector.tensor_tensor(gate[:, h], acc[:, h], keep["mask"][:, h], ALU.mult).then_inc(mask_done, 1)
            dve.wait_ge(mask_done, h + 1)
            nc.vector.scalar_tensor_tensor(out=val[:, h], in0=gate[:, h], scalar=-1.0, in1=gate[:, h], op0=ALU.mult,
                                           op1=ALU.max).then_inc(abs_done, 1)
            dve.wait_ge(abs_done, h + 1)
            nc.vector.tensor_scalar(val[:, h], val[:, h], 1.0, None, ALU.max).then_inc(a_done, 1)
            dve.wait_ge(a_done, h + 1)
            nc.vector.tensor_copy(keep["at_hi"][:, h], val[:, h]).then_inc(ahi_done, 1)
            dve.wait_ge(ahi_done, h + 1)
            nc.vector.tensor_tensor(keep["at_lo"][:, h], val[:, h], f32(keep["at_hi"][:, h]), ALU.subtract).then_inc(alo_done, 1)

    @block.tensor
    def _(pe):
        pe.sem_inc(scores_done, START)
        pe.wait_ge(consts_done, 2)
        for h in range(HEADS):
            nc.tensor.matmul(acc[:, h], zeros[:, 0:P], zeros[:], start=True, stop=False, skip_group_check=True)

        def free(i, use):
            if use < 4:
                pe.wait_ge(q_done, START + 4 * i)
                pe.wait_ge(val_done, START + 4 * i)
            elif use < 8:
                pe.wait_ge(xnT_done, 4 * i + use - 3)
            elif use < 10:
                pe.wait_ge(val_done, START + 4 * i + use - 7)
            elif use < 14:
                pe.wait_ge(gate_done, 4 * i + use - 9)
            else:
                pe.wait_ge(q_done, START + 4 * i + use - 13)

        def values(i, j, use):
            free(i, use)
            for h in range(HEADS):
                last = products(nc, bank[use % 4][:, h * P:(h + 1) * P], c_hi[:, h, j * P:(j + 1) * P],
                                c_lo[:, h, j * P:(j + 1) * P], keep["wh_hi"][:, h], keep["wh_lo"][:, h], True, True)
            last.then_inc(filled, 1)

        with pe.Fori(0, NCH) as i:
            pe.wait_ge(xn_done, START + 4 * (i + 1))
            for k in range(KT):
                free(i, k)
                for j in range(TJ):
                    last = nc.tensor.transpose(bank[k][:, j * P:(j + 1) * P], xn[:, j, k * P:(k + 1) * P], keep["ident"][:])
                last.then_inc(filled, 1)
            pe.wait_ge(clo_done, START + i + 1)
            values(i, 0, 4)
            values(i, 1, 5)
            pe.wait_ge(xnT_done, 4 * (i + 1))
            for m in range(KT):
                free(i, 6 + m)
                for k in range(KT):
                    last = products(nc, bank[(6 + m) % 4][:], keep["wg_hi"][:, k, m * P:(m + 1) * P],
                                    keep["wg_lo"][:, k, m * P:(m + 1) * P], xnT_hi[:, k], xnT_lo[:, k], k == 0, k == KT - 1)
                last.then_inc(filled, 1)
            for h in range(HEADS):
                free(i, 10 + h)
                last = products(nc, bank[(10 + h) % 4][:], keep["g_hi"][:, h], keep["g_lo"][:, h], xnT_hi[:, h],
                                xnT_lo[:, h], True, True)
                last.then_inc(filled, 1)
            values(i, 2, 14)
            values(i, 3, 15)
            for h in range(HEADS):
                pe.wait_ge(q_done, START + 4 * i + h + 1)
                for b in range(2):
                    for t in range(2):
                        keys = slice(b * S + t * P, b * S + (t + 1) * P)
                        last = products(nc, acc[:, h, t * S:(t + 1) * S], c_hi[:, h, keys], c_lo[:, h, keys],
                                        q_hi[:, h, b * S:(b + 1) * S], q_lo[:, h, b * S:(b + 1) * S], False, False, skip=True)
            last.then_inc(scores_done, 1)

    st.close()


def attn_block(nc, ctx, dram, keep):
    st = ctx.enter_context(ExitStack())
    sb = lambda n, s, d=F32: st.enter_context(nc.sbuf_tensor(n, s, d))
    sem = lambda n: ctx.enter_context(nc.semaphore("a_" + n))
    x = sb("ax", [P, TJ, D])
    v = sb("av", [P, 2, 2, D])
    v_hi, v_lo = sb("av_hi", [P, 2, 2, D], F32R), sb("av_lo", [P, 2, 2, D], F32R)
    gate = sb("agate", [P, KT, CH])
    o = sb("ao", [P, TJ, D])
    og = sb("aog", [P, 2, CH])
    z = sb("az", [P, 2, CH])
    z_hi, z_lo = sb("az_hi", [P, KT, CH], F32R), sb("az_lo", [P, KT, CH], F32R)
    x1 = sb("ax1", [P, TJ, D])
    y = sb("ay", [P, TJ, D])
    yq = sb("ayq", [P, TJ, D], BF16)
    yqT = sb("ayqT", [P, KT, CH], BF16)
    h = sb("ah", [P, 2, HID])
    hq = sb("ahq", [P, 2, HID], BF16)
    hqT = sb("ahqT", [P, HT, P], BF16)
    x2 = sb("ax2", [P, TJ, D])
    ostats, omom = sb("aostats", [P, 2, 6]), sb("aomom", [P, 5, 2])
    ove, orstd, oshift = (sb(n, [P, 2]) for n in ("aove", "aorstd", "aoshift"))
    stats, mom = sb("astats", [P, TJ, 6]), sb("amom", [P, 5, TJ])
    ve, rstd, sq, r2in, r2, scale, shift, amax, qrec, qscale, dq1 = (
        sb("a" + n, [P, TJ]) for n in "ve rstd sq r2in r2 scale shift amax qrec qscale dq1".split())
    hmax, hrec, hscale, dq2 = (sb("a" + n, [P, TJ]) for n in "hmax hrec hscale dq2".split())
    mhalf, rnd, dq2w = sb("amhalf", [P, TJ]), sb("arnd", [P, 1]), sb("adq2w", [P, 1])
    ps_o = st.enter_context(nc.psum_tensor("ps_o", [P, HEADS, 2, P], F32))
    ps_r = [st.enter_context(nc.psum_tensor(f"ps_r{n}", [P, CH], F32)) for n in range(2)]
    ps_t = st.enter_context(nc.psum_tensor("ps_t", [P, 2, 4, P], BF16))
    ps_h = [st.enter_context(nc.psum_tensor(f"ps_h{n}", [P, 512], F32)) for n in range(2)]
    ps_y = st.enter_context(nc.psum_tensor("ps_y", [P, D], F32))
    (v_in, gate_in, x_in, vhi_done, vlo_done, o_done, ostats_done, omom_done, orstd_done, oshift_done, on_done,
     oT_done, og_done, z_done, zhi_done, zlo_done, wo_done, x1_done, stats_done, mom_done, rstd_done, rms_step,
     r2_done, y_done, yg_done, amax_done, qs_done, round_done, yq_done, t_done, t_read, h_done, gelu_done,
     hmax_done, hs_done, hround_done, hq_done, mm2_done, x2_done, x2_out, consts_done, dq2w_done, shift_done) = (sem(n) for n in (
         "v_in gate_in x_in vhi_done vlo_done o_done ostats_done omom_done orstd_done oshift_done on_done "
         "oT_done og_done z_done zhi_done zlo_done wo_done x1_done stats_done mom_done rstd_done rms_step "
         "r2_done y_done yg_done amax_done qs_done round_done yq_done t_done t_read h_done gelu_done "
         "hmax_done hs_done hround_done hq_done mm2_done x2_done x2_out consts_done dq2w_done shift_done").split())
    TU = 2 + 2 * TJ
    x_v = dram["x"].rearrange("(c j p) d -> c p j d", j=TJ, p=P)
    x2_v = dram["x2"].rearrange("(c j p) d -> c j p d", j=TJ, p=P)
    block = st.enter_context(nc.Block())

    @block.sync
    def _(sp):
        def load(c):
            sp.wait_ge(vlo_done, START + c)
            sp.dma_start(v[:].rearrange("p a b d -> p (a b) d"), dram["vals"][c]).then_inc(v_in, 16)
            sp.wait_ge(z_done, START + 4 * c)
            sp.dma_start(gate[:], dram["gates"][c]).then_inc(gate_in, 16)
            sp.wait_ge(x1_done, START + 4 * c)
            sp.dma_start(x[:], x_v[c]).then_inc(x_in, 16)

        def store(c):
            for j in range(TJ):
                sp.wait_ge(x2_done, START + 4 * c + j + 1)
                sp.dma_start(x2_v[c, j], x2[:, j]).then_inc(x2_out, 16)

        sp.sem_inc(x2_out, START)
        load(0)
        with sp.Fori(0, NCH - 1) as c:
            load(c + 1)
            store(c)
        store(NCH - 1)
        sp.wait_ge(x2_out, START + 16 * TJ * NCH)

    @block.gpsimd
    def _(pool):
        nc.gpsimd.memset(mhalf[:], -0.5).then_inc(consts_done, 1)
        nc.gpsimd.memset(rnd[:], ROUND).then_inc(consts_done, 1)
        pool.wait_ge(consts_done, 1)
        with pool.Fori(0, NCH) as c:
            for s in range(2):
                pool.wait_ge(omom_done, 12 * c + 6 * s + 6)
                nc.gpsimd.tensor_tensor(orstd[:], ove[:], mhalf[:, 0:2], ALU.pow).then_inc(orstd_done, 1)
            pool.wait_ge(mom_done, 6 * c + 6)
            nc.gpsimd.tensor_tensor(rstd[:], ve[:], mhalf[:], ALU.pow).then_inc(rstd_done, 1)
            pool.wait_ge(rms_step, 3 * c + 3)
            nc.gpsimd.tensor_tensor(r2[:], r2in[:], mhalf[:], ALU.pow).then_inc(r2_done, 1)

    @block.scalar
    def _(act):
        def attention(c):
            act.wait_ge(v_in, 16 * (c + 1))
            nc.scalar.activation(v_hi[:], v[:], ACT.Copy).then_inc(vhi_done, 1)
            for s in range(2):
                act.wait_ge(oshift_done, 2 * c + s + 1)
                for b in range(2):
                    nc.scalar.activation(o[:, 2 * b + s].rearrange("p (h e) -> p h e", e=P), ps_o[:, :, b], ACT.Identity,
                                         bias=oshift[:, b:b + 1], scale=orstd[:, b:b + 1]).then_inc(on_done, 1)

            def times_gamma(k):
                act.wait_ge(oT_done, 4 * c + k + 1)
                act.wait_ge(z_done, START + 4 * c + max(k - 1, 0))
                nc.scalar.activation(og[:, k % 2], ps_r[k % 2][:], ACT.Identity, bias=keep["vecs"][:, V_BETA + k:V_BETA + k + 1],
                                     scale=keep["vecs"][:, V_GAMMA + k:V_GAMMA + k + 1]).then_inc(og_done, 1)

            def cut_hi(k):
                act.wait_ge(z_done, START + 4 * c + k + 1)
                nc.scalar.activation(z_hi[:, k], z[:, k % 2], ACT.Copy).then_inc(zhi_done, 1)

            times_gamma(0)
            times_gamma(1)
            cut_hi(0)
            times_gamma(2)
            cut_hi(1)
            times_gamma(3)
            cut_hi(2)
            cut_hi(3)
            act.wait_ge(qs_done, 5 * c + 5)
            for j in range(TJ):
                nc.scalar.activation(y[:, j], y[:, j], ACT.Identity, bias=rnd[:], scale=qscale[:, j:j + 1]).then_inc(round_done, 1)

        def gelu(c, j):
            for n in range(4):
                act.wait_ge(h_done, 16 * c + 4 * j + n + 1)
                if n == 0:
                    act.wait_ge(hq_done, START + 4 * c + max(j - 1, 0))
                nc.scalar.activation(h[:, j % 2, n * 512:(n + 1) * 512], ps_h[n % 2][:], ACT.Gelu,
                                     scale=dq1[:, j:j + 1]).then_inc(gelu_done, 1)

        def round_h(c, j):
            act.wait_ge(hs_done, 4 * (4 * c + j + 1))
            nc.scalar.activation(h[:, j % 2], h[:, j % 2], ACT.Identity, bias=rnd[:], scale=hscale[:, j:j + 1]).then_inc(hround_done, 1)

        act.sem_inc(gelu_done, START)
        act.sem_inc(on_done, START)
        act.wait_ge(consts_done, 2)
        with act.Fori(0, NCH) as c:
            attention(c)
            gelu(c, 0)
            gelu(c, 1)
            round_h(c, 0)
            gelu(c, 2)
            round_h(c, 1)
            gelu(c, 3)
            round_h(c, 2)
            round_h(c, 3)

    @block.vector
    def _(dve):
        def attention(c):
            dve.wait_ge(vhi_done, c + 1)
            nc.vector.tensor_tensor(v_lo[:], v[:], f32(v_hi[:]), ALU.subtract).then_inc(vlo_done, 1)
            for s in range(2):
                dve.wait_ge(o_done, 2 * c + s + 1)
                for b in range(2):
                    nc.vector.bn_stats(ostats[:, b], ps_o[:, :, b]).then_inc(ostats_done, 1)
                dve.wait_ge(ostats_done, 4 * c + 2 * s + 2)
                variance(nc, dve, ostats, omom, ove[:], GN_EPS, omom_done, 12 * c + 6 * s)
                dve.wait_ge(orstd_done, 2 * c + s + 1)
                dve.wait_ge(on_done, START + 4 * c + 2 * s)
                nc.vector.scalar_tensor_tensor(out=oshift[:], in0=omom[:, 0], scalar=-0.5, in1=orstd[:], op0=ALU.mult,
                                               op1=ALU.mult).then_inc(oshift_done, 1)

            def gated(k):
                dve.wait_ge(og_done, 4 * c + k + 1)
                if k >= 2:
                    dve.wait_ge(zlo_done, 4 * c + k - 1)
                nc.vector.tensor_tensor(z[:, k % 2], og[:, k % 2], gate[:, k], ALU.mult).then_inc(z_done, 1)

            def cut_lo(k):
                dve.wait_ge(zhi_done, 4 * c + k + 1)
                nc.vector.tensor_tensor(z_lo[:, k], z[:, k % 2], f32(z_hi[:, k]), ALU.subtract).then_inc(zlo_done, 1)

            dve.wait_ge(gate_in, 16 * (c + 1))
            gated(0)
            gated(1)
            cut_lo(0)
            gated(2)
            cut_lo(1)
            gated(3)
            cut_lo(2)
            cut_lo(3)
            dve.wait_ge(x_in, 16 * (c + 1))
            for j in range(TJ):
                dve.wait_ge(wo_done, 4 * c + j + 1)
                nc.vector.scalar_tensor_tensor(out=x1[:, j], in0=ps_r[j % 2][:], scalar=keep["gains"][:, 0:1], in1=x[:, j],
                                               op0=ALU.mult, op1=ALU.add).then_inc(x1_done, 1)
                dve.wait_ge(x1_done, START + 4 * c + j + 1)
                nc.vector.bn_stats(stats[:, j], x1[:, j]).then_inc(stats_done, 1)
            dve.wait_ge(stats_done, 4 * (c + 1))
            variance(nc, dve, stats, mom, ve[:], LN_EPS, mom_done, 6 * c)
            dve.wait_ge(rstd_done, c + 1)
            nc.vector.tensor_tensor(sq[:], rstd[:], rstd[:], ALU.mult).then_inc(rms_step, 1)
            dve.wait_ge(rms_step, 3 * c + 1)
            nc.vector.scalar_tensor_tensor(out=r2in[:], in0=ve[:], scalar=LN_EPS, in1=sq[:], op0=ALU.subtract,
                                           op1=ALU.mult).then_inc(rms_step, 1)
            dve.wait_ge(rms_step, 3 * c + 2)
            nc.vector.tensor_scalar(r2in[:], r2in[:], RMS_EPS, None, ALU.add).then_inc(rms_step, 1)
            dve.wait_ge(r2_done, c + 1)
            nc.vector.tensor_tensor(scale[:], rstd[:], r2[:], ALU.mult).then_inc(shift_done, 1)
            dve.wait_ge(shift_done, 2 * c + 1)
            nc.vector.scalar_tensor_tensor(out=shift[:], in0=mom[:, 0], scalar=-0.5, in1=scale[:], op0=ALU.mult,
                                           op1=ALU.mult).then_inc(shift_done, 1)
            dve.wait_ge(shift_done, 2 * c + 2)
            for j in range(TJ):
                nc.vector.tensor_scalar(y[:, j], x1[:, j], scale[:, j:j + 1], shift[:, j:j + 1], ALU.mult,
                                        ALU.add).then_inc(y_done, 1)
            for j in range(TJ):
                dve.wait_ge(y_done, 4 * c + j + 1)
                nc.vector.tensor_tensor(y[:, j], y[:, j], keep["gam"][:], ALU.mult).then_inc(yg_done, 1)
            dve.wait_ge(yg_done, 4 * c + 4)
            nc.vector.tensor_reduce(amax[:], y[:], AX.X, ALU.max, apply_absolute_value=True).then_inc(amax_done, 1)
            dve.wait_ge(amax_done, c + 1)
            nc.vector.tensor_scalar(amax[:], amax[:], 1e-5, None, ALU.max).then_inc(qs_done, 1)
            dve.wait_ge(qs_done, 5 * c + 1)
            nc.vector.reciprocal(qrec[:], amax[:]).then_inc(qs_done, 1)
            nc.vector.tensor_scalar(dq1[:], amax[:], 1.0 / QMAX, keep["wmean"][:, 0:1], ALU.mult, ALU.mult).then_inc(qs_done, 2)
            dve.wait_ge(qs_done, 5 * c + 4)
            nc.vector.tensor_scalar(qscale[:], qrec[:], QMAX, None, ALU.mult).then_inc(qs_done, 1)
            for j in range(TJ):
                dve.wait_ge(round_done, 4 * c + j + 1)
                nc.vector.tensor_scalar(yq[:, j], y[:, j], ROUND, None, ALU.subtract).then_inc(yq_done, 1)
            for a in range(2):
                dve.wait_ge(t_done, TU * c + a + 1)
                nc.vector.tensor_copy(yqT[:, :, 2 * a * P:(2 * a + 2) * P].rearrange("p k (j n) -> p j k n", n=P),
                                      ps_t[:]).then_inc(t_read, 1)

        def scale_h(c, j):
            col = slice(j, j + 1)
            dve.wait_ge(gelu_done, START + 16 * c + 4 * j + 4)
            nc.vector.tensor_reduce(hmax[:, col], h[:, j % 2], AX.X, ALU.max, apply_absolute_value=True).then_inc(hmax_done, 1)
            n = 4 * (4 * c + j)
            dve.wait_ge(hmax_done, 4 * c + j + 1)
            nc.vector.tensor_scalar(hmax[:, col], hmax[:, col], 1e-5, None, ALU.max).then_inc(hs_done, 1)
            dve.wait_ge(hs_done, n + 1)
            nc.vector.reciprocal(hrec[:, col], hmax[:, col]).then_inc(hs_done, 1)
            nc.vector.tensor_scalar(dq2[:, col], hmax[:, col], dq2w[:], None, ALU.mult).then_inc(hs_done, 1)
            dve.wait_ge(hs_done, n + 3)
            nc.vector.tensor_scalar(hscale[:, col], hrec[:, col], QMAX, None, ALU.mult).then_inc(hs_done, 1)

        def to_bf16(c, j):
            dve.wait_ge(hround_done, 4 * c + j + 1)
            dve.wait_ge(t_done, TU * c + (2 + 2 * (j - 1) if j >= 2 else 2))
            nc.vector.tensor_scalar(hq[:, j % 2], h[:, j % 2], ROUND, None, ALU.subtract).then_inc(hq_done, 1)

        def read_hT(c, j, a):
            dve.wait_ge(t_done, TU * c + 2 + 2 * j + a + 1)
            if a == 0:
                dve.wait_ge(mm2_done, START + 4 * c + j)
            nc.vector.tensor_copy(hqT[:, 8 * a:8 * a + 8], ps_t[:].rearrange("p a b n -> p (a b) n")).then_inc(t_read, 1)

        def residual(c, j):
            if j == 0:
                dve.wait_ge(x2_out, START + 16 * TJ * c)
            dve.wait_ge(mm2_done, START + 4 * c + j + 1)
            nc.vector.scalar_tensor_tensor(out=x2[:, j], in0=ps_y[:], scalar=dq2[:, j:j + 1], in1=x1[:, j], op0=ALU.mult,
                                           op1=ALU.add).then_inc(x2_done, 1)

        for s in (vlo_done, z_done, x1_done, hq_done, t_read, x2_done):
            dve.sem_inc(s, START)
        nc.vector.tensor_scalar(dq2w[:], keep["wmean"][:, 1:2], keep["gains"][:, 2:3], 1.0 / QMAX, ALU.mult, ALU.mult).then_inc(dq2w_done, 1)
        dve.wait_ge(dq2w_done, 1)
        with dve.Fori(0, NCH) as c:
            attention(c)
            scale_h(c, 0)
            to_bf16(c, 0)
            scale_h(c, 1)
            read_hT(c, 0, 0)
            read_hT(c, 0, 1)
            to_bf16(c, 1)
            residual(c, 0)
            scale_h(c, 2)
            read_hT(c, 1, 0)
            read_hT(c, 1, 1)
            to_bf16(c, 2)
            residual(c, 1)
            scale_h(c, 3)
            read_hT(c, 2, 0)
            read_hT(c, 2, 1)
            to_bf16(c, 3)
            residual(c, 2)
            read_hT(c, 3, 0)
            read_hT(c, 3, 1)
            residual(c, 3)

    @block.tensor
    def _(pe):
        def attention(c):
            pe.wait_ge(vlo_done, START + c + 1)
            for s in range(2):
                pe.wait_ge(on_done, START + 4 * c + 2 * s)
                for h_ in range(HEADS):
                    for t in range(2):
                        q = slice(t * S + s * P, t * S + (s + 1) * P)
                        last = products(nc, ps_o[:, h_], keep["at_hi"][:, h_, q], keep["at_lo"][:, h_, q],
                                        v_hi[:, :, t, h_ * P:(h_ + 1) * P], v_lo[:, :, t, h_ * P:(h_ + 1) * P], t == 0, t == 1,
                                        skip=True)
                last.then_inc(o_done, 1)
            pe.wait_ge(on_done, START + 4 * c + 4)
            for k in range(KT):
                if k < 2:
                    pe.wait_ge(x1_done, START + 4 * c)
                else:
                    pe.wait_ge(og_done, 4 * c + k - 1)
                for j in range(TJ):
                    last = nc.tensor.transpose(ps_r[k % 2][:, j * P:(j + 1) * P], o[:, j, k * P:(k + 1) * P], keep["ident"][:])
                last.then_inc(oT_done, 1)
            pe.wait_ge(zlo_done, 4 * c + 4)
            for j in range(TJ):
                if j < 2:
                    pe.wait_ge(og_done, 4 * c + 3 + j)
                else:
                    pe.wait_ge(x1_done, START + 4 * c + j - 1)
                for k in range(KT):
                    last = products(nc, ps_r[j % 2][:], z_hi[:, k, j * P:(j + 1) * P], z_lo[:, k, j * P:(j + 1) * P],
                                    keep["wo_hi"][:, k], keep["wo_lo"][:, k], k == 0, k == KT - 1)
                last.then_inc(wo_done, 1)
            for a in range(2):
                pe.wait_ge(yq_done, 4 * c + 2 * a + 2)
                pe.wait_ge(t_read, START + TU * c + a)
                for j in range(2):
                    for k in range(KT):
                        last = nc.tensor.transpose(ps_t[:, j, k], yq[:, 2 * a + j, k * P:(k + 1) * P], keep["identb"][:])
                last.then_inc(t_done, 1)
            pe.wait_ge(t_read, START + TU * c + 2)

        def mm1(c, j, ns):
            for n in ns:
                if j == 0 and n < 2:
                    pe.wait_ge(gelu_done, START + 16 * c)
                else:
                    pe.wait_ge(gelu_done, START + 16 * c + 4 * j + n - 1)
                for k in range(KT):
                    last = nc.tensor.matmul(ps_h[n % 2][:], yqT[:, k, j * P:(j + 1) * P], keep["w1q"][:, k, n * 512:(n + 1) * 512],
                                            start=(k == 0), stop=(k == KT - 1))
                last.then_inc(h_done, 1)

        def turn(c, j, a):
            pe.wait_ge(hq_done, START + 4 * c + j + 1)
            pe.wait_ge(t_read, START + TU * c + 2 + 2 * j + a)
            for m in range(8):
                last = nc.tensor.transpose(ps_t[:, m // 4, m % 4], hq[:, j % 2, (8 * a + m) * P:(8 * a + m + 1) * P], keep["identb"][:])
            last.then_inc(t_done, 1)

        def mm2(c, j):
            pe.wait_ge(x2_done, START + 4 * c + j)
            for a in range(2):
                pe.wait_ge(t_read, START + TU * c + 2 + 2 * j + a + 1)
                for k in range(8 * a, 8 * a + 8):
                    last = nc.tensor.matmul(ps_y[:], hqT[:, k], keep["w2q"][:, k], start=(k == 0), stop=(k == HT - 1))
            last.then_inc(mm2_done, 1)

        pe.sem_inc(mm2_done, START)
        with pe.Fori(0, NCH) as c:
            attention(c)
            mm1(c, 0, range(4))
            mm1(c, 1, range(4))
            for j in range(TJ):
                turn(c, j, 0)
                if j + 2 < TJ:
                    mm1(c, j + 2, (0, 1))
                turn(c, j, 1)
                if j + 2 < TJ:
                    mm1(c, j + 2, (2, 3))
                mm2(c, j)

    st.close()


def experts_block(nc, ctx, dram, keep):
    st = ctx.enter_context(ExitStack())
    sb = lambda n, s, d=F32: st.enter_context(nc.sbuf_tensor("e_" + n, s, d))
    ps = lambda n, s: st.enter_context(nc.psum_tensor("e_" + n, s, F32))
    sem = lambda n: ctx.enter_context(nc.semaphore("e_" + n))
    START = 2
    gu_raw, gu_hi, gu_lo = sb("gu_raw", [P, 2, 2, KT, P]), sb("gu_hi", [P, 2, 2, KT, P], F32R), sb("gu_lo", [P, 2, 2, KT, P], F32R)
    dn_raw, dn_hi, dn_lo = sb("dn_raw", [P, 2, D]), sb("dn_hi", [P, 2, D], F32R), sb("dn_lo", [P, 2, D], F32R)
    x = sb("x", [P, TJ, D])
    xq = sb("xq", [P, TJ, D])
    x2T = sb("x2T", [P, KT, CH])
    qe = sb("qe", [P, KT * B * CHD, EXT])
    c = sb("c", [P, KT, CH])
    ke = sb("ke", [P, KT * B, EXT])
    kv_raw = sb("kv_raw", [P, 2, B, PAIRS])
    kv_hi, kv_lo = sb("kv_hi", [P, KT, B, PAIRS], F32R), sb("kv_lo", [P, KT, B, PAIRS], F32R)
    t_raw, t_hi, t_lo = sb("t_raw", [P, D]), sb("t_hi", [P, D], F32R), sb("t_lo", [P, D], F32R)
    ZW, ZROW = 160, 20
    zp = sb("zp", [P, B, ZW])
    skip = sb("skip", [P, NCH * CHD])
    x3T = sb("x3T", [P, KT, CH])
    xnat = sb("xnat", [P, TJ, D])
    xn_hi, xn_lo = sb("xn_hi", [P, KT, CH], F32R), sb("xn_lo", [P, KT, CH], F32R)
    wb = sb("wb", [P, NE, CH])
    wT_hi, wT_lo = sb("wT_hi", [8, CH], F32R), sb("wT_lo", [8, CH], F32R)
    sg, sgw, hd = sb("sg", [P, CH]), sb("sgw", [P, CH]), sb("hd", [P, CH])
    hd_hi, hd_lo = sb("hd_hi", [P, 2, CH], F32R), sb("hd_lo", [P, 2, CH], F32R)
    y = sb("y", [P, KT, CH])
    bd_raw, bd_hi, bd_lo = hd[0:8], sb("bd_hi", [8, D], F32R), sb("bd_lo", [8, D], F32R)
    sel_raw, sel = y[0:8, 0:2].rearrange("p k n -> p (k n)")[:, 0:NE * P], sb("sel", [8, NE * P], F32R)
    wr_raw, wr_hi, wr_lo = xnat[:, 0:KT, 0:8], sb("wr_hi", [P, KT, 8], F32R), sb("wr_lo", [P, KT, 8], F32R)
    lg, lx, rank, keepw, ew, w = (sb(n, [P, TJ, 8]) for n in "lg lx rank keepw ew w".split())
    ge, gt, below, above = (sb(n, [P, 4 * 64]) for n in "ge gt below above".split())
    lmax, wsum, wrec = (sb(n, [P, TJ]) for n in "lmax wsum wrec".split())
    base_e = sb("base_e", [P, TJ * 8])
    stats, mom = sb("stats", [P, TJ, 6]), sb("mom", [P, 5, TJ])
    ve, rstd, shift, mhalf = (sb(n, [P, TJ]) for n in "ve rstd shift mhalf".split())
    pstats, pmom = sb("pstats", [P, 2, 6]), sb("pmom", [P, 5, 2])
    pve, prstd, pshift = (sb(n, [P, 2]) for n in "pve prstd pshift".split())
    gb = sb("gb", [P, KT])

    ps_out = ps("ps_out", [P, KT, CH])
    ps_g, ps_u, ps_m = ps("ps_g", [P, CH]), ps("ps_u", [P, CH]), ps("ps_m", [P, 2, CH])
    m_units = ps_m[:].rearrange("p a (b n) -> p (a b) n", n=64)

    names = ("const_in const_done setup_hi setup_lo gb_done guhi_done gulo_done dnhi_done dnlo_done gate_done gu_done "
             "silu_done sgw_done stt_done hdhi_done hdlo_done down_done y_copied y_done y_out x_in c_in t_in "
             "stats_done mom_done rstd_done shift_done xq_done x2T_filled x2T_done q_filled qe_done ke_done kvraw_done "
             "kvhi_done kvlo_done td_done thi_done tlo_done unit_done prod_done red_done x3_done nat_filled pstats_done "
             "pmom_done prstd_done pshift_done xnat_done xnT_filled xnhi_done xn_done lg_filled lg_done rt exp_done w_done "
             "wT_filled wThi_done wT_done wb_filled wb_done bias_done skip_in")
    (const_in, const_done, setup_hi, setup_lo, gb_done, guhi_done, gulo_done, dnhi_done, dnlo_done, gate_done, gu_done,
     silu_done, sgw_done, stt_done, hdhi_done, hdlo_done, down_done, y_copied, y_done, y_out, x_in, c_in, t_in,
     stats_done, mom_done, rstd_done, shift_done, xq_done, x2T_filled, x2T_done, q_filled, qe_done, ke_done, kvraw_done,
     kvhi_done, kvlo_done, td_done, thi_done, tlo_done, unit_done, prod_done, red_done, x3_done, nat_filled, pstats_done,
     pmom_done, prstd_done, pshift_done, xnat_done, xnT_filled, xnhi_done, xn_done, lg_filled, lg_done, rt, exp_done, w_done,
     wT_filled, wThi_done, wT_done, wb_filled, wb_done, bias_done, skip_in) = (sem(n) for n in names.split())
    gu_in, dn_in = ([sem(n + "0"), sem(n + "1")] for n in ("gu_in", "dn_in"))
    RT = 15

    def view(t, offset, *dims):
        return bass.AP(t[:].tensor, t[:].offset + offset, [list(t[:].ap[0])] + [list(d) for d in dims])

    FIRST_UNIT_STEP = 2
    UNITS = {FIRST_UNIT_STEP: [0]}
    u = 1
    for s in range(3, 13):
        UNITS[s] = list(range(u, u + (2 if s % 2 else 1)))
        u += len(UNITS[s])
    assert u == CHD * KT
    T_STEPS = (0, 3, 5, 8)
    routed = lambda s: s < RSTEPS
    block = st.enter_context(nc.Block())

    @block.sync
    def _(sp):
        def load_gu(g, s):
            n = STEPS * g + s
            s %= STEPS
            sp.wait_ge(gulo_done, START + n - 1)
            if routed(s):
                sp.dma_start(gu_raw[:, s % 2].rearrange("p a k n -> p (a k n)"), dram["mgu"][s]).then_inc(gu_in[s % 2], 16)
            else:
                sp.dma_start(gu_raw[:, s % 2, 1].rearrange("p k n -> p (k n)"), dram["msu"][s - RSTEPS]).then_inc(gu_in[s % 2], 16)

        def load_dn(g, s):
            n = STEPS * g + s
            s %= STEPS
            sp.wait_ge(dnlo_done, START + n - 1)
            sp.dma_start(dn_raw[:, s % 2], dram["md"][s]).then_inc(dn_in[s % 2], 16)

        def load_x(q):
            sp.wait_ge(xq_done, START + 4 * q)
            sp.wait_ge(x2T_done, START + 2 * q)
            for b in range(B):
                j, r = b // 4, (b % 4) * 32
                sp.dma_start(x[r:r + 32, j], dram["x2"].rearrange("(b g r) d -> g b r d", b=B, g=NCH)[q, b]).then_inc(x_in, 16)

        def load_c(q):
            sp.wait_ge(ke_done, START + 2 * CHD * q)
            sp.dma_start(c[:], dram["ctxG"].rearrange("g (k p) n -> g p k n", p=P)[q]).then_inc(c_in, 16)

        def load_t(q, hh):
            sp.wait_ge(tlo_done, START + CHD * q + hh)
            sp.dma_start(t_raw[:], dram["toep"][CHD * q + hh]).then_inc(t_in, 16)

        def store(g):
            sp.wait_ge(y_done, START + 4 * g + 4)
            sp.dma_start(dram["out"].rearrange("g (k p) n -> g p k n", p=P)[g], y[:]).then_inc(y_out, 16)

        sp.sem_inc(y_out, START)
        for t, name in ((bd_raw, "bdown"), (sel_raw, "sel"), (wr_raw, "wroute"), (below[:], "below"), (above[:], "above"),
                        (skip[:], "skipD")):
            sp.dma_start(t, dram[name]).then_inc(const_in, 16)
        load_x(0)
        load_c(0)
        load_gu(0, 0)
        load_dn(0, 0)
        load_gu(0, 1)
        for hh in range(CHD):
            load_t(0, hh)

        def round_(g, q):
            for s in range(STEPS):
                if q is not None and s == 0:
                    load_x(q)
                    load_c(q)
                if q is not None or s < STEPS - 2:
                    load_gu(g, s + 2)
                if q is not None or s < STEPS - 1:
                    load_dn(g, s + 1)
                if q is not None and s in T_STEPS:
                    load_t(q, T_STEPS.index(s))
            store(g)

        with sp.Fori(0, NCH - 1) as g:
            round_(g, g + 1)
        round_(NCH - 1, None)
        sp.wait_ge(y_out, START + 16 * NCH)

    @block.gpsimd
    def _(pool):
        def cut_gu(g, s):
            n = STEPS * g + s
            s %= STEPS
            pool.wait_ge(guhi_done, n + 1)
            a = slice(0 if routed(s) else 1, 2)
            nc.gpsimd.tensor_tensor(gu_lo[:, s % 2, a], gu_raw[:, s % 2, a], f32(gu_hi[:, s % 2, a]), ALU.subtract).then_inc(gulo_done, 1)

        def cut_dn(g, s):
            n = STEPS * g + s
            pool.wait_ge(dnhi_done, n + 1)
            nc.gpsimd.tensor_tensor(dn_lo[:, s % 2], dn_raw[:, s % 2], f32(dn_hi[:, s % 2]), ALU.subtract).then_inc(dnlo_done, 1)

        def weigh(g, s):
            if not routed(s):
                return
            pool.wait_ge(silu_done, START + STEPS * g + s + 1)
            pool.wait_ge(wb_done, START + 3 * g + s // 4 + 1)
            pool.wait_ge(stt_done, START + RSTEPS * g + s)
            nc.gpsimd.tensor_tensor(sgw[:], sg[:], wb[:, s // 2], ALU.mult).then_inc(sgw_done, 1)

        def pairs(q, u):
            v = CHD * KT * q + u
            m = u % KT
            pool.wait_ge(ke_done, START + 2 * (CHD * q + u // KT + 1))
            pool.wait_ge(kvlo_done, START + v - 1)
            out = kv_raw[:, u % 2]
            nc.gpsimd.tensor_tensor(out[:, :, 0:32].rearrange("p b (d i) -> p b d i", i=CD),
                                    view(ke, m * B * EXT, (EXT, B), (0, 4), (1, CD)),
                                    view(ke, m * B * EXT, (EXT, B), (1, 4), (1, CD)), ALU.mult).then_inc(kvraw_done, 1)
            nc.gpsimd.tensor_tensor(out[:, :, 32:36], ke[:, m * B:(m + 1) * B, 0:4], ke[:, m * B:(m + 1) * B, 4:8],
                                    ALU.mult).then_inc(kvraw_done, 1)

        def conv_pow(q):
            pool.wait_ge(mom_done, 6 * q + 6)
            nc.gpsimd.tensor_tensor(rstd[:], ve[:], mhalf[:], ALU.pow).then_inc(rstd_done, 1)

        def nat_pow(q, a):
            pool.wait_ge(pmom_done, 12 * q + 6 * a + 6)
            nc.gpsimd.tensor_tensor(prstd[:], pve[:], mhalf[:, 0:2], ALU.pow).then_inc(prstd_done, 1)

        def exp(q):
            pool.wait_ge(rt, RT * q + 9)
            nc.gpsimd.tensor_tensor(ew[:], base_e[:].rearrange("p (j e) -> p j e", e=8), lx[:], ALU.pow).then_inc(exp_done, 1)

        for s in (gulo_done, dnlo_done, sgw_done, kvraw_done):
            pool.sem_inc(s, START)
        nc.gpsimd.memset(mhalf[:], -0.5).then_inc(const_done, 1)
        nc.gpsimd.memset(base_e[:], 2.718281828459045).then_inc(const_done, 1)
        pool.wait_ge(const_done, 2)
        conv_pow(0)
        cut_gu(0, 0)
        pairs(0, 0)
        pairs(0, 1)
        for u in range(CHD * KT):
            if u + 2 < CHD * KT:
                pairs(0, u + 2)
        nat_pow(0, 0)
        nat_pow(0, 1)
        exp(0)

        def round_(g, q):
            for s in range(STEPS):
                units = UNITS.get(s, []) if q is not None else []
                weigh(g, s)
                if q is not None and s == 0:
                    conv_pow(q)
                if q is not None and s == 1:
                    pairs(q, 0)
                if q is not None and s == 2:
                    pairs(q, 1)
                if units and units[0] + 2 < CHD * KT:
                    pairs(q, units[0] + 2)
                if q is not None or s < STEPS - 1:
                    cut_gu(g, s + 1)
                if len(units) > 1 and units[1] + 2 < CHD * KT:
                    pairs(q, units[1] + 2)
                cut_dn(g, s)
                if q is not None and s in (13, 14):
                    nat_pow(q, s - 13)
            if q is not None:
                exp(q)

        with pool.Fori(0, NCH - 1) as g:
            round_(g, g + 1)
        round_(NCH - 1, None)

    @block.scalar
    def _(act):
        vecs = keep["vecs"]

        def cut_gu(g, s):
            n = STEPS * g + s
            act.wait_ge(gu_in[s % 2], 16 * (STEPS // 2 * g + s // 2 + 1))
            s %= STEPS
            act.wait_ge(gu_done, START + n - 1)
            a = slice(0 if routed(s) else 1, 2)
            nc.scalar.activation(gu_hi[:, s % 2, a], gu_raw[:, s % 2, a], ACT.Copy).then_inc(guhi_done, 1)

        def cut_dn(g, s):
            n = STEPS * g + s
            act.wait_ge(dn_in[s % 2], 16 * (STEPS // 2 * g + s // 2 + 1))
            act.wait_ge(down_done, START + n - 1)
            nc.scalar.activation(dn_hi[:, s % 2], dn_raw[:, s % 2], ACT.Copy).then_inc(dnhi_done, 1)

        def silu(g, s):
            n = STEPS * g + s
            if routed(s):
                act.wait_ge(gate_done, RSTEPS * g + s + 1)
                act.wait_ge(sgw_done, START + RSTEPS * g + s)
                nc.scalar.activation(sg[:], ps_g[:], ACT.Silu, bias=vecs[:, V_BG + s:V_BG + s + 1]).then_inc(silu_done, 1)
            else:
                act.wait_ge(gu_done, START + n + 1)
                act.wait_ge(hdlo_done, START + n)
                nc.scalar.activation(hd[:], ps_u[:], ACT.Silu,
                                     bias=vecs[:, V_BSU + s - RSTEPS:V_BSU + s - RSTEPS + 1]).then_inc(silu_done, 1)

        def cut_hd(g, s):
            n = STEPS * g + s
            if routed(s):
                act.wait_ge(stt_done, START + RSTEPS * g + s + 1)
            else:
                act.wait_ge(silu_done, START + n + 1)
            act.wait_ge(down_done, START + n - 1)
            nc.scalar.activation(hd_hi[:, s % 2], hd[:], ACT.Copy).then_inc(hdhi_done, 1)

        def norm_x(q):
            act.wait_ge(shift_done, q + 1)
            act.wait_ge(q_filled, START + 2 * q)
            for j in range(TJ):
                nc.scalar.activation(xq[:, j], x[:, j], ACT.Identity, bias=shift[:, j:j + 1], scale=rstd[:, j:j + 1]).then_inc(xq_done, 1)

        def read_x2T(q, a):
            act.wait_ge(x2T_filled, 2 * q + a + 1)
            act.wait_ge(x3_done, START + q)
            nc.scalar.activation(x2T[:, 2 * a:2 * a + 2], ps_m[:], ACT.Copy).then_inc(x2T_done, 1)

        def read_q(q, a):
            act.wait_ge(q_filled, START + 2 * q + a + 1)
            act.wait_ge(prod_done, START + 4 * CHD * KT * q)
            half = B * CHD * 2
            src = ps_m[:].rearrange("p a (n i) -> p (a n) i", i=CD)
            nc.scalar.activation(qe[:, half * a:half * (a + 1), 0:CD], src, ACT.Copy).then_inc(qe_done, 1)
            nc.scalar.activation(qe[:, half * a:half * (a + 1), CD:EXT], src[:, :, 0:EXT - CD], ACT.Copy).then_inc(qe_done, 1)

        def keys(q, hh):
            n = CHD * q + hh
            act.wait_ge(c_in, 16 * (q + 1))
            act.wait_ge(kvraw_done, START + 2 * KT * n)
            src = c[:].rearrange("p k (b n) -> p (k b) n", b=B)
            nc.scalar.activation(ke[:, :, 0:CD], src[:, :, hh * CD:(hh + 1) * CD], ACT.Copy).then_inc(ke_done, 1)
            nc.scalar.activation(ke[:, :, CD:EXT], src[:, :, hh * CD:hh * CD + EXT - CD], ACT.Copy).then_inc(ke_done, 1)

        def cut_t(q, hh):
            n = CHD * q + hh
            act.wait_ge(td_done, n + 1)
            act.wait_ge(unit_done, START + KT * n)
            nc.scalar.activation(t_hi[:], t_raw[:], ACT.Copy).then_inc(thi_done, 1)

        def cut_kv(q, u):
            v = CHD * KT * q + u
            act.wait_ge(kvraw_done, START + 2 * (v + 1))
            act.wait_ge(unit_done, START + v - u % KT)
            nc.scalar.activation(kv_hi[:, u % KT], kv_raw[:, u % 2], ACT.Copy).then_inc(kvhi_done, 1)

        def unit(q, u):
            if u % KT == 2 and u // KT < CHD - 1:
                keys(q, u // KT + 1)
            if u + 1 < CHD * KT:
                if (u + 1) % KT == 0:
                    cut_t(q, (u + 1) // KT)
                cut_kv(q, u + 1)

        def norm_nat(q, a):
            act.wait_ge(pshift_done, 2 * q + a + 1)
            act.wait_ge(xnT_filled, START + 2 * q)
            for j in range(2):
                nc.scalar.activation(xnat[:, 2 * a + j], ps_m[:, j], ACT.Identity, bias=pshift[:, j:j + 1],
                                     scale=prstd[:, j:j + 1]).then_inc(xnat_done, 1)

        def cut_xn(q, a):
            act.wait_ge(xnT_filled, START + 2 * q + a + 1)
            nc.scalar.activation(xn_hi[:, 2 * a:2 * a + 2], ps_m[:], ACT.Copy).then_inc(xnhi_done, 1)

        def cut_wT(g):
            act.wait_ge(wT_filled, g + 1)
            nc.scalar.activation(wT_hi[:], ps_m[0:8, 0], ACT.Copy).then_inc(wThi_done, 1)

        def read_wb(g, a):
            act.wait_ge(wb_filled, 3 * g + a + 1)
            act.wait_ge(sgw_done, START + RSTEPS * g)
            nc.scalar.activation(wb[:, 2 * a:2 * a + 2], ps_m[:], ACT.Copy).then_inc(wb_done, 1)

        def copy_x3(g):
            act.wait_ge(x3_done, START + g + 1)
            act.wait_ge(y_out, START + 16 * g)
            for k in range(KT):
                nc.scalar.activation(y[:, k], x3T[:, k], ACT.Identity, bias=gb[:, k:k + 1]).then_inc(y_copied, 1)

        for s in (silu_done, xq_done, x2T_done, ke_done, qe_done, xnat_done, wb_done, y_copied):
            act.sem_inc(s, START)
        act.wait_ge(const_in, 16 * 6)
        nc.scalar.activation(bd_hi[:], bd_raw, ACT.Copy).then_inc(setup_hi, 1)
        nc.scalar.activation(wr_hi[:], wr_raw, ACT.Copy).then_inc(setup_hi, 1)
        nc.scalar.activation(sel[:], sel_raw, ACT.Copy).then_inc(setup_hi, 1)
        act.wait_ge(gb_done, 1)
        norm_x(0)
        read_x2T(0, 0)
        read_x2T(0, 1)
        read_q(0, 0)
        read_q(0, 1)
        cut_gu(0, 0)
        keys(0, 0)
        cut_t(0, 0)
        cut_kv(0, 0)
        for u in range(CHD * KT):
            unit(0, u)
        norm_nat(0, 0)
        norm_nat(0, 1)
        cut_xn(0, 0)
        cut_xn(0, 1)

        def round_(g, q):
            for s in range(STEPS):
                units = UNITS.get(s, []) if q is not None else []
                silu(g, s)
                if s == 0:
                    cut_wT(g)
                    read_wb(g, 0)
                if s == 1:
                    read_wb(g, 1)
                if q is not None and s == 2:
                    read_q(q, 1)
                if q is not None or s < STEPS - 1:
                    cut_gu(g, s + 1)
                if q is not None and s == 2:
                    cut_t(q, 0)
                    cut_kv(q, 0)
                if units and s > FIRST_UNIT_STEP:
                    unit(q, units[0])
                if q is not None and s == STEPS - 1:
                    cut_xn(q, 0)
                cut_hd(g, s)
                if units and s == FIRST_UNIT_STEP:
                    unit(q, units[0])
                if len(units) > 1:
                    unit(q, units[1])
                if s == 0:
                    copy_x3(g)
                if q is not None and s == 0:
                    read_x2T(q, 0)
                    read_x2T(q, 1)
                    norm_x(q)
                if s == 1:
                    read_wb(g, 2)
                if q is not None and s == 1:
                    read_q(q, 0)
                    keys(q, 0)
                cut_dn(g, s)
                if q is not None and s in (13, 14):
                    norm_nat(q, s - 13)
                if q is not None and s == STEPS - 1:
                    cut_xn(q, 1)

        with act.Fori(0, NCH - 1) as g:
            round_(g, g + 1)
        round_(NCH - 1, None)

    @block.vector
    def _(dve):
        vecs = keep["vecs"]

        def gated(g, s):
            if not routed(s):
                return
            n = STEPS * g + s
            dve.wait_ge(gu_done, START + n + 1)
            dve.wait_ge(sgw_done, START + RSTEPS * g + s + 1)
            dve.wait_ge(hdlo_done, START + n)
            nc.vector.scalar_tensor_tensor(out=hd[:], in0=ps_u[:], scalar=vecs[:, V_BU + s:V_BU + s + 1], in1=sgw[:], op0=ALU.add,
                                           op1=ALU.mult).then_inc(stt_done, 1)

        def cut_hd(g, s):
            dve.wait_ge(hdhi_done, STEPS * g + s + 1)
            nc.vector.tensor_tensor(hd_lo[:, s % 2], hd[:], f32(hd_hi[:, s % 2]), ALU.subtract).then_inc(hdlo_done, 1)

        def norm_stats(q):
            dve.wait_ge(x_in, 16 * B * (q + 1))
            for j in range(TJ):
                nc.vector.bn_stats(stats[:, j], x[:, j]).then_inc(stats_done, 1)
            dve.wait_ge(stats_done, 4 * (q + 1))
            variance(nc, dve, stats, mom, ve[:], LN_EPS, mom_done, 6 * q)
            dve.wait_ge(rstd_done, q + 1)
            nc.vector.scalar_tensor_tensor(out=shift[:], in0=mom[:, 0], scalar=-0.5, in1=rstd[:], op0=ALU.mult,
                                           op1=ALU.mult).then_inc(shift_done, 1)

        def add_skip(q, hh):
            n = CHD * q + hh
            dve.wait_ge(t_in, 16 * (n + 1))
            nc.vector.scalar_tensor_tensor(out=t_raw[:, 0:P], in0=keep["ident"][:], scalar=skip[:, bass.ds(n, 1)], in1=t_raw[:, 0:P],
                                           op0=ALU.mult, op1=ALU.add).then_inc(td_done, 1)

        def cut_t(q, hh):
            dve.wait_ge(thi_done, CHD * q + hh + 1)
            nc.vector.tensor_tensor(t_lo[:], t_raw[:], f32(t_hi[:]), ALU.subtract).then_inc(tlo_done, 1)

        def cut_kv(q, u):
            dve.wait_ge(kvhi_done, CHD * KT * q + u + 1)
            nc.vector.tensor_tensor(kv_lo[:, u % KT], kv_raw[:, u % 2], f32(kv_hi[:, u % KT]), ALU.subtract).then_inc(kvlo_done, 1)

        def unit(q, u):
            hh, lb = u // KT, u % KT
            v = CHD * KT * q + u
            if u + 1 < CHD * KT:
                if (u + 1) % KT == 0:
                    add_skip(q, hh + 1)
                    cut_t(q, hh + 1)
                cut_kv(q, u + 1)
            if u == 0:
                dve.wait_ge(qe_done, START + 4 * (q + 1))
                dve.wait_ge(y_copied, START + 4 * q)
            dve.wait_ge(red_done, START + v)
            dve.wait_ge(unit_done, START + v + 1)
            qo = (lb * B * CHD + hh) * EXT
            qv = lambda off, *dims: view(qe, qo + off, (CHD * EXT, B), *dims)
            yv = lambda off, *dims: bass.AP(ps_m[:].tensor, ps_m[:].offset + off, [list(ps_m[:].ap[0]), [64, B]] + [list(d) for d in dims])
            zv = lambda off, *dims: view(zp, off, (ZW, B), *dims)
            nc.vector.tensor_tensor(zv(68, (21, 4), (1, 8)), yv(0, (8, 4), (1, 8)), qv(0, (1, 4), (1, 8)), ALU.mult).then_inc(prod_done, 1)
            nc.vector.tensor_tensor(zv(152, (4, 2), (1, 4)), yv(32, (0, 2), (1, 4)), qv(4, (4, 2), (1, 4)), ALU.mult).then_inc(prod_done, 1)
            nc.vector.tensor_tensor(zv(2 * ZROW + 8, (-ZROW, 3), (1, 8)), yv(8, (8, 3), (1, 8)), qv(0, (0, 3), (1, 8)),
                                    ALU.mult).then_inc(prod_done, 1)
            nc.vector.tensor_tensor(zv(2 * ZROW + 5, (-ZROW, 3), (1, 3)), yv(8 + 5, (8, 3), (1, 3)), qv(5, (0, 3), (1, 3)),
                                    ALU.mult).then_inc(prod_done, 1)
            dve.wait_ge(prod_done, START + 4 * (v + 1))
            nc.vector.tensor_reduce(x3T[:, lb].rearrange("p (b n) -> p b n", b=B)[:, :, hh * CD:(hh + 1) * CD],
                                    zv(5, (1, 8), (21, 8)), AX.X, ALU.add).then_inc(red_done, 1)

        def add_x2(q):
            dve.wait_ge(red_done, START + CHD * KT * (q + 1))
            dve.wait_ge(x2T_done, START + 2 * (q + 1))
            nc.vector.scalar_tensor_tensor(out=x3T[:], in0=x3T[:], scalar=keep["gains"][:, 1:2], in1=x2T[:], op0=ALU.mult,
                                           op1=ALU.add).then_inc(x3_done, 1)

        def nat_stats(q, a):
            dve.wait_ge(nat_filled, 2 * q + a + 1)
            for j in range(2):
                nc.vector.bn_stats(pstats[:, j], ps_m[:, j]).then_inc(pstats_done, 1)
            dve.wait_ge(pstats_done, 4 * q + 2 * a + 2)
            variance(nc, dve, pstats, pmom, pve[:], LN_EPS, pmom_done, 12 * q + 6 * a)
            dve.wait_ge(prstd_done, 2 * q + a + 1)
            dve.wait_ge(xnat_done, START + 4 * q + 2 * a)
            nc.vector.scalar_tensor_tensor(out=pshift[:], in0=pmom[:, 0], scalar=-0.5, in1=prstd[:], op0=ALU.mult,
                                           op1=ALU.mult).then_inc(pshift_done, 1)

        def cut_xn(q, a):
            dve.wait_ge(xnhi_done, 2 * q + a + 1)
            nc.vector.tensor_tensor(xn_lo[:, 2 * a:2 * a + 2], ps_m[:], f32(xn_hi[:, 2 * a:2 * a + 2]), ALU.subtract).then_inc(xn_done, 1)

        def route(q):
            r0 = RT * q
            n8 = lambda t: t[:].rearrange("p (j i e) -> p j i e", i=8, e=8)
            other, own = view(lg, 0, (8, TJ), (0, 8), (1, 8)), view(lg, 0, (8, TJ), (1, 8), (0, 8))
            row = lambda t: view(t, 0, (1, TJ), (0, 8))
            dve.wait_ge(lg_filled, q + 1)
            nc.vector.tensor_tensor(lg[:], ps_m[:, 0, 0:TJ * 8].rearrange("p (j e) -> p j e", e=8), view(vecs, V_BGATE, (0, TJ), (1, 8)),
                                    ALU.add).then_inc(lg_done, 1)
            dve.wait_ge(lg_done, START + q + 1)
            nc.vector.tensor_tensor(n8(ge), other, own, ALU.is_ge).then_inc(rt, 1)
            nc.vector.tensor_tensor(n8(gt), other, own, ALU.is_gt).then_inc(rt, 1)
            nc.vector.tensor_reduce(lmax[:], lg[:], AX.X, ALU.max).then_inc(rt, 1)
            dve.wait_ge(rt, r0 + 3)
            nc.vector.tensor_tensor(ge[:], ge[:], below[:], ALU.mult).then_inc(rt, 1)
            nc.vector.tensor_tensor(gt[:], gt[:], above[:], ALU.mult).then_inc(rt, 1)
            nc.vector.tensor_tensor(lx[:], lg[:], row(lmax), ALU.subtract).then_inc(rt, 4)
            dve.wait_ge(rt, r0 + 9)
            nc.vector.tensor_tensor(ge[:], ge[:], gt[:], ALU.add).then_inc(rt, 1)
            dve.wait_ge(rt, r0 + 10)
            nc.vector.tensor_reduce(rank[:], n8(ge), AX.X, ALU.add).then_inc(rt, 1)
            dve.wait_ge(rt, r0 + 11)
            nc.vector.tensor_scalar(keepw[:], rank[:], float(NE) - 0.5, None, ALU.is_lt).then_inc(rt, 1)
            dve.wait_ge(rt, r0 + 12)
            dve.wait_ge(exp_done, q + 1)
            nc.vector.tensor_tensor(ew[:], ew[:], keepw[:], ALU.mult).then_inc(rt, 1)
            dve.wait_ge(rt, r0 + 13)
            nc.vector.tensor_reduce(wsum[:], ew[:], AX.X, ALU.add).then_inc(rt, 1)
            dve.wait_ge(rt, r0 + 14)
            nc.vector.reciprocal(wrec[:], wsum[:]).then_inc(rt, 1)
            dve.wait_ge(rt, r0 + 15)
            nc.vector.tensor_tensor(w[:], ew[:], row(wrec), ALU.mult).then_inc(w_done, 1)

        def cut_wT(g):
            dve.wait_ge(wThi_done, g + 1)
            nc.vector.tensor_tensor(wT_lo[:], ps_m[0:8, 0], f32(wT_hi[:]), ALU.subtract).then_inc(wT_done, 1)

        def finish(g):
            dve.wait_ge(down_done, START + STEPS * (g + 1))
            dve.wait_ge(y_copied, START + 4 * (g + 1))
            for k in range(KT):
                nc.vector.scalar_tensor_tensor(out=y[:, k], in0=ps_out[:, k], scalar=keep["gains"][:, 3:4], in1=y[:, k], op0=ALU.mult,
                                               op1=ALU.add).then_inc(y_done, 1)

        for s in (hdlo_done, stt_done, kvlo_done, tlo_done, prod_done, red_done, x3_done, xn_done, lg_done, wT_done, y_done):
            dve.sem_inc(s, START)
        dve.wait_ge(const_in, 16 * 6)
        nc.vector.tensor_scalar(gb[:], vecs[:, V_BSD:V_BSD + KT], keep["gains"][:, 3:4], None, ALU.mult).then_inc(gb_done, 1)
        dve.wait_ge(setup_hi, 2)
        nc.vector.tensor_tensor(bd_lo[:], bd_raw, f32(bd_hi[:]), ALU.subtract).then_inc(setup_lo, 1)
        nc.vector.tensor_tensor(wr_lo[:], wr_raw, f32(wr_hi[:]), ALU.subtract).then_inc(setup_lo, 1)
        norm_stats(0)
        add_skip(0, 0)
        cut_t(0, 0)
        cut_kv(0, 0)
        for u in range(CHD * KT):
            unit(0, u)
        add_x2(0)
        nat_stats(0, 0)
        nat_stats(0, 1)
        cut_xn(0, 0)
        cut_xn(0, 1)
        dve.wait_ge(setup_lo, 2)
        route(0)

        def round_(g, q):
            for s in range(STEPS):
                units = UNITS.get(s, []) if q is not None else []
                if q is not None and s == 2:
                    add_skip(q, 0)
                if q is not None and s == 13:
                    add_x2(q)
                if s == 0:
                    cut_wT(g)
                gated(g, s)
                if q is not None and s == 0:
                    norm_stats(q)
                if q is not None and s == 2:
                    cut_t(q, 0)
                    cut_kv(q, 0)
                if units and s > FIRST_UNIT_STEP:
                    unit(q, units[0])
                if q is not None and s == STEPS - 1:
                    cut_xn(q, 0)
                cut_hd(g, s)
                if units and s == FIRST_UNIT_STEP:
                    unit(q, units[0])
                if len(units) > 1:
                    unit(q, units[1])
                if q is not None and s in (13, 14):
                    nat_stats(q, s - 13)
                if q is not None and s == STEPS - 1:
                    cut_xn(q, 1)
            if q is not None:
                route(q)
            finish(g)

        with dve.Fori(0, NCH - 1) as g:
            round_(g, g + 1)
        round_(NCH - 1, None)

    @block.tensor
    def _(pe):
        ident = keep["ident"]

        def gate_up(g, s):
            n = STEPS * g + s
            pe.wait_ge(gulo_done, START + n + 1)
            if s == 0:
                pe.wait_ge(xn_done, START + 2 * (g + 1))
            pe.wait_ge(silu_done, START + n)
            if routed(s):
                for k in range(KT):
                    last = products(nc, ps_g[:], gu_hi[:, s % 2, 0, k], gu_lo[:, s % 2, 0, k], xn_hi[:, k], xn_lo[:, k], k == 0, k == KT - 1)
                last.then_inc(gate_done, 1)
            if s <= RSTEPS:
                pe.wait_ge(stt_done, START + RSTEPS * g + s)
            for k in range(KT):
                last = products(nc, ps_u[:], gu_hi[:, s % 2, 1, k], gu_lo[:, s % 2, 1, k], xn_hi[:, k], xn_lo[:, k], k == 0, k == KT - 1)
            last.then_inc(gu_done, 1)

        def bias(g):
            pe.wait_ge(y_done, START + 4 * g)
            pe.wait_ge(wT_done, START + g + 1)
            for k in range(KT):
                col = slice(k * P, (k + 1) * P)
                products(nc, ps_out[:, k], bd_hi[:, col], bd_lo[:, col], wT_hi[:], wT_lo[:], True, False, skip=True)

        def down(g, s):
            n = STEPS * g + s
            pe.wait_ge(hdlo_done, START + n + 1)
            pe.wait_ge(dnlo_done, START + n + 1)
            for k in range(KT):
                col = slice(k * P, (k + 1) * P)
                last = products(nc, ps_out[:, k], dn_hi[:, s % 2, col], dn_lo[:, s % 2, col], hd_hi[:, s % 2], hd_lo[:, s % 2], False,
                                s == STEPS - 1, skip=True)
            last.then_inc(down_done, 1)

        def turn_x2(q, a, after):
            pe.wait_ge(x_in, 16 * B * (q + 1))
            pe.wait_ge(*after)
            for kk in range(2):
                for j in range(TJ):
                    k = 2 * a + kk
                    last = nc.tensor.transpose(ps_m[:, kk, j * P:(j + 1) * P], x[:, j, k * P:(k + 1) * P], ident[:])
            last.then_inc(x2T_filled, 1)

        def turn_q(q, a, after):
            pe.wait_ge(xq_done, START + 4 * (q + 1))
            pe.wait_ge(*after)
            for kk in range(2):
                for j in range(TJ):
                    k = 2 * a + kk
                    last = nc.tensor.transpose(ps_m[:, kk, j * P:(j + 1) * P], xq[:, j, k * P:(k + 1) * P], ident[:])
            last.then_inc(q_filled, 1)

        def unit(q, u, after):
            hh, lb = u // KT, u % KT
            v = CHD * KT * q + u
            if u > 0:
                after = (prod_done, START + 4 * v)
            pe.wait_ge(kvlo_done, START + v + 1)
            pe.wait_ge(tlo_done, START + CHD * q + hh + 1)
            pe.wait_ge(*after)
            for half in range(2):
                bs = slice(half * B // 2, (half + 1) * B // 2)
                for m in range(lb + 1):
                    t = slice((lb - m) * P, (lb - m + 1) * P)
                    last = products(nc, m_units[:, bs, 0:PAIRS], t_hi[:, t], t_lo[:, t], kv_hi[:, m, bs], kv_lo[:, m, bs], m == 0, m == lb)
            last.then_inc(unit_done, 1)

        def turn_x3(q, a, after):
            pe.wait_ge(x3_done, START + q + 1)
            pe.wait_ge(*after)
            for jj in range(2):
                for k in range(KT):
                    j = 2 * a + jj
                    last = nc.tensor.transpose(ps_m[:, jj, k * P:(k + 1) * P], x3T[:, k, j * P:(j + 1) * P], ident[:])
            last.then_inc(nat_filled, 1)

        def turn_xn(q, a, after):
            pe.wait_ge(xnat_done, START + 4 * (q + 1))
            pe.wait_ge(*after)
            for kk in range(2):
                for j in range(TJ):
                    k = 2 * a + kk
                    last = nc.tensor.transpose(ps_m[:, kk, j * P:(j + 1) * P], xnat[:, j, k * P:(k + 1) * P], ident[:])
            last.then_inc(xnT_filled, 1)

        def logits(q):
            pe.wait_ge(xn_done, START + 2 * (q + 1))
            for j in range(TJ):
                tok = slice(j * P, (j + 1) * P)
                for k in range(KT):
                    last = products(nc, ps_m[:, 0, 8 * j:8 * j + 8], xn_hi[:, k, tok], xn_lo[:, k, tok], wr_hi[:, k], wr_lo[:, k],
                                    k == 0, k == KT - 1)
            last.then_inc(lg_filled, 1)

        def turn_w(g):
            pe.wait_ge(w_done, g + 1)
            for j in range(TJ):
                last = nc.tensor.transpose(ps_m[0:8, 0, j * P:(j + 1) * P], w[:, j], ident[:])
            last.then_inc(wT_filled, 1)

        def spread(g, a, after):
            pe.wait_ge(wT_done, START + g + 1)
            pe.wait_ge(*after)
            for e in range(2):
                nc.tensor.matmul(ps_m[:, e], sel[:, (2 * a + e) * P:(2 * a + e + 1) * P], wT_hi[:], start=True, stop=False)
                last = nc.tensor.matmul(ps_m[:, e], sel[:, (2 * a + e) * P:(2 * a + e + 1) * P], wT_lo[:], start=False, stop=True)
            last.then_inc(wb_filled, 1)

        for s in (gu_done, down_done, unit_done, q_filled, xnT_filled):
            pe.sem_inc(s, START)
        pe.wait_ge(setup_lo, 2)
        pe.wait_ge(setup_hi, 3)
        turn_x2(0, 0, (x2T_done, START))
        turn_x2(0, 1, (x2T_done, START + 1))
        turn_q(0, 0, (x2T_done, START + 2))
        turn_q(0, 1, (qe_done, START + 2))
        for u in range(CHD * KT):
            unit(0, u, (qe_done, START + 4))
        turn_x3(0, 0, (prod_done, START + 4 * CHD * KT))
        turn_x3(0, 1, (xnat_done, START + 2))
        turn_xn(0, 0, (xnat_done, START + 4))
        turn_xn(0, 1, (xn_done, START + 1))
        logits(0)

        def round_(g, q):
            for s in range(STEPS):
                units = UNITS.get(s, []) if q is not None else []
                gate_up(g, s)
                if s == 0:
                    turn_w(g)
                    spread(g, 0, (wT_done, START + g + 1))
                if s == 1:
                    bias(g)
                    spread(g, 1, (x2T_done, START + 2 * q + 2) if q is not None else (wb_done, START + 3 * g + 1))
                if q is not None and s == 2:
                    turn_q(q, 1, (qe_done, START + 4 * q + 2))
                if units and s > FIRST_UNIT_STEP:
                    unit(q, units[0], None)
                if q is not None and s == STEPS - 1:
                    turn_xn(q, 0, (xnat_done, START + 4 * q + 4))
                if s > 0:
                    down(g, s - 1)
                if q is not None and s == 0:
                    turn_x2(q, 0, (wb_done, START + 3 * g + 1))
                    turn_x2(q, 1, (x2T_done, START + 2 * q + 1))
                if s == 1:
                    spread(g, 2, (wb_done, START + 3 * g + 2))
                if q is not None and s == 1:
                    turn_q(q, 0, (wb_done, START + 3 * g + 3))
                if units and s == FIRST_UNIT_STEP:
                    unit(q, units[0], (qe_done, START + 4 * q + 4))
                if len(units) > 1:
                    unit(q, units[1], None)
                if q is not None and s == 13:
                    turn_x3(q, 0, (prod_done, START + 4 * CHD * KT * (q + 1)))
                if q is not None and s == 14:
                    turn_x3(q, 1, (xnat_done, START + 4 * q + 2))
                if q is not None and s == STEPS - 1:
                    turn_xn(q, 1, (xn_done, START + 2 * q + 1))
            down(g, STEPS - 1)
            if q is not None:
                logits(q)

        with pe.Fori(0, NCH - 1) as g:
            round_(g, g + 1)
        round_(NCH - 1, None)

    st.close()


def expert_constants(np):
    own, other = np.meshgrid(np.arange(8), np.arange(8), indexing="ij")
    rep = lambda m: np.broadcast_to(m.astype(np.float32).reshape(1, 1, 64), (P, 4, 64)).reshape(P, 256)
    sel = np.zeros((8, NE * P), np.float32)
    for e in range(NE):
        sel[e, e * P:(e + 1) * P] = 1.0
    return {"sel": sel, "below": rep(other < own), "above": rep(other > own)}


def build(nc, dram):
    with ExitStack() as ctx:
        sb = lambda n, s, d=F32: ctx.enter_context(nc.sbuf_tensor(n, s, d))
        keep = {"vecs": sb("vecs", [P, V_COLS]), "gains": sb("gains", [P, 4]), "ident": sb("ident", [P, P]),
                "identb": sb("identb", [P, P], BF16), "wmean": sb("wmean", [P, 2])}
        attn = ctx.enter_context(ExitStack())
        at = lambda n, s, d=F32: attn.enter_context(nc.sbuf_tensor(n, s, d))
        keep.update({"at_hi": at("at_hi", [P, HEADS, CH], F32R), "at_lo": at("at_lo", [P, HEADS, CH], F32R),
                     "wo_hi": at("wo_hi", [P, KT, D], F32R), "wo_lo": at("wo_lo", [P, KT, D], F32R),
                     "w1q": at("w1q", [P, KT, HID], BF16), "w2q": at("w2q", [P, HT, D], BF16), "gam": at("gam", [P, D])})
        sc = ctx.enter_context(ExitStack())
        at = lambda n, s, d=F32: sc.enter_context(nc.sbuf_tensor(n, s, d))
        keep.update({"wg_hi": at("wg_hi", [P, KT, D], F32R), "wg_lo": at("wg_lo", [P, KT, D], F32R),
                     "wh_hi": at("wh_hi", [P, HEADS, P], F32R), "wh_lo": at("wh_lo", [P, HEADS, P], F32R),
                     "g_hi": at("g_hi", [P, HEADS, P], F32R), "g_lo": at("g_lo", [P, HEADS, P], F32R),
                     "mask": at("mask", [P, HEADS, CH])})
        setup_block(nc, ctx, dram, keep)
        scores_block(nc, ctx, dram, keep)
        sc.close()
        attn_block(nc, ctx, dram, keep)
        attn.close()
        experts_block(nc, ctx, dram, keep)


def decay_mask(np):
    gam = 1.0 - 2.0 ** (-5.0 - np.arange(HEADS))
    expo = (np.arange(S)[None, :] - np.arange(S)[:, None]).astype(np.float64)
    d = np.where(expo[None] <= 0, gam[:, None, None] ** np.minimum(expo[None], 0), 0.0)
    d = d / np.sqrt(d.sum(-1))[:, None, :] / np.sqrt(P)
    return np.ascontiguousarray(d.reshape(HEADS, S, 2, P).transpose(3, 0, 2, 1).reshape(P, HEADS, CH)).astype(np.float32)


def kernel(**inputs):
    import numpy as np
    import concourse.bacc as bacc
    from concourse import mybir as mb
    from concourse.bass_utils import run_bass_kernel_spmd

    a = {k: np.asarray(v) for k, v in inputs.items()}
    lay = np.ascontiguousarray
    ctx_t = a["ctx_2048"].reshape(B * S, D).T
    gains = [a["g_xattn"][0:1], a["g_xattn"][1:2], a["g_ffn"][0:1], a["g_ffn"][1:2], ]
    cols = lambda v: v.reshape(-1, P).T
    rows = lambda v: np.broadcast_to(v.reshape(1, -1), (P, v.size))
    vecs = np.concatenate([rows(g) for g in gains] + [
        cols(a["L0_xattn_gn_gamma"]), cols(a["L0_xattn_gn_beta"]), cols(a["L1_ffn_bgate"]), cols(a["L1_ffn_bup"]),
        cols(a["L1_ffn_bs_up"]), cols(a["L1_ffn_bs_down"]), rows(a["L1_ffn_bg"])], axis=1)
    ctx_g = a["ctx_2048"].reshape(B, NCH, S // NCH, D).transpose(1, 3, 0, 2).reshape(NCH, D, CH)
    padded = np.concatenate([np.zeros((S // CD, P), np.float32), a["L1_xattn_ssm_kernel"]], axis=1)
    toep = np.stack([padded[:, P - m:P - m + D] for m in range(P)], axis=1)
    tiles = lambda w, n: w.reshape(KT, P, n, P).transpose(2, 1, 0, 3).reshape(n, P, D)
    of = lambda w: np.concatenate([tiles(w[e], EH // P) for e in range(NE)])
    mgu = np.stack([of(a["L1_ffn_Wgate"]), of(a["L1_ffn_Wup"])], axis=2).reshape(RSTEPS, P, 2 * D)
    md = np.concatenate([a["L1_ffn_Wdown"].reshape(RSTEPS, P, D), a["L1_ffn_Ws_down"].reshape(SH // P, P, D)])
    bdown = np.concatenate([a["L1_ffn_bdown"], np.zeros((2, D), np.float32)])
    arrays = {
        "x": a["x"].reshape(B * S, D), "ctxT": ctx_t, "ctxG": ctx_g, "toep": toep,
        "skipD": rows(a["L1_xattn_D"]),
        "wh": a["L0_xattn_Wh"], "whT": a["L0_xattn_Wh"].transpose(0, 2, 1), "wg": a["L0_xattn_wg_w"],
        "wo": a["L0_xattn_wo_w"], "w1T": a["L0_ffn_w1"].T, "w2T": a["L0_ffn_w2"].T, "vecs": vecs,
        "gam": rows(a["L0_ffn_gamma"]), "ident": np.eye(P, dtype=np.float32), "mask": decay_mask(np),
        "mgu": mgu, "msu": tiles(a["L1_ffn_Ws_up"], SH // P), "md": md,
        "wroute": a["L1_ffn_Wg"].reshape(KT, P, 8).transpose(1, 0, 2), "bdown": bdown, **expert_constants(np),
    }
    arrays = {"in_" + n: lay(v) for n, v in arrays.items()}
    nc = bacc.Bacc("TRN2", target_bir_lowering=False, num_devices=1)
    dram = {n[3:]: nc.dram_tensor(n, v.shape, mb.dt.from_np(v.dtype), kind="ExternalInput").ap() for n, v in arrays.items()}
    dram["gates"] = nc.dram_tensor("gates", (NCH, P, KT, CH), mb.dt.float32, kind="Internal").ap()
    dram["vals"] = nc.dram_tensor("vals", (NCH, P, TJ, D), mb.dt.float32, kind="Internal").ap()
    dram["x2"] = nc.dram_tensor("x2", (B * S, D), mb.dt.float32, kind="Internal").ap()
    dram["out"] = nc.dram_tensor("out", (NCH, D, CH), mb.dt.float32, kind="ExternalOutput").ap()
    build(nc, dram)
    got = run_bass_kernel_spmd(nc, [arrays], core_ids=[0]).results[0]["out"]
    return lay(got.reshape(NCH, D, B, S // NCH).transpose(2, 0, 3, 1).reshape(B, S, D))
```

```python
from contextlib import ExitStack

import concourse.bass as bass
from concourse import mybir

F32 = mybir.dt.float32
F32R = mybir.dt.float32r
BF16 = mybir.dt.bfloat16
ACT = mybir.ActivationFunctionType
ALU = mybir.AluOpType
AX = mybir.AxisListType

P = 128
B, S, D = 16, 256, 512
KT = D // P
HEADS = 4
CH = 512
NCH = B * S // CH
TJ = CH // P
HID = 2048
HT = HID // P
START = 1
ROUND = 1.5 * 2.0 ** 23
LN_EPS, GN_EPS, RMS_EPS = 1e-5, 1e-3, 1e-6
QMAX = 127.0
NE, EH = 6, 256
SH = 512
CD = 8
CHD = 4
PAIRS = 36
EXT = 12
STEPS = (NE * EH + SH) // P
RSTEPS = NE * EH // P
V_GAIN, V_GAMMA, V_BETA, V_BG, V_BU, V_BSU, V_BSD, V_BGATE = 0, 4, 8, 12, 24, 36, 40, 44
V_COLS = 52


def f32(ap):
    return ap.bitcast(F32)


def products(nc, out, w_hi, w_lo, x_hi, x_lo, first, last, skip=False):
    nc.tensor.matmul(out, w_hi, x_hi, start=first, stop=False, skip_group_check=skip)
    nc.tensor.matmul(out, w_hi, x_lo, start=False, stop=False, skip_group_check=skip)
    return nc.tensor.matmul(out, w_lo, x_hi, start=False, stop=last, skip_group_check=skip)


def variance(nc, dve, stats, mom, var, eps, step, done):
    nc.vector.tensor_tensor(mom[:, 0], stats[:, :, 1], stats[:, :, 4], ALU.add).then_inc(step, 1)
    nc.vector.tensor_tensor(mom[:, 1], stats[:, :, 1], stats[:, :, 4], ALU.subtract).then_inc(step, 1)
    nc.vector.tensor_tensor(mom[:, 2], stats[:, :, 2], stats[:, :, 5], ALU.add).then_inc(step, 1)
    dve.wait_ge(step, done + 3)
    nc.vector.scalar_tensor_tensor(out=mom[:, 3], in0=mom[:, 1], scalar=0.25, in1=mom[:, 1], op0=ALU.mult,
                                   op1=ALU.mult).then_inc(step, 1)
    nc.vector.tensor_scalar(mom[:, 4], mom[:, 2], 1.0 / D, eps, ALU.mult, ALU.add).then_inc(step, 1)
    dve.wait_ge(step, done + 5)
    nc.vector.tensor_tensor(var, mom[:, 3], mom[:, 4], ALU.add).then_inc(step, 1)


def setup_block(nc, ctx, dram, keep):
    st = ctx.enter_context(ExitStack())
    sb = lambda n, s, d=F32: st.enter_context(nc.sbuf_tensor(n, s, d))
    sem = lambda n: ctx.enter_context(nc.semaphore(n))
    raw1 = sb("raw1", [P, KT, HID])
    raw2 = sb("raw2", [P, HT, D])
    raw_wo = sb("raw_wo", [P, KT, D])
    raw_wg = sb("raw_wg", [P, KT, D])
    raw_wh = sb("raw_wh", [P, HEADS, P])
    raw_wht = sb("raw_wht", [P, HEADS, P])
    wht_hi, wht_lo = sb("wht_hi", [P, HEADS, P], F32R), sb("wht_lo", [P, HEADS, P], F32R)
    ones = sb("ones_f32", [P, P])
    wsum = sb("wsum", [P, 2])
    wrec = sb("wrec", [P, 2])
    ps_mean = st.enter_context(nc.psum_tensor("ps_mean", [P, 512], F32))
    ps_g = st.enter_context(nc.psum_tensor("ps_g", [P, 512], F32))
    vecs_in, ident_in, gam_in, wo_in, wg_in, wh_in, w1_in, w2_in, mask_in = (
        sem(n) for n in ("vecs_in", "ident_in", "gam_in", "wo_in", "wg_in", "wh_in", "w1_in", "w2_in", "mask_in"))
    hi_done, lo_done, g_done, ghi_done, ones_done, sum_done, mean_done, scale_done, clip_done = (
        sem(n) for n in ("hi_done", "lo_done", "g_done", "ghi_done", "ones_done", "sum_done",
                         "mean_done", "scale_done", "clip_done"))
    cuts = [(raw_wht, wht_hi, wht_lo, wh_in, 32), (raw_wh, keep["wh_hi"], keep["wh_lo"], wh_in, 32),
            (raw_wg, keep["wg_hi"], keep["wg_lo"], wg_in, 16), (raw_wo, keep["wo_hi"], keep["wo_lo"], wo_in, 16)]
    block = st.enter_context(nc.Block())

    @block.sync
    def _(sp):
        sp.dma_start(raw_wht[:], dram["whT"].rearrange("h e d -> e h d")).then_inc(wh_in, 16)
        sp.dma_start(raw_wh[:], dram["wh"].rearrange("h d e -> d h e")).then_inc(wh_in, 16)
        sp.dma_start(raw_wg[:], dram["wg"].rearrange("(k p) n -> p k n", p=P)).then_inc(wg_in, 16)
        sp.dma_start(raw1[:], dram["w1T"].rearrange("(k p) n -> p k n", p=P)).then_inc(w1_in, 16)
        sp.dma_start(raw2[:], dram["w2T"].rearrange("(k p) n -> p k n", p=P)).then_inc(w2_in, 16)

    @block.scalar
    def _(act):
        act.dma_start(keep["vecs"][:], dram["vecs"]).then_inc(vecs_in, 16)
        act.dma_start(keep["ident"][:], dram["ident"]).then_inc(ident_in, 16)
        act.dma_start(raw_wo[:], dram["wo"].rearrange("(k p) n -> p k n", p=P)).then_inc(wo_in, 16)
        act.dma_start(keep["mask"][:], dram["mask"]).then_inc(mask_in, 16)
        act.dma_start(keep["gam"][:], dram["gam"]).then_inc(gam_in, 16)
        act.wait_ge(vecs_in, 16)
        nc.scalar.activation(keep["gains"][:], keep["vecs"][:, V_GAIN:V_GAIN + 4], ACT.Tanh)
        for raw, hi, lo, arrived, n in cuts:
            act.wait_ge(arrived, n)
            nc.scalar.activation(hi[:], raw[:], ACT.Copy).then_inc(hi_done, 1)
        act.wait_ge(g_done, 1)
        nc.scalar.activation(keep["g_hi"][:], ps_g[:].rearrange("p (h d) -> p h d", h=HEADS), ACT.Copy).then_inc(ghi_done, 1)
        act.wait_ge(mask_in, 16)
        act.wait_ge(gam_in, 16)

    @block.gpsimd
    def _(pool):
        nc.gpsimd.memset(ones[:], 1.0).then_inc(ones_done, 1)
        pool.wait_ge(ident_in, 16)
        nc.gpsimd.tensor_copy(keep["identb"][:], keep["ident"][:])

    @block.vector
    def _(dve):
        for n, (raw, hi, lo, arrived, _) in enumerate(cuts):
            dve.wait_ge(hi_done, n + 1)
            nc.vector.tensor_tensor(lo[:], raw[:], f32(hi[:]), ALU.subtract).then_inc(lo_done, 1)
        dve.wait_ge(ghi_done, 1)
        nc.vector.tensor_tensor(keep["g_lo"][:], ps_g[:].rearrange("p (h d) -> p h d", h=HEADS), f32(keep["g_hi"][:]),
                                ALU.subtract)
        for n, (raw, arrived) in enumerate(((raw1, w1_in), (raw2, w2_in))):
            dve.wait_ge(arrived, 16)
            nc.vector.tensor_reduce(wsum[:, n:n + 1], raw[:].rearrange("p a b -> p (a b)"), AX.X, ALU.add,
                                    apply_absolute_value=True).then_inc(sum_done, 1)
        dve.wait_ge(mean_done, 1)
        nc.vector.tensor_scalar(keep["wmean"][:], ps_mean[:, 0:2], 1.0 / (D * HID), 1e-5, ALU.mult, ALU.max).then_inc(scale_done, 1)
        dve.wait_ge(scale_done, 1)
        nc.vector.reciprocal(wrec[:], keep["wmean"][:]).then_inc(scale_done, 1)
        dve.wait_ge(scale_done, 2)
        for n, (raw, out) in enumerate(((raw1, keep["w1q"]), (raw2, keep["w2q"]))):
            nc.vector.tensor_scalar(raw[:], raw[:], wrec[:, n:n + 1], 1.0, ALU.mult, ALU.min).then_inc(clip_done, 1)
            dve.wait_ge(clip_done, 3 * n + 1)
            nc.vector.tensor_scalar(raw[:], raw[:], -1.0, ROUND, ALU.max, ALU.add).then_inc(clip_done, 1)
            dve.wait_ge(clip_done, 3 * n + 2)
            nc.vector.tensor_scalar(out[:], raw[:], ROUND, None, ALU.subtract).then_inc(clip_done, 1)

    @block.tensor
    def _(pe):
        pe.wait_ge(lo_done, 1)
        for h in range(HEADS):
            last = products(nc, ps_g[:, h * P:(h + 1) * P], wht_hi[:, h], wht_lo[:, h], wht_hi[:, h], wht_lo[:, h], True, True)
        last.then_inc(g_done, 1)
        pe.wait_ge(ones_done, 1)
        pe.wait_ge(sum_done, 2)
        nc.tensor.matmul(ps_mean[:, 0:2], ones[:], wsum[:], start=True, stop=True).then_inc(mean_done, 1)

    st.close()


def scores_block(nc, ctx, dram, keep):
    st = ctx.enter_context(ExitStack())
    sb = lambda n, s, d=F32: st.enter_context(nc.sbuf_tensor(n, s, d))
    sem = lambda n: ctx.enter_context(nc.semaphore(n))
    x = sb("x", [P, TJ, D])
    xn = sb("xn", [P, TJ, D])
    xnT_hi, xnT_lo = sb("xnT_hi", [P, KT, CH], F32R), sb("xnT_lo", [P, KT, CH], F32R)
    c = sb("c", [P, KT, CH])
    c_hi, c_lo = sb("c_hi", [P, KT, CH], F32R), sb("c_lo", [P, KT, CH], F32R)
    q_hi, q_lo = sb("q_hi", [P, HEADS, CH], F32R), sb("q_lo", [P, HEADS, CH], F32R)
    gate = sb("gate", [P, KT, CH])
    val = sb("val", [P, TJ, D])
    zeros = sb("zeros", [P, CH], F32R)
    stats = sb("stats", [P, TJ, 6])
    mom = sb("mom", [P, 5, TJ])
    ve, rstd, shift, mhalf = (sb(n, [P, TJ]) for n in ("ve", "rstd", "shift", "mhalf"))
    acc = st.enter_context(nc.psum_tensor("acc", [P, HEADS, CH], F32))
    bank = [st.enter_context(nc.psum_tensor(f"bank{n}", [P, CH], F32)) for n in range(4)]
    USES = 4 + 4 + 4 + 4
    (x_in, c_in, stats_done, mom_done, rstd_done, shift_done, xn_done, chi_done, clo_done,
     filled, hi_done, xnT_done, val_done, gate_done, q_done, scores_done, consts_done, val_out,
     gate_out, mask_done, abs_done, a_done, ahi_done) = (sem("s_" + n) for n in (
         "x_in c_in stats_done mom_done rstd_done shift_done xn_done chi_done clo_done "
         "filled hi_done xnT_done val_done gate_done q_done scores_done consts_done val_out "
         "gate_out mask_done abs_done a_done ahi_done").split())
    x_v = dram["x"].rearrange("(i j p) d -> i p j d", j=TJ, p=P)
    c_v = dram["ctxT"].rearrange("(k p) (i n) -> i p k n", p=P, n=CH)
    block = st.enter_context(nc.Block())

    @block.sync
    def _(sp):
        def load(i):
            sp.wait_ge(xn_done, START + 4 * i)
            sp.dma_start(x[:], x_v[i]).then_inc(x_in, 16)
            sp.wait_ge(clo_done, START + i)
            sp.dma_start(c[:], c_v[i]).then_inc(c_in, 16)

        def store(i):
            sp.wait_ge(gate_done, 4 * (i + 1))
            sp.dma_start(dram["gates"][i], gate[:]).then_inc(gate_out, 16)
            sp.wait_ge(val_done, START + 4 * (i + 1))
            sp.dma_start(dram["vals"][i], val[:]).then_inc(val_out, 16)

        sp.sem_inc(gate_out, START)
        sp.sem_inc(val_out, START)
        load(0)
        with sp.Fori(0, NCH - 1) as i:
            load(i + 1)
            store(i)
        store(NCH - 1)
        sp.wait_ge(gate_out, START + 16 * NCH)
        sp.wait_ge(val_out, START + 16 * NCH)

    @block.gpsimd
    def _(pool):
        nc.gpsimd.memset(mhalf[:], -0.5).then_inc(consts_done, 1)
        nc.gpsimd.memset(f32(zeros[:]), 0.0).then_inc(consts_done, 1)
        pool.wait_ge(consts_done, 1)
        with pool.Fori(0, NCH) as i:
            pool.wait_ge(mom_done, 6 * i + 6)
            nc.gpsimd.tensor_tensor(rstd[:], ve[:], mhalf[:], ALU.pow).then_inc(rstd_done, 1)

    @block.scalar
    def _(act):
        act.sem_inc(xn_done, START)
        with act.Fori(0, NCH) as i:
            act.wait_ge(shift_done, i + 1)
            for j in range(TJ):
                nc.scalar.activation(xn[:, j], x[:, j], ACT.Identity, bias=shift[:, j:j + 1],
                                     scale=rstd[:, j:j + 1]).then_inc(xn_done, 1)
            act.wait_ge(c_in, 16 * (i + 1))
            act.wait_ge(scores_done, START + i)
            nc.scalar.activation(c_hi[:], c[:], ACT.Copy).then_inc(chi_done, 1)
            for k in range(KT):
                act.wait_ge(filled, USES * i + k + 1)
                nc.scalar.activation(xnT_hi[:, k], bank[k][:], ACT.Copy).then_inc(hi_done, 1)
            for h in range(HEADS):
                act.wait_ge(filled, USES * i + 11 + h)
                nc.scalar.activation(q_hi[:, h], bank[(10 + h) % 4][:], ACT.Copy).then_inc(hi_done, 1)

    @block.vector
    def _(dve):
        def evac(i, use, k, hi, lo, done):
            dve.wait_ge(hi_done, 8 * i + k + 1)
            nc.vector.tensor_tensor(lo, bank[use % 4][:], f32(hi), ALU.subtract).then_inc(done, 1)

        for s in (clo_done, q_done, val_done):
            dve.sem_inc(s, START)
        with dve.Fori(0, NCH) as i:
            dve.wait_ge(x_in, 16 * (i + 1))
            for j in range(TJ):
                nc.vector.bn_stats(stats[:, j], x[:, j]).then_inc(stats_done, 1)
            dve.wait_ge(stats_done, 4 * (i + 1))
            variance(nc, dve, stats, mom, ve[:], LN_EPS, mom_done, 6 * i)
            dve.wait_ge(rstd_done, i + 1)
            nc.vector.scalar_tensor_tensor(out=shift[:], in0=mom[:, 0], scalar=-0.5, in1=rstd[:], op0=ALU.mult,
                                           op1=ALU.mult).then_inc(shift_done, 1)
            dve.wait_ge(chi_done, i + 1)
            nc.vector.tensor_tensor(c_lo[:], c[:], f32(c_hi[:]), ALU.subtract).then_inc(clo_done, 1)
            for k in range(KT):
                evac(i, k, k, xnT_hi[:, k], xnT_lo[:, k], xnT_done)
            dve.wait_ge(val_out, START + 16 * i)
            for j in range(2):
                dve.wait_ge(filled, USES * i + 5 + j)
                nc.vector.tensor_copy(val[:, j], bank[j][:]).then_inc(val_done, 1)
            dve.wait_ge(gate_out, START + 16 * i)
            for m in range(KT):
                dve.wait_ge(filled, USES * i + 7 + m)
                nc.vector.tensor_scalar(gate[:, m], bank[(6 + m) % 4][:], 0.0, None, ALU.max).then_inc(gate_done, 1)
            for h in range(HEADS):
                evac(i, 10 + h, 4 + h, q_hi[:, h], q_lo[:, h], q_done)
            for j in range(2, 4):
                dve.wait_ge(filled, USES * i + 13 + j)
                nc.vector.tensor_copy(val[:, j], bank[j][:]).then_inc(val_done, 1)
        dve.wait_ge(scores_done, START + NCH)
        dve.wait_ge(gate_out, START + 16 * NCH)
        dve.wait_ge(val_out, START + 16 * NCH)
        for h in range(HEADS):
            nc.vector.tensor_tensor(gate[:, h], acc[:, h], keep["mask"][:, h], ALU.mult).then_inc(mask_done, 1)
            dve.wait_ge(mask_done, h + 1)
            nc.vector.scalar_tensor_tensor(out=val[:, h], in0=gate[:, h], scalar=-1.0, in1=gate[:, h], op0=ALU.mult,
                                           op1=ALU.max).then_inc(abs_done, 1)
            dve.wait_ge(abs_done, h + 1)
            nc.vector.tensor_scalar(val[:, h], val[:, h], 1.0, None, ALU.max).then_inc(a_done, 1)
            dve.wait_ge(a_done, h + 1)
            nc.vector.tensor_copy(keep["at_hi"][:, h], val[:, h]).then_inc(ahi_done, 1)
            dve.wait_ge(ahi_done, h + 1)
            nc.vector.tensor_tensor(keep["at_lo"][:, h], val[:, h], f32(keep["at_hi"][:, h]), ALU.subtract)

    @block.tensor
    def _(pe):
        pe.sem_inc(scores_done, START)
        pe.wait_ge(consts_done, 2)
        for h in range(HEADS):
            nc.tensor.matmul(acc[:, h], zeros[:, 0:P], zeros[:], start=True, stop=False, skip_group_check=True)

        def free(i, use):
            if use < 4:
                pe.wait_ge(q_done, START + 4 * i)
                pe.wait_ge(val_done, START + 4 * i)
            elif use < 8:
                pe.wait_ge(xnT_done, 4 * i + use - 3)
            elif use < 10:
                pe.wait_ge(val_done, START + 4 * i + use - 7)
            elif use < 14:
                pe.wait_ge(gate_done, 4 * i + use - 9)
            else:
                pe.wait_ge(q_done, START + 4 * i + use - 13)

        def values(i, j, use):
            free(i, use)
            for h in range(HEADS):
                last = products(nc, bank[use % 4][:, h * P:(h + 1) * P], c_hi[:, h, j * P:(j + 1) * P],
                                c_lo[:, h, j * P:(j + 1) * P], keep["wh_hi"][:, h], keep["wh_lo"][:, h], True, True)
            last.then_inc(filled, 1)

        with pe.Fori(0, NCH) as i:
            pe.wait_ge(xn_done, START + 4 * (i + 1))
            for k in range(KT):
                free(i, k)
                for j in range(TJ):
                    last = nc.tensor.transpose(bank[k][:, j * P:(j + 1) * P], xn[:, j, k * P:(k + 1) * P], keep["ident"][:])
                last.then_inc(filled, 1)
            pe.wait_ge(clo_done, START + i + 1)
            values(i, 0, 4)
            values(i, 1, 5)
            pe.wait_ge(xnT_done, 4 * (i + 1))
            for m in range(KT):
                free(i, 6 + m)
                for k in range(KT):
                    last = products(nc, bank[(6 + m) % 4][:], keep["wg_hi"][:, k, m * P:(m + 1) * P],
                                    keep["wg_lo"][:, k, m * P:(m + 1) * P], xnT_hi[:, k], xnT_lo[:, k], k == 0, k == KT - 1)
                last.then_inc(filled, 1)
            for h in range(HEADS):
                free(i, 10 + h)
                last = products(nc, bank[(10 + h) % 4][:], keep["g_hi"][:, h], keep["g_lo"][:, h], xnT_hi[:, h],
                                xnT_lo[:, h], True, True)
                last.then_inc(filled, 1)
            values(i, 2, 14)
            values(i, 3, 15)
            for h in range(HEADS):
                pe.wait_ge(q_done, START + 4 * i + h + 1)
                for b in range(2):
                    for t in range(2):
                        keys = slice(b * S + t * P, b * S + (t + 1) * P)
                        last = products(nc, acc[:, h, t * S:(t + 1) * S], c_hi[:, h, keys], c_lo[:, h, keys],
                                        q_hi[:, h, b * S:(b + 1) * S], q_lo[:, h, b * S:(b + 1) * S], False, False, skip=True)
            last.then_inc(scores_done, 1)

    st.close()


def attn_block(nc, ctx, dram, keep):
    st = ctx.enter_context(ExitStack())
    sb = lambda n, s, d=F32: st.enter_context(nc.sbuf_tensor(n, s, d))
    sem = lambda n: ctx.enter_context(nc.semaphore("a_" + n))
    START = 2
    x = sb("ax", [P, TJ, D])
    v = sb("av", [P, 2, 2, D])
    v_hi, v_lo = sb("av_hi", [P, 2, 2, D], F32R), sb("av_lo", [P, 2, 2, D], F32R)
    gate = sb("agate", [P, KT, CH])
    o = sb("ao", [P, TJ, D])
    og = sb("aog", [P, 2, CH])
    z = sb("az", [P, 2, CH])
    z_hi, z_lo = sb("az_hi", [P, KT, CH], F32R), sb("az_lo", [P, KT, CH], F32R)
    x1 = sb("ax1", [P, TJ, D])
    y = sb("ay", [P, TJ, D])
    yq = sb("ayq", [P, TJ, D], BF16)
    yqT = sb("ayqT", [P, KT, CH], BF16)
    h = sb("ah", [P, 2, HID])
    hq = sb("ahq", [P, 2, HID], BF16)
    hqT = sb("ahqT", [P, HT, P], BF16)
    x2 = sb("ax2", [P, TJ, D])
    x1_held = sb("ax1_held", [P, D])
    ostats, omom = sb("aostats", [P, 2, 6]), sb("aomom", [P, 5, 2])
    ove, orstd, oshift = (sb(n, [P, 2]) for n in ("aove", "aorstd", "aoshift"))
    stats, mom = sb("astats", [P, TJ, 6]), sb("amom", [P, 5, TJ])
    ve, rstd, sq, r2in, r2, scale, shift, amax, qrec, qscale, dq1 = (
        sb("a" + n, [P, TJ]) for n in "ve rstd sq r2in r2 scale shift amax qrec qscale dq1".split())
    hmax, hrec, hscale, dq2 = (sb("a" + n, [P, TJ]) for n in "hmax hrec hscale dq2".split())
    mhalf, rnd, dq2w = sb("amhalf", [P, TJ]), sb("arnd", [P, 1]), sb("adq2w", [P, 1])
    ps_o = st.enter_context(nc.psum_tensor("ps_o", [P, HEADS, 2, P], F32))
    ps_r = [st.enter_context(nc.psum_tensor(f"ps_r{n}", [P, CH], F32)) for n in range(2)]
    ps_t = st.enter_context(nc.psum_tensor("ps_t", [P, 2, 4, P], BF16))
    ps_h = [st.enter_context(nc.psum_tensor(f"ps_h{n}", [P, 512], F32)) for n in range(2)]
    ps_y = st.enter_context(nc.psum_tensor("ps_y", [P, D], F32))
    (v_in, gate_in, x_in, vhi_done, vlo_done, o_done, ostats_done, omom_done, orstd_done, oshift_done, on_done,
     oT_done, og_done, z_done, zhi_done, zlo_done, wo_done, x1_done, stats_done, mom_done, rstd_done, rms_step,
     r2_done, y_done, yg_done, amax_done, qs_done, round_done, yq_done, t_done, t_read, h_done, gelu_done,
     hmax_done, hs_done, hround_done, hq_done, mm2_done, x2_done, x2_out, consts_done, dq2w_done, shift_done, held_done) = (sem(n) for n in (
         "v_in gate_in x_in vhi_done vlo_done o_done ostats_done omom_done orstd_done oshift_done on_done "
         "oT_done og_done z_done zhi_done zlo_done wo_done x1_done stats_done mom_done rstd_done rms_step "
         "r2_done y_done yg_done amax_done qs_done round_done yq_done t_done t_read h_done gelu_done "
         "hmax_done hs_done hround_done hq_done mm2_done x2_done x2_out consts_done dq2w_done shift_done held_done").split())
    TU = 2 * TJ + 2
    x_v = dram["x"].rearrange("(c j p) d -> c p j d", j=TJ, p=P)
    x2_v = dram["x2"].rearrange("(c j p) d -> c j p d", j=TJ, p=P)

    def h_filling(c, j, f):
        return 2 + TU * c + 2 * j + f

    def y_filling(c, a):
        return 2 + TU * c + 2 * TJ + a if c is not None else a

    block = st.enter_context(nc.Block())

    @block.sync
    def _(sp):
        def load_v(n):
            sp.wait_ge(vlo_done, START + n)
            sp.dma_start(v[:].rearrange("p a b d -> p (a b) d"), dram["vals"][n]).then_inc(v_in, 16)

        def load_gate(n):
            sp.wait_ge(z_done, START + 4 * n)
            sp.dma_start(gate[:], dram["gates"][n]).then_inc(gate_in, 16)

        def load_x(n):
            sp.wait_ge(x1_done, START + 4 * n)
            sp.dma_start(x[:], x_v[n]).then_inc(x_in, 16)

        def round_(c, q, ahead):
            for j in range(TJ):
                sp.wait_ge(x2_done, START + 4 * c + j + 1)
                sp.dma_start(x2_v[c, j], x2[:, j]).then_inc(x2_out, 16)
                if ahead and j == 0:
                    load_v(q + 1)
                if ahead and j == 1:
                    load_gate(q + 1)
            if ahead:
                load_x(q + 1)

        sp.sem_inc(x2_out, START)
        for n in range(2):
            load_v(n)
            load_gate(n)
            load_x(n)
        with sp.Fori(0, NCH - 2) as c:
            round_(c, c + 1, True)
        round_(NCH - 2, NCH - 1, False)
        round_(NCH - 1, None, False)
        sp.wait_ge(x2_out, START + 16 * TJ * NCH)

    @block.gpsimd
    def _(pool):
        def cut_v(q):
            pool.wait_ge(vhi_done, q + 1)
            nc.gpsimd.tensor_tensor(v_lo[:], v[:], f32(v_hi[:]), ALU.subtract).then_inc(vlo_done, 1)

        def group_pow(q, s):
            pool.wait_ge(omom_done, 12 * q + 6 * s + 6)
            nc.gpsimd.tensor_tensor(orstd[:], ove[:], mhalf[:, 0:2], ALU.pow).then_inc(orstd_done, 1)

        def cut_z(q, k):
            pool.wait_ge(zhi_done, 4 * q + k + 1)
            nc.gpsimd.tensor_tensor(z_lo[:, k], z[:, k % 2], f32(z_hi[:, k]), ALU.subtract).then_inc(zlo_done, 1)

        def layer_pow(q, a):
            pool.wait_ge(mom_done, 12 * q + 6 * a + 6)
            cols = slice(2 * a, 2 * a + 2)
            nc.gpsimd.tensor_tensor(rstd[:, cols], ve[:, cols], mhalf[:, cols], ALU.pow).then_inc(rstd_done, 1)
            pool.wait_ge(rms_step, 6 * q + 3 * a + 3)
            nc.gpsimd.tensor_tensor(r2[:, cols], r2in[:, cols], mhalf[:, cols], ALU.pow).then_inc(r2_done, 1)

        def times_gain(q, a):
            for j in (2 * a, 2 * a + 1):
                pool.wait_ge(y_done, 4 * q + j + 1)
                nc.gpsimd.tensor_tensor(y[:, j], y[:, j], keep["gam"][:], ALU.mult).then_inc(yg_done, 1)

        def attention(q):
            cut_v(q)
            group_pow(q, 0)
            group_pow(q, 1)
            for k in range(KT):
                cut_z(q, k)
            for a in range(2):
                layer_pow(q, a)
                times_gain(q, a)

        for s in (vlo_done, zlo_done):
            pool.sem_inc(s, START)
        nc.gpsimd.memset(mhalf[:], -0.5).then_inc(consts_done, 1)
        nc.gpsimd.memset(rnd[:], ROUND).then_inc(consts_done, 1)
        pool.wait_ge(consts_done, 1)
        with pool.Fori(0, NCH) as q:
            attention(q)

    @block.scalar
    def _(act):
        def cut_v(q):
            act.wait_ge(v_in, 16 * (q + 1))
            nc.scalar.activation(v_hi[:], v[:], ACT.Copy).then_inc(vhi_done, 1)

        def group_norm(q, s):
            act.wait_ge(oshift_done, 2 * q + s + 1)
            for b in range(2):
                nc.scalar.activation(o[:, 2 * b + s].rearrange("p (h e) -> p h e", e=P), ps_o[:, :, b], ACT.Identity,
                                     bias=oshift[:, b:b + 1], scale=orstd[:, b:b + 1]).then_inc(on_done, 1)

        def times_gamma(q, k):
            act.wait_ge(oT_done, 4 * q + k + 1)
            act.wait_ge(z_done, START + 4 * q + k - 1)
            nc.scalar.activation(og[:, k % 2], ps_r[k % 2][:], ACT.Identity, bias=keep["vecs"][:, V_BETA + k:V_BETA + k + 1],
                                 scale=keep["vecs"][:, V_GAMMA + k:V_GAMMA + k + 1]).then_inc(og_done, 1)

        def cut_z(q, k):
            act.wait_ge(z_done, START + 4 * q + k + 1)
            nc.scalar.activation(z_hi[:, k], z[:, k % 2], ACT.Copy).then_inc(zhi_done, 1)

        def layer_norm(q, a):
            act.wait_ge(shift_done, 4 * q + 2 * a + 2)
            act.wait_ge(yq_done, START + 4 * q)
            for j in (2 * a, 2 * a + 1):
                nc.scalar.activation(y[:, j], x1[:, j], ACT.Identity, bias=shift[:, j:j + 1], scale=scale[:, j:j + 1]).then_inc(y_done, 1)

        def round_y(q, a):
            act.wait_ge(qs_done, 10 * q + 5 * a + 5)
            for j in (2 * a, 2 * a + 1):
                nc.scalar.activation(y[:, j], y[:, j], ACT.Identity, bias=rnd[:], scale=qscale[:, j:j + 1]).then_inc(round_done, 1)

        def gelu(c, j, ns=range(4)):
            act.wait_ge(hq_done, START + 4 * c + j - 1)
            for n in ns:
                act.wait_ge(h_done, 16 * c + 4 * j + n + 1)
                nc.scalar.activation(h[:, j % 2, n * 512:(n + 1) * 512], ps_h[n % 2][:], ACT.Gelu,
                                     scale=dq1[:, j:j + 1]).then_inc(gelu_done, 1)

        def round_h(c, j):
            act.wait_ge(hs_done, 4 * (4 * c + j + 1))
            nc.scalar.activation(h[:, j % 2], h[:, j % 2], ACT.Identity, bias=rnd[:], scale=hscale[:, j:j + 1]).then_inc(hround_done, 1)

        def hold_x1(c):
            act.wait_ge(x2_done, START + 4 * c)
            nc.scalar.activation(x1_held[:], x1[:, TJ - 1], ACT.Copy).then_inc(held_done, 1)

        for s in (gelu_done, on_done):
            act.sem_inc(s, START)
        act.wait_ge(consts_done, 2)
        cut_v(0)
        group_norm(0, 0)
        group_norm(0, 1)
        times_gamma(0, 0)
        times_gamma(0, 1)
        cut_z(0, 0)
        times_gamma(0, 2)
        cut_z(0, 1)
        times_gamma(0, 3)
        cut_z(0, 2)
        cut_z(0, 3)
        layer_norm(0, 0)
        round_y(0, 0)
        layer_norm(0, 1)
        round_y(0, 1)
        gelu(0, 0)

        def round_(c, q):
            last = q is None
            if not last:
                cut_v(q)
            gelu(c, 1, (0, 1))
            round_h(c, 0)
            gelu(c, 1, (2, 3))
            if not last:
                group_norm(q, 0)
            gelu(c, 2)
            if not last:
                group_norm(q, 1)
            round_h(c, 1)
            hold_x1(c)
            if not last:
                times_gamma(q, 0)
                times_gamma(q, 1)
                cut_z(q, 0)
                times_gamma(q, 2)
                cut_z(q, 1)
            gelu(c, 3, (0, 1))
            if not last:
                times_gamma(q, 3)
                cut_z(q, 2)
            gelu(c, 3, (2, 3))
            if not last:
                cut_z(q, 3)
            round_h(c, 2)
            round_h(c, 3)
            if not last:
                layer_norm(q, 0)
                round_y(q, 0)
                layer_norm(q, 1)
                gelu(q, 0)
                round_y(q, 1)

        with act.Fori(0, NCH - 1) as c:
            round_(c, c + 1)
        round_(NCH - 1, None)

    @block.vector
    def _(dve):
        def group_stats(q, s):
            dve.wait_ge(o_done, 2 * q + s + 1)
            for b in range(2):
                nc.vector.bn_stats(ostats[:, b], ps_o[:, :, b]).then_inc(ostats_done, 1)
            dve.wait_ge(ostats_done, 4 * q + 2 * s + 2)
            variance(nc, dve, ostats, omom, ove[:], GN_EPS, omom_done, 12 * q + 6 * s)

        def group_shift(q, s):
            dve.wait_ge(orstd_done, 2 * q + s + 1)
            dve.wait_ge(on_done, START + 4 * q + 2 * s)
            nc.vector.scalar_tensor_tensor(out=oshift[:], in0=omom[:, 0], scalar=-0.5, in1=orstd[:], op0=ALU.mult,
                                           op1=ALU.mult).then_inc(oshift_done, 1)

        def gated(q, k):
            if k == 0:
                dve.wait_ge(gate_in, 16 * (q + 1))
            dve.wait_ge(og_done, 4 * q + k + 1)
            if k >= 2:
                dve.wait_ge(zlo_done, START + 4 * q + k - 1)
            nc.vector.tensor_tensor(z[:, k % 2], og[:, k % 2], gate[:, k], ALU.mult).then_inc(z_done, 1)

        def add_x(q, j, c=None):
            dve.wait_ge(wo_done, 4 * q + j + 1)
            if j == 0:
                dve.wait_ge(x_in, 16 * (q + 1))
            if c is not None and j < TJ - 1:
                dve.wait_ge(x2_done, START + 4 * c + j + 1)
            if c is not None and j == TJ - 1:
                dve.wait_ge(held_done, c + 1)
            nc.vector.scalar_tensor_tensor(out=x1[:, j], in0=ps_r[j % 2][:], scalar=keep["gains"][:, 0:1], in1=x[:, j],
                                           op0=ALU.mult, op1=ALU.add).then_inc(x1_done, 1)
            dve.wait_ge(x1_done, START + 4 * q + j + 1)
            nc.vector.bn_stats(stats[:, j], x1[:, j]).then_inc(stats_done, 1)

        def pair_variance(q, a):
            cols = slice(2 * a, 2 * a + 2)
            dve.wait_ge(stats_done, 4 * q + 2 * a + 2)
            variance(nc, dve, stats[:, cols], mom[:, :, cols], ve[:, cols], LN_EPS, mom_done, 12 * q + 6 * a)

        def pair_rms(q, a):
            cols = slice(2 * a, 2 * a + 2)
            n = 6 * q + 3 * a
            dve.wait_ge(rstd_done, 2 * q + a + 1)
            nc.vector.tensor_tensor(sq[:, cols], rstd[:, cols], rstd[:, cols], ALU.mult).then_inc(rms_step, 1)
            dve.wait_ge(rms_step, n + 1)
            nc.vector.scalar_tensor_tensor(out=r2in[:, cols], in0=ve[:, cols], scalar=LN_EPS, in1=sq[:, cols], op0=ALU.subtract,
                                           op1=ALU.mult).then_inc(rms_step, 1)
            dve.wait_ge(rms_step, n + 2)
            nc.vector.tensor_scalar(r2in[:, cols], r2in[:, cols], RMS_EPS, None, ALU.add).then_inc(rms_step, 1)

        def pair_shift(q, a):
            cols = slice(2 * a, 2 * a + 2)
            dve.wait_ge(r2_done, 2 * q + a + 1)
            nc.vector.tensor_tensor(scale[:, cols], rstd[:, cols], r2[:, cols], ALU.mult).then_inc(shift_done, 1)
            dve.wait_ge(shift_done, 4 * q + 2 * a + 1)
            nc.vector.scalar_tensor_tensor(out=shift[:, cols], in0=mom[:, 0, cols], scalar=-0.5, in1=scale[:, cols], op0=ALU.mult,
                                           op1=ALU.mult).then_inc(shift_done, 1)

        def pair_scale(q, a):
            cols = slice(2 * a, 2 * a + 2)
            n = 10 * q + 5 * a
            dve.wait_ge(yg_done, 4 * q + 2 * a + 2)
            nc.vector.tensor_reduce(amax[:, cols], y[:, cols], AX.X, ALU.max, apply_absolute_value=True).then_inc(amax_done, 1)
            dve.wait_ge(amax_done, 2 * q + a + 1)
            nc.vector.tensor_scalar(amax[:, cols], amax[:, cols], 1e-5, None, ALU.max).then_inc(qs_done, 1)
            dve.wait_ge(qs_done, n + 1)
            nc.vector.reciprocal(qrec[:, cols], amax[:, cols]).then_inc(qs_done, 1)
            nc.vector.tensor_scalar(dq1[:, cols], amax[:, cols], 1.0 / QMAX, keep["wmean"][:, 0:1], ALU.mult, ALU.mult).then_inc(qs_done, 2)
            dve.wait_ge(qs_done, n + 4)
            nc.vector.tensor_scalar(qscale[:, cols], qrec[:, cols], QMAX, None, ALU.mult).then_inc(qs_done, 1)

        def pair_bf16(q, a):
            for j in (2 * a, 2 * a + 1):
                dve.wait_ge(round_done, 4 * q + j + 1)
                nc.vector.tensor_scalar(yq[:, j], y[:, j], ROUND, None, ALU.subtract).then_inc(yq_done, 1)

        def read_yT(c, a):
            dve.wait_ge(t_done, y_filling(c, a) + 1)
            nc.vector.tensor_copy(yqT[:, :, 2 * a * P:(2 * a + 2) * P].rearrange("p k (j n) -> p j k n", n=P),
                                  ps_t[:]).then_inc(t_read, 1)

        def scale_h(c, j):
            col = slice(j, j + 1)
            dve.wait_ge(gelu_done, START + 16 * c + 4 * j + 4)
            nc.vector.tensor_reduce(hmax[:, col], h[:, j % 2], AX.X, ALU.max, apply_absolute_value=True).then_inc(hmax_done, 1)
            n = 4 * (4 * c + j)
            dve.wait_ge(hmax_done, 4 * c + j + 1)
            nc.vector.tensor_scalar(hmax[:, col], hmax[:, col], 1e-5, None, ALU.max).then_inc(hs_done, 1)
            dve.wait_ge(hs_done, n + 1)
            nc.vector.reciprocal(hrec[:, col], hmax[:, col]).then_inc(hs_done, 1)
            nc.vector.tensor_scalar(dq2[:, col], hmax[:, col], dq2w[:], None, ALU.mult).then_inc(hs_done, 1)
            dve.wait_ge(hs_done, n + 3)
            nc.vector.tensor_scalar(hscale[:, col], hrec[:, col], QMAX, None, ALU.mult).then_inc(hs_done, 1)

        def to_bf16(c, j):
            dve.wait_ge(hround_done, 4 * c + j + 1)
            nc.vector.tensor_scalar(hq[:, j % 2], h[:, j % 2], ROUND, None, ALU.subtract).then_inc(hq_done, 1)

        def read_hT(c, j, fs):
            for f in fs:
                dve.wait_ge(t_done, h_filling(c, j, f) + 1)
                if f == 0:
                    dve.wait_ge(mm2_done, START + 4 * c + j)
                nc.vector.tensor_copy(hqT[:, 8 * f:8 * f + 8], ps_t[:].rearrange("p a b n -> p (a b) n")).then_inc(t_read, 1)

        def residual(c, j):
            if j == 0:
                dve.wait_ge(x2_out, START + 16 * TJ * c)
            if j == TJ - 1:
                dve.wait_ge(held_done, c + 1)
            dve.wait_ge(mm2_done, START + 4 * c + j + 1)
            nc.vector.scalar_tensor_tensor(out=x2[:, j], in0=ps_y[:], scalar=dq2[:, j:j + 1],
                                           in1=x1[:, j] if j < TJ - 1 else x1_held[:], op0=ALU.mult,
                                           op1=ALU.add).then_inc(x2_done, 1)

        for s in (z_done, x1_done, hq_done, t_read, x2_done, yq_done):
            dve.sem_inc(s, START)
        nc.vector.tensor_scalar(dq2w[:], keep["wmean"][:, 1:2], keep["gains"][:, 2:3], 1.0 / QMAX, ALU.mult, ALU.mult).then_inc(dq2w_done, 1)
        dve.wait_ge(dq2w_done, 1)
        for s in range(2):
            group_stats(0, s)
            group_shift(0, s)
        for k in range(KT):
            gated(0, k)
        for a in range(2):
            add_x(0, 2 * a)
            add_x(0, 2 * a + 1)
            pair_variance(0, a)
            pair_rms(0, a)
            pair_shift(0, a)
            pair_scale(0, a)
            pair_bf16(0, a)
            read_yT(None, a)

        def round_(c, q):
            last = q is None
            scale_h(c, 0)
            to_bf16(c, 0)
            if not last:
                group_stats(q, 0)
                group_shift(q, 0)
            read_hT(c, 0, (0,))
            read_hT(c, 0, (1,))
            if not last:
                group_stats(q, 1)
                group_shift(q, 1)
            scale_h(c, 1)
            residual(c, 0)
            to_bf16(c, 1)
            if not last:
                gated(q, 0)
                gated(q, 1)
            read_hT(c, 1, (0,))
            if not last:
                gated(q, 2)
            read_hT(c, 1, (1,))
            if not last:
                gated(q, 3)
            scale_h(c, 2)
            residual(c, 1)
            to_bf16(c, 2)
            read_hT(c, 2, (0,))
            scale_h(c, 3)
            if not last:
                add_x(q, 0, c)
            read_hT(c, 2, (1,))
            if not last:
                add_x(q, 1, c)
                pair_variance(q, 0)
            to_bf16(c, 3)
            if not last:
                pair_rms(q, 0)
            residual(c, 2)
            if not last:
                pair_shift(q, 0)
                add_x(q, 2, c)
            read_hT(c, 3, (0,))
            if not last:
                add_x(q, 3, c)
                pair_variance(q, 1)
            read_hT(c, 3, (1,))
            if not last:
                pair_scale(q, 0)
                pair_rms(q, 1)
                pair_bf16(q, 0)
                pair_shift(q, 1)
            residual(c, 3)
            if not last:
                read_yT(c, 0)
                pair_scale(q, 1)
                pair_bf16(q, 1)
                read_yT(c, 1)

        with dve.Fori(0, NCH - 1) as c:
            round_(c, c + 1)
        round_(NCH - 1, None)

    @block.tensor
    def _(pe):
        def retention(q, s):
            if s == 0:
                pe.wait_ge(vlo_done, START + q + 1)
            pe.wait_ge(on_done, START + 4 * q + 2 * s)
            for h_ in range(HEADS):
                for t in range(2):
                    cols = slice(t * S + s * P, t * S + (s + 1) * P)
                    last = products(nc, ps_o[:, h_], keep["at_hi"][:, h_, cols], keep["at_lo"][:, h_, cols],
                                    v_hi[:, :, t, h_ * P:(h_ + 1) * P], v_lo[:, :, t, h_ * P:(h_ + 1) * P], t == 0, t == 1,
                                    skip=True)
            last.then_inc(o_done, 1)

        def turn_o(q, k):
            if k == 0:
                pe.wait_ge(on_done, START + 4 * q + 4)
            if k < 2:
                pe.wait_ge(x1_done, START + 4 * q)
            else:
                pe.wait_ge(og_done, 4 * q + k - 1)
            for j in range(TJ):
                last = nc.tensor.transpose(ps_r[k % 2][:, j * P:(j + 1) * P], o[:, j, k * P:(k + 1) * P], keep["ident"][:])
            last.then_inc(oT_done, 1)

        def project(q, j):
            if j == 0:
                pe.wait_ge(zlo_done, START + 4 * q + 4)
            if j < 2:
                pe.wait_ge(og_done, 4 * q + 3 + j)
            else:
                pe.wait_ge(x1_done, START + 4 * q + j - 1)
            for k in range(KT):
                last = products(nc, ps_r[j % 2][:], z_hi[:, k, j * P:(j + 1) * P], z_lo[:, k, j * P:(j + 1) * P],
                                keep["wo_hi"][:, k], keep["wo_lo"][:, k], k == 0, k == KT - 1)
            last.then_inc(wo_done, 1)

        def turn_y(q, c, a):
            pe.wait_ge(yq_done, START + 4 * q + 2 * a + 2)
            pe.wait_ge(t_read, START + y_filling(c, a))
            for j in range(2):
                for k in range(KT):
                    last = nc.tensor.transpose(ps_t[:, j, k], yq[:, 2 * a + j, k * P:(k + 1) * P], keep["identb"][:])
            last.then_inc(t_done, 1)

        def mm1(c, j, ready, ns=range(4)):
            pe.wait_ge(t_read, START + ready)
            for n in ns:
                pe.wait_ge(gelu_done, START + 16 * c + 4 * j + n - 1)
                for k in range(KT):
                    last = nc.tensor.matmul(ps_h[n % 2][:], yqT[:, k, j * P:(j + 1) * P], keep["w1q"][:, k, n * 512:(n + 1) * 512],
                                            start=(k == 0), stop=(k == KT - 1))
                last.then_inc(h_done, 1)

        def turn_h(c, j, f):
            pe.wait_ge(hq_done, START + 4 * c + j + 1)
            pe.wait_ge(t_read, START + h_filling(c, j, f))
            for m in range(8):
                last = nc.tensor.transpose(ps_t[:, m // 4, m % 4], hq[:, j % 2, (8 * f + m) * P:(8 * f + m + 1) * P], keep["identb"][:])
            last.then_inc(t_done, 1)

        def mm2(c, j):
            pe.wait_ge(x2_done, START + 4 * c + j)
            for f in range(2):
                pe.wait_ge(t_read, START + h_filling(c, j, f) + 1)
                for k in range(8 * f, 8 * f + 8):
                    last = nc.tensor.matmul(ps_y[:], hqT[:, k], keep["w2q"][:, k], start=(k == 0), stop=(k == HT - 1))
            last.then_inc(mm2_done, 1)

        pe.sem_inc(mm2_done, START)
        retention(0, 0)
        retention(0, 1)
        for k in range(KT):
            turn_o(0, k)
        for j in range(TJ):
            project(0, j)
        turn_y(0, None, 0)
        turn_y(0, None, 1)
        mm1(0, 0, 1)

        def round_(c, q):
            last = q is None
            before = h_filling(c, 0, 0)
            mm1(c, 1, before)
            if not last:
                retention(q, 0)
            turn_h(c, 0, 0)
            mm1(c, 2, before, (0, 1))
            turn_h(c, 0, 1)
            if not last:
                retention(q, 1)
            mm1(c, 2, before, (2, 3))
            mm2(c, 0)
            if not last:
                turn_o(q, 0)
                turn_o(q, 1)
            turn_h(c, 1, 0)
            if not last:
                turn_o(q, 2)
            turn_h(c, 1, 1)
            if not last:
                turn_o(q, 3)
            mm1(c, 3, before)
            mm2(c, 1)
            turn_h(c, 2, 0)
            if not last:
                project(q, 0)
            turn_h(c, 2, 1)
            if not last:
                project(q, 1)
            mm2(c, 2)
            if not last:
                project(q, 2)
            turn_h(c, 3, 0)
            if not last:
                project(q, 3)
            turn_h(c, 3, 1)
            mm2(c, 3)
            if not last:
                turn_y(q, c, 0)
                mm1(q, 0, y_filling(c, 0) + 1)
                turn_y(q, c, 1)

        with pe.Fori(0, NCH - 1) as c:
            round_(c, c + 1)
        round_(NCH - 1, None)

    st.close()


def experts_block(nc, ctx, dram, keep):
    st = ctx.enter_context(ExitStack())
    sb = lambda n, s, d=F32: st.enter_context(nc.sbuf_tensor("e_" + n, s, d))
    ps = lambda n, s: st.enter_context(nc.psum_tensor("e_" + n, s, F32))
    sem = lambda n: ctx.enter_context(nc.semaphore("e_" + n))
    START = 2
    gu_raw, gu_hi, gu_lo = sb("gu_raw", [P, 2, 2, KT, P]), sb("gu_hi", [P, 2, 2, KT, P], F32R), sb("gu_lo", [P, 2, 2, KT, P], F32R)
    dn_raw, dn_hi, dn_lo = sb("dn_raw", [P, 2, D]), sb("dn_hi", [P, 2, D], F32R), sb("dn_lo", [P, 2, D], F32R)
    x = sb("x", [P, TJ, D])
    xq = sb("xq", [P, TJ, D])
    x2T = sb("x2T", [P, KT, CH])
    qe = sb("qe", [P, KT * B * CHD, EXT])
    c = sb("c", [P, KT, CH])
    ke = sb("ke", [P, KT * B, EXT])
    kv_raw = sb("kv_raw", [P, 2, B, PAIRS])
    kv_hi, kv_lo = sb("kv_hi", [P, KT, B, PAIRS], F32R), sb("kv_lo", [P, KT, B, PAIRS], F32R)
    t_raw, t_hi, t_lo = sb("t_raw", [P, D]), sb("t_hi", [P, D], F32R), sb("t_lo", [P, D], F32R)
    ZW, ZROW = 160, 20
    zp = sb("zp", [P, B, ZW])
    skip = sb("skip", [P, NCH * CHD])
    x3T = sb("x3T", [P, KT, CH])
    xnat = sb("xnat", [P, TJ, D])
    xn_hi, xn_lo = sb("xn_hi", [P, KT, CH], F32R), sb("xn_lo", [P, KT, CH], F32R)
    wb = sb("wb", [P, NE, CH])
    wT_hi, wT_lo = sb("wT_hi", [8, CH], F32R), sb("wT_lo", [8, CH], F32R)
    sg, sgw, hd = sb("sg", [P, CH]), sb("sgw", [P, CH]), sb("hd", [P, CH])
    hd_hi, hd_lo = sb("hd_hi", [P, 2, CH], F32R), sb("hd_lo", [P, 2, CH], F32R)
    y = sb("y", [P, KT, CH])
    bd_raw, bd_hi, bd_lo = hd[0:8], sb("bd_hi", [8, D], F32R), sb("bd_lo", [8, D], F32R)
    sel_raw, sel = y[0:8, 0:2].rearrange("p k n -> p (k n)")[:, 0:NE * P], sb("sel", [8, NE * P], F32R)
    wr_raw, wr_hi, wr_lo = xnat[:, 0:KT, 0:8], sb("wr_hi", [P, KT, 8], F32R), sb("wr_lo", [P, KT, 8], F32R)
    lg, lx, rank, keepw, ew, w = (sb(n, [P, TJ, 8]) for n in "lg lx rank keepw ew w".split())
    ge, gt, below, above = (sb(n, [P, 4 * 64]) for n in "ge gt below above".split())
    lmax, wsum, wrec = (sb(n, [P, TJ]) for n in "lmax wsum wrec".split())
    base_e = sb("base_e", [P, TJ * 8])
    stats, mom = sb("stats", [P, TJ, 6]), sb("mom", [P, 5, TJ])
    ve, rstd, shift, mhalf = (sb(n, [P, TJ]) for n in "ve rstd shift mhalf".split())
    pstats, pmom = sb("pstats", [P, 2, 6]), sb("pmom", [P, 5, 2])
    pve, prstd, pshift = (sb(n, [P, 2]) for n in "pve prstd pshift".split())
    gb = sb("gb", [P, KT])

    ps_out = ps("ps_out", [P, KT, CH])
    ps_g, ps_u, ps_m = ps("ps_g", [P, CH]), ps("ps_u", [P, CH]), ps("ps_m", [P, 2, CH])
    m_units = ps_m[:].rearrange("p a (b n) -> p (a b) n", n=64)

    names = ("const_in const_done setup_hi setup_lo gb_done guhi_done gulo_done dnhi_done dnlo_done gate_done gu_done "
             "silu_done sgw_done stt_done hdhi_done hdlo_done down_done y_copied y_done y_out x_in c_in t_in "
             "stats_done mom_done rstd_done shift_done xq_done x2T_filled x2T_done q_filled qe_done ke_done kvraw_done "
             "kvhi_done kvlo_done td_done thi_done tlo_done unit_done prod_done red_done x3_done nat_filled pstats_done "
             "pmom_done prstd_done pshift_done xnat_done xnT_filled xnhi_done xn_done lg_filled lg_done rt exp_done w_done "
             "wT_filled wThi_done wT_done wb_filled wb_done")
    (const_in, const_done, setup_hi, setup_lo, gb_done, guhi_done, gulo_done, dnhi_done, dnlo_done, gate_done, gu_done,
     silu_done, sgw_done, stt_done, hdhi_done, hdlo_done, down_done, y_copied, y_done, y_out, x_in, c_in, t_in,
     stats_done, mom_done, rstd_done, shift_done, xq_done, x2T_filled, x2T_done, q_filled, qe_done, ke_done, kvraw_done,
     kvhi_done, kvlo_done, td_done, thi_done, tlo_done, unit_done, prod_done, red_done, x3_done, nat_filled, pstats_done,
     pmom_done, prstd_done, pshift_done, xnat_done, xnT_filled, xnhi_done, xn_done, lg_filled, lg_done, rt, exp_done, w_done,
     wT_filled, wThi_done, wT_done, wb_filled, wb_done) = (sem(n) for n in names.split())
    gu_in, dn_in = ([sem(n + "0"), sem(n + "1")] for n in ("gu_in", "dn_in"))
    RT = 15

    def view(t, offset, *dims):
        return bass.AP(t[:].tensor, t[:].offset + offset, [list(t[:].ap[0])] + [list(d) for d in dims])

    FIRST_UNIT_STEP = 2
    UNITS = {FIRST_UNIT_STEP: [0]}
    u = 1
    for s in range(3, 13):
        UNITS[s] = list(range(u, u + (2 if s % 2 else 1)))
        u += len(UNITS[s])
    assert u == CHD * KT
    T_STEPS = (3, 5, 8)
    routed = lambda s: s < RSTEPS
    block = st.enter_context(nc.Block())

    @block.sync
    def _(sp):
        def load_gu(g, s):
            n = STEPS * g + s
            s %= STEPS
            sp.wait_ge(gulo_done, START + n - 1)
            if routed(s):
                sp.dma_start(gu_raw[:, s % 2].rearrange("p a k n -> p (a k n)"), dram["mgu"][s]).then_inc(gu_in[s % 2], 16)
            else:
                sp.dma_start(gu_raw[:, s % 2, 1].rearrange("p k n -> p (k n)"), dram["msu"][s - RSTEPS]).then_inc(gu_in[s % 2], 16)

        def load_dn(g, s):
            n = STEPS * g + s
            s %= STEPS
            sp.wait_ge(dnlo_done, START + n - 1)
            sp.dma_start(dn_raw[:, s % 2], dram["md"][s]).then_inc(dn_in[s % 2], 16)

        def load_x(q):
            sp.wait_ge(xq_done, START + 4 * q)
            sp.wait_ge(x2T_done, START + 2 * q)
            for j in range(TJ):
                sp.dma_start(x[:, j],
                             dram["x2"].rearrange("(j b g r) d -> g j b r d", j=TJ, b=4, g=NCH)[q, j]).then_inc(x_in, 16)

        def load_c(q):
            sp.wait_ge(ke_done, START + 2 * CHD * q)
            sp.dma_start(c[:], dram["ctxG"].rearrange("g (k p) n -> g p k n", p=P)[q]).then_inc(c_in, 16)

        def load_t(q, hh):
            sp.wait_ge(tlo_done, START + CHD * q + hh)
            sp.dma_start(t_raw[:], dram["toep"][CHD * q + hh]).then_inc(t_in, 16)

        def store(g):
            sp.wait_ge(y_done, START + 4 * g + 4)
            sp.dma_start(dram["out"].rearrange("g (k p) n -> g p k n", p=P)[g], y[:]).then_inc(y_out, 16)

        sp.sem_inc(y_out, START)
        for t, name in ((bd_raw, "bdown"), (sel_raw, "sel"), (wr_raw, "wroute"), (below[:], "below"), (above[:], "above"),
                        (skip[:], "skipD")):
            sp.dma_start(t, dram[name]).then_inc(const_in, 16)
        load_x(0)
        load_c(0)
        load_gu(0, 0)
        load_dn(0, 0)
        load_gu(0, 1)
        for hh in range(CHD):
            load_t(0, hh)
        load_x(1)
        load_c(1)
        load_t(1, 0)

        def round_(g, q, ahead):
            for s in range(STEPS):
                if q is not None or s < STEPS - 2:
                    load_gu(g, s + 2)
                if q is not None or s < STEPS - 1:
                    load_dn(g, s + 1)
                if q is not None and s in T_STEPS:
                    load_t(q, T_STEPS.index(s) + 1)
                if ahead and s == 2:
                    load_x(q + 1)
                if ahead and s == 11:
                    load_c(q + 1)
                    load_t(q + 1, 0)
            store(g)

        with sp.Fori(0, NCH - 2) as g:
            round_(g, g + 1, True)
        round_(NCH - 2, NCH - 1, False)
        round_(NCH - 1, None, False)
        sp.wait_ge(y_out, START + 16 * NCH)

    @block.gpsimd
    def _(pool):
        def cut_gu(g, s):
            n = STEPS * g + s
            s %= STEPS
            pool.wait_ge(guhi_done, n + 1)
            a = slice(0 if routed(s) else 1, 2)
            nc.gpsimd.tensor_tensor(gu_lo[:, s % 2, a], gu_raw[:, s % 2, a], f32(gu_hi[:, s % 2, a]), ALU.subtract).then_inc(gulo_done, 1)

        def cut_dn(g, s):
            n = STEPS * g + s
            pool.wait_ge(dnhi_done, n + 1)
            nc.gpsimd.tensor_tensor(dn_lo[:, s % 2], dn_raw[:, s % 2], f32(dn_hi[:, s % 2]), ALU.subtract).then_inc(dnlo_done, 1)

        def weigh(g, s):
            if not routed(s):
                return
            pool.wait_ge(silu_done, START + STEPS * g + s + 1)
            pool.wait_ge(wb_done, START + 3 * g + s // 4 + 1)
            pool.wait_ge(stt_done, START + RSTEPS * g + s)
            nc.gpsimd.tensor_tensor(sgw[:], sg[:], wb[:, s // 2], ALU.mult).then_inc(sgw_done, 1)

        def pairs(q, u):
            v = CHD * KT * q + u
            m = u % KT
            pool.wait_ge(ke_done, START + 2 * (CHD * q + u // KT + 1))
            pool.wait_ge(kvlo_done, START + v - 1)
            out = kv_raw[:, u % 2]
            nc.gpsimd.tensor_tensor(out[:, :, 0:32].rearrange("p b (d i) -> p b d i", i=CD),
                                    view(ke, m * B * EXT, (EXT, B), (0, 4), (1, CD)),
                                    view(ke, m * B * EXT, (EXT, B), (1, 4), (1, CD)), ALU.mult).then_inc(kvraw_done, 1)
            nc.gpsimd.tensor_tensor(out[:, :, 32:36], ke[:, m * B:(m + 1) * B, 0:4], ke[:, m * B:(m + 1) * B, 4:8],
                                    ALU.mult).then_inc(kvraw_done, 1)

        def conv_pow(q):
            pool.wait_ge(mom_done, 6 * q + 6)
            nc.gpsimd.tensor_tensor(rstd[:], ve[:], mhalf[:], ALU.pow).then_inc(rstd_done, 1)

        def nat_pow(q, a):
            pool.wait_ge(pmom_done, 12 * q + 6 * a + 6)
            nc.gpsimd.tensor_tensor(prstd[:], pve[:], mhalf[:, 0:2], ALU.pow).then_inc(prstd_done, 1)

        def exp(q):
            pool.wait_ge(rt, RT * q + 9)
            nc.gpsimd.tensor_tensor(ew[:], base_e[:].rearrange("p (j e) -> p j e", e=8), lx[:], ALU.pow).then_inc(exp_done, 1)

        for s in (gulo_done, dnlo_done, sgw_done, kvraw_done):
            pool.sem_inc(s, START)
        nc.gpsimd.memset(mhalf[:], -0.5).then_inc(const_done, 1)
        nc.gpsimd.memset(base_e[:], 2.718281828459045).then_inc(const_done, 1)
        pool.wait_ge(const_done, 2)
        conv_pow(0)
        cut_gu(0, 0)
        pairs(0, 0)
        pairs(0, 1)
        for u in range(CHD * KT):
            if u + 2 < CHD * KT:
                pairs(0, u + 2)
        nat_pow(0, 0)
        nat_pow(0, 1)
        exp(0)

        def round_(g, q):
            for s in range(STEPS):
                units = UNITS.get(s, []) if q is not None else []
                if q is not None or s < STEPS - 1:
                    cut_gu(g, s + 1)
                cut_dn(g, s)
                weigh(g, s)
                if q is not None and s == 0:
                    conv_pow(q)
                if q is not None and s in (1, 2):
                    pairs(q, s - 1)
                for u in units:
                    if u + 2 < CHD * KT:
                        pairs(q, u + 2)
                if q is not None and s in (13, 14):
                    nat_pow(q, s - 13)
            if q is not None:
                exp(q)

        with pool.Fori(0, NCH - 1) as g:
            round_(g, g + 1)
        round_(NCH - 1, None)

    @block.scalar
    def _(act):
        vecs = keep["vecs"]

        def cut_gu(g, s):
            n = STEPS * g + s
            act.wait_ge(gu_in[s % 2], 16 * (STEPS // 2 * g + s // 2 + 1))
            s %= STEPS
            act.wait_ge(gu_done, START + n - 1)
            a = slice(0 if routed(s) else 1, 2)
            nc.scalar.activation(gu_hi[:, s % 2, a], gu_raw[:, s % 2, a], ACT.Copy).then_inc(guhi_done, 1)

        def cut_dn(g, s):
            n = STEPS * g + s
            act.wait_ge(dn_in[s % 2], 16 * (STEPS // 2 * g + s // 2 + 1))
            act.wait_ge(down_done, START + n - 1)
            nc.scalar.activation(dn_hi[:, s % 2], dn_raw[:, s % 2], ACT.Copy).then_inc(dnhi_done, 1)

        def silu(g, s):
            n = STEPS * g + s
            if routed(s):
                act.wait_ge(gate_done, RSTEPS * g + s + 1)
                act.wait_ge(sgw_done, START + RSTEPS * g + s)
                nc.scalar.activation(sg[:], ps_g[:], ACT.Silu, bias=vecs[:, V_BG + s:V_BG + s + 1]).then_inc(silu_done, 1)
            else:
                act.wait_ge(gu_done, START + n + 1)
                act.wait_ge(hdlo_done, START + n)
                nc.scalar.activation(hd[:], ps_u[:], ACT.Silu,
                                     bias=vecs[:, V_BSU + s - RSTEPS:V_BSU + s - RSTEPS + 1]).then_inc(silu_done, 1)

        def cut_hd(g, s):
            n = STEPS * g + s
            if routed(s):
                act.wait_ge(stt_done, START + RSTEPS * g + s + 1)
            else:
                act.wait_ge(silu_done, START + n + 1)
            act.wait_ge(down_done, START + n - 1)
            nc.scalar.activation(hd_hi[:, s % 2], hd[:], ACT.Copy).then_inc(hdhi_done, 1)

        def norm_x(q):
            act.wait_ge(shift_done, q + 1)
            act.wait_ge(q_filled, START + 2 * q)
            for j in range(TJ):
                nc.scalar.activation(xq[:, j], x[:, j], ACT.Identity, bias=shift[:, j:j + 1], scale=rstd[:, j:j + 1]).then_inc(xq_done, 1)

        def read_x2T(q, a):
            act.wait_ge(x2T_filled, 2 * q + a + 1)
            act.wait_ge(x3_done, START + q)
            nc.scalar.activation(x2T[:, 2 * a:2 * a + 2], ps_m[:], ACT.Copy).then_inc(x2T_done, 1)

        def read_q(q, a):
            act.wait_ge(q_filled, START + 2 * q + a + 1)
            act.wait_ge(prod_done, START + 4 * CHD * KT * q)
            half = B * CHD * 2
            src = ps_m[:].rearrange("p a (n i) -> p (a n) i", i=CD)
            nc.scalar.activation(qe[:, half * a:half * (a + 1), 0:CD], src, ACT.Copy).then_inc(qe_done, 1)
            nc.scalar.activation(qe[:, half * a:half * (a + 1), CD:EXT], src[:, :, 0:EXT - CD], ACT.Copy).then_inc(qe_done, 1)

        def keys(q, hh):
            n = CHD * q + hh
            act.wait_ge(c_in, 16 * (q + 1))
            act.wait_ge(kvraw_done, START + 2 * KT * n)
            src = c[:].rearrange("p k (b n) -> p (k b) n", b=B)
            nc.scalar.activation(ke[:, :, 0:CD], src[:, :, hh * CD:(hh + 1) * CD], ACT.Copy).then_inc(ke_done, 1)
            nc.scalar.activation(ke[:, :, CD:EXT], src[:, :, hh * CD:hh * CD + EXT - CD], ACT.Copy).then_inc(ke_done, 1)

        def cut_t(q, hh):
            n = CHD * q + hh
            act.wait_ge(td_done, n + 1)
            act.wait_ge(unit_done, START + KT * n)
            nc.scalar.activation(t_hi[:], t_raw[:], ACT.Copy).then_inc(thi_done, 1)

        def cut_kv(q, u):
            v = CHD * KT * q + u
            act.wait_ge(kvraw_done, START + 2 * (v + 1))
            act.wait_ge(unit_done, START + v - u % KT)
            nc.scalar.activation(kv_hi[:, u % KT], kv_raw[:, u % 2], ACT.Copy).then_inc(kvhi_done, 1)

        def unit(q, u):
            if u % KT == 2 and u // KT < CHD - 1:
                keys(q, u // KT + 1)
            if u + 1 < CHD * KT:
                if (u + 1) % KT == 0:
                    cut_t(q, (u + 1) // KT)
                cut_kv(q, u + 1)

        def norm_nat(q, a):
            act.wait_ge(pshift_done, 2 * q + a + 1)
            act.wait_ge(xnT_filled, START + 2 * q)
            for j in range(2):
                nc.scalar.activation(xnat[:, 2 * a + j], ps_m[:, j], ACT.Identity, bias=pshift[:, j:j + 1],
                                     scale=prstd[:, j:j + 1]).then_inc(xnat_done, 1)

        def cut_xn(q, a):
            act.wait_ge(xnT_filled, START + 2 * q + a + 1)
            nc.scalar.activation(xn_hi[:, 2 * a:2 * a + 2], ps_m[:], ACT.Copy).then_inc(xnhi_done, 1)

        def cut_wT(g):
            act.wait_ge(wT_filled, g + 1)
            nc.scalar.activation(wT_hi[:], ps_m[0:8, 0], ACT.Copy).then_inc(wThi_done, 1)

        def read_wb(g, a):
            act.wait_ge(wb_filled, 3 * g + a + 1)
            act.wait_ge(sgw_done, START + RSTEPS * g)
            nc.scalar.activation(wb[:, 2 * a:2 * a + 2], ps_m[:], ACT.Copy).then_inc(wb_done, 1)

        def copy_x3(g):
            act.wait_ge(x3_done, START + g + 1)
            act.wait_ge(y_out, START + 16 * g)
            for k in range(KT):
                nc.scalar.activation(y[:, k], x3T[:, k], ACT.Identity, bias=gb[:, k:k + 1]).then_inc(y_copied, 1)

        for s in (silu_done, xq_done, x2T_done, ke_done, qe_done, xnat_done, wb_done, y_copied):
            act.sem_inc(s, START)
        act.wait_ge(const_in, 16 * 6)
        nc.scalar.activation(bd_hi[:], bd_raw, ACT.Copy).then_inc(setup_hi, 1)
        nc.scalar.activation(wr_hi[:], wr_raw, ACT.Copy).then_inc(setup_hi, 1)
        nc.scalar.activation(sel[:], sel_raw, ACT.Copy).then_inc(setup_hi, 1)
        act.wait_ge(gb_done, 1)
        norm_x(0)
        read_x2T(0, 0)
        read_x2T(0, 1)
        read_q(0, 0)
        read_q(0, 1)
        cut_gu(0, 0)
        keys(0, 0)
        cut_t(0, 0)
        cut_kv(0, 0)
        for u in range(CHD * KT):
            unit(0, u)
        norm_nat(0, 0)
        norm_nat(0, 1)
        cut_xn(0, 0)
        cut_xn(0, 1)

        def round_(g, q):
            for s in range(STEPS):
                units = UNITS.get(s, []) if q is not None else []
                if q is not None or s < STEPS - 1:
                    cut_gu(g, s + 1)
                cut_dn(g, s)
                silu(g, s)
                if s == 0:
                    cut_wT(g)
                    read_wb(g, 0)
                    if q is not None:
                        read_x2T(q, 0)
                if s == 1:
                    read_wb(g, 1)
                    if q is not None:
                        norm_x(q)
                if q is not None and s == 2:
                    read_q(q, 0)
                    read_q(q, 1)
                    cut_kv(q, 0)
                if units and s > FIRST_UNIT_STEP:
                    unit(q, units[0])
                if q is not None and s == STEPS - 1:
                    cut_xn(q, 0)
                cut_hd(g, s)
                if units and s == FIRST_UNIT_STEP:
                    unit(q, units[0])
                if len(units) > 1:
                    unit(q, units[1])
                if q is not None and s == 0:
                    read_x2T(q, 1)
                if s == 1:
                    read_wb(g, 2)
                    if q is not None:
                        keys(q, 0)
                        cut_t(q, 0)
                    copy_x3(g)
                if q is not None and s in (13, 14):
                    norm_nat(q, s - 13)
                if q is not None and s == STEPS - 1:
                    cut_xn(q, 1)

        with act.Fori(0, NCH - 1) as g:
            round_(g, g + 1)
        round_(NCH - 1, None)

    @block.vector
    def _(dve):
        vecs = keep["vecs"]

        def gated(g, s):
            if not routed(s):
                return
            n = STEPS * g + s
            dve.wait_ge(gu_done, START + n + 1)
            dve.wait_ge(sgw_done, START + RSTEPS * g + s + 1)
            dve.wait_ge(hdlo_done, START + n)
            nc.vector.scalar_tensor_tensor(out=hd[:], in0=ps_u[:], scalar=vecs[:, V_BU + s:V_BU + s + 1], in1=sgw[:], op0=ALU.add,
                                           op1=ALU.mult).then_inc(stt_done, 1)

        def cut_hd(g, s):
            dve.wait_ge(hdhi_done, STEPS * g + s + 1)
            nc.vector.tensor_tensor(hd_lo[:, s % 2], hd[:], f32(hd_hi[:, s % 2]), ALU.subtract).then_inc(hdlo_done, 1)

        def norm_stats(q):
            dve.wait_ge(x_in, 16 * TJ * (q + 1))
            for j in range(TJ):
                nc.vector.bn_stats(stats[:, j], x[:, j]).then_inc(stats_done, 1)
            dve.wait_ge(stats_done, 4 * (q + 1))
            variance(nc, dve, stats, mom, ve[:], LN_EPS, mom_done, 6 * q)

        def norm_shift(q):
            dve.wait_ge(rstd_done, q + 1)
            nc.vector.scalar_tensor_tensor(out=shift[:], in0=mom[:, 0], scalar=-0.5, in1=rstd[:], op0=ALU.mult,
                                           op1=ALU.mult).then_inc(shift_done, 1)

        def add_skip(q, hh):
            n = CHD * q + hh
            dve.wait_ge(t_in, 16 * (n + 1))
            nc.vector.scalar_tensor_tensor(out=t_raw[:, 0:P], in0=keep["ident"][:], scalar=skip[:, bass.ds(n, 1)], in1=t_raw[:, 0:P],
                                           op0=ALU.mult, op1=ALU.add).then_inc(td_done, 1)

        def cut_t(q, hh):
            dve.wait_ge(thi_done, CHD * q + hh + 1)
            nc.vector.tensor_tensor(t_lo[:], t_raw[:], f32(t_hi[:]), ALU.subtract).then_inc(tlo_done, 1)

        def cut_kv(q, u):
            dve.wait_ge(kvhi_done, CHD * KT * q + u + 1)
            nc.vector.tensor_tensor(kv_lo[:, u % KT], kv_raw[:, u % 2], f32(kv_hi[:, u % KT]), ALU.subtract).then_inc(kvlo_done, 1)

        def unit(q, u):
            hh, lb = u // KT, u % KT
            v = CHD * KT * q + u
            if u + 1 < CHD * KT:
                if (u + 1) % KT == 0:
                    add_skip(q, hh + 1)
                    cut_t(q, hh + 1)
                cut_kv(q, u + 1)
            if u == 0:
                dve.wait_ge(qe_done, START + 4 * (q + 1))
                dve.wait_ge(y_copied, START + 4 * q)
            dve.wait_ge(red_done, START + v)
            dve.wait_ge(unit_done, START + v + 1)
            qo = (lb * B * CHD + hh) * EXT
            qv = lambda off, *dims: view(qe, qo + off, (CHD * EXT, B), *dims)
            yv = lambda off, *dims: bass.AP(ps_m[:].tensor, ps_m[:].offset + off, [list(ps_m[:].ap[0]), [64, B]] + [list(d) for d in dims])
            zv = lambda off, *dims: view(zp, off, (ZW, B), *dims)
            nc.vector.tensor_tensor(zv(68, (21, 4), (1, 8)), yv(0, (8, 4), (1, 8)), qv(0, (1, 4), (1, 8)), ALU.mult).then_inc(prod_done, 1)
            nc.vector.tensor_tensor(zv(152, (4, 2), (1, 4)), yv(32, (0, 2), (1, 4)), qv(4, (4, 2), (1, 4)), ALU.mult).then_inc(prod_done, 1)
            nc.vector.tensor_tensor(zv(2 * ZROW + 8, (-ZROW, 3), (1, 8)), yv(8, (8, 3), (1, 8)), qv(0, (0, 3), (1, 8)),
                                    ALU.mult).then_inc(prod_done, 1)
            nc.vector.tensor_tensor(zv(2 * ZROW + 5, (-ZROW, 3), (1, 3)), yv(8 + 5, (8, 3), (1, 3)), qv(5, (0, 3), (1, 3)),
                                    ALU.mult).then_inc(prod_done, 1)
            dve.wait_ge(prod_done, START + 4 * (v + 1))
            nc.vector.tensor_reduce(x3T[:, lb].rearrange("p (b n) -> p b n", b=B)[:, :, hh * CD:(hh + 1) * CD],
                                    zv(5, (1, 8), (21, 8)), AX.X, ALU.add).then_inc(red_done, 1)

        def add_x2(q):
            dve.wait_ge(red_done, START + CHD * KT * (q + 1))
            dve.wait_ge(x2T_done, START + 2 * (q + 1))
            nc.vector.scalar_tensor_tensor(out=x3T[:], in0=x3T[:], scalar=keep["gains"][:, 1:2], in1=x2T[:], op0=ALU.mult,
                                           op1=ALU.add).then_inc(x3_done, 1)

        def nat_stats(q, a):
            dve.wait_ge(nat_filled, 2 * q + a + 1)
            for j in range(2):
                nc.vector.bn_stats(pstats[:, j], ps_m[:, j]).then_inc(pstats_done, 1)
            dve.wait_ge(pstats_done, 4 * q + 2 * a + 2)
            variance(nc, dve, pstats, pmom, pve[:], LN_EPS, pmom_done, 12 * q + 6 * a)
            dve.wait_ge(prstd_done, 2 * q + a + 1)
            dve.wait_ge(xnat_done, START + 4 * q + 2 * a)
            nc.vector.scalar_tensor_tensor(out=pshift[:], in0=pmom[:, 0], scalar=-0.5, in1=prstd[:], op0=ALU.mult,
                                           op1=ALU.mult).then_inc(pshift_done, 1)

        def cut_xn(q, a):
            dve.wait_ge(xnhi_done, 2 * q + a + 1)
            nc.vector.tensor_tensor(xn_lo[:, 2 * a:2 * a + 2], ps_m[:], f32(xn_hi[:, 2 * a:2 * a + 2]), ALU.subtract).then_inc(xn_done, 1)

        def route(q):
            r0 = RT * q
            n8 = lambda t: t[:].rearrange("p (j i e) -> p j i e", i=8, e=8)
            other, own = view(lg, 0, (8, TJ), (0, 8), (1, 8)), view(lg, 0, (8, TJ), (1, 8), (0, 8))
            row = lambda t: view(t, 0, (1, TJ), (0, 8))
            dve.wait_ge(lg_filled, q + 1)
            nc.vector.tensor_tensor(lg[:], ps_m[:, 0, 0:TJ * 8].rearrange("p (j e) -> p j e", e=8), view(vecs, V_BGATE, (0, TJ), (1, 8)),
                                    ALU.add).then_inc(lg_done, 1)
            dve.wait_ge(lg_done, START + q + 1)
            nc.vector.tensor_tensor(n8(ge), other, own, ALU.is_ge).then_inc(rt, 1)
            nc.vector.tensor_tensor(n8(gt), other, own, ALU.is_gt).then_inc(rt, 1)
            nc.vector.tensor_reduce(lmax[:], lg[:], AX.X, ALU.max).then_inc(rt, 1)
            dve.wait_ge(rt, r0 + 3)
            nc.vector.tensor_tensor(ge[:], ge[:], below[:], ALU.mult).then_inc(rt, 1)
            nc.vector.tensor_tensor(gt[:], gt[:], above[:], ALU.mult).then_inc(rt, 1)
            nc.vector.tensor_tensor(lx[:], lg[:], row(lmax), ALU.subtract).then_inc(rt, 4)
            dve.wait_ge(rt, r0 + 9)
            nc.vector.tensor_tensor(ge[:], ge[:], gt[:], ALU.add).then_inc(rt, 1)
            dve.wait_ge(rt, r0 + 10)
            nc.vector.tensor_reduce(rank[:], n8(ge), AX.X, ALU.add).then_inc(rt, 1)
            dve.wait_ge(rt, r0 + 11)
            nc.vector.tensor_scalar(keepw[:], rank[:], float(NE) - 0.5, None, ALU.is_lt).then_inc(rt, 1)
            dve.wait_ge(rt, r0 + 12)
            dve.wait_ge(exp_done, q + 1)
            nc.vector.tensor_tensor(ew[:], ew[:], keepw[:], ALU.mult).then_inc(rt, 1)
            dve.wait_ge(rt, r0 + 13)
            nc.vector.tensor_reduce(wsum[:], ew[:], AX.X, ALU.add).then_inc(rt, 1)
            dve.wait_ge(rt, r0 + 14)
            nc.vector.reciprocal(wrec[:], wsum[:]).then_inc(rt, 1)
            dve.wait_ge(rt, r0 + 15)
            nc.vector.tensor_tensor(w[:], ew[:], row(wrec), ALU.mult).then_inc(w_done, 1)

        def cut_wT(g):
            dve.wait_ge(wThi_done, g + 1)
            nc.vector.tensor_tensor(wT_lo[:], ps_m[0:8, 0], f32(wT_hi[:]), ALU.subtract).then_inc(wT_done, 1)

        def finish(g):
            dve.wait_ge(down_done, START + STEPS * (g + 1))
            dve.wait_ge(y_copied, START + 4 * (g + 1))
            for k in range(KT):
                nc.vector.scalar_tensor_tensor(out=y[:, k], in0=ps_out[:, k], scalar=keep["gains"][:, 3:4], in1=y[:, k], op0=ALU.mult,
                                               op1=ALU.add).then_inc(y_done, 1)

        for s in (hdlo_done, stt_done, kvlo_done, tlo_done, prod_done, red_done, x3_done, xn_done, lg_done, wT_done, y_done):
            dve.sem_inc(s, START)
        dve.wait_ge(const_in, 16 * 6)
        nc.vector.tensor_scalar(gb[:], vecs[:, V_BSD:V_BSD + KT], keep["gains"][:, 3:4], None, ALU.mult).then_inc(gb_done, 1)
        dve.wait_ge(setup_hi, 2)
        nc.vector.tensor_tensor(bd_lo[:], bd_raw, f32(bd_hi[:]), ALU.subtract).then_inc(setup_lo, 1)
        nc.vector.tensor_tensor(wr_lo[:], wr_raw, f32(wr_hi[:]), ALU.subtract).then_inc(setup_lo, 1)
        norm_stats(0)
        norm_shift(0)
        add_skip(0, 0)
        cut_t(0, 0)
        cut_kv(0, 0)
        for u in range(CHD * KT):
            unit(0, u)
        add_x2(0)
        nat_stats(0, 0)
        nat_stats(0, 1)
        cut_xn(0, 0)
        cut_xn(0, 1)
        dve.wait_ge(setup_lo, 2)
        route(0)

        def round_(g, q):
            for s in range(STEPS):
                units = UNITS.get(s, []) if q is not None else []
                if q is not None and s == 13:
                    add_x2(q)
                if s == 0:
                    cut_wT(g)
                    if q is not None:
                        norm_stats(q)
                gated(g, s)
                if q is not None and s == 0:
                    norm_shift(q)
                if q is not None and s == 2:
                    cut_kv(q, 0)
                if units and s > FIRST_UNIT_STEP:
                    unit(q, units[0])
                if q is not None and s == STEPS - 1:
                    cut_xn(q, 0)
                cut_hd(g, s)
                if q is not None and s == 1:
                    add_skip(q, 0)
                    cut_t(q, 0)
                if units and s == FIRST_UNIT_STEP:
                    unit(q, units[0])
                if len(units) > 1:
                    unit(q, units[1])
                if q is not None and s in (13, 14):
                    nat_stats(q, s - 13)
                if q is not None and s == STEPS - 1:
                    cut_xn(q, 1)
            finish(g)
            if q is not None:
                route(q)

        with dve.Fori(0, NCH - 1) as g:
            round_(g, g + 1)
        round_(NCH - 1, None)

    @block.tensor
    def _(pe):
        ident = keep["ident"]

        def gate(g, s):
            pe.wait_ge(gulo_done, START + STEPS * g + s + 1)
            if s == 0:
                pe.wait_ge(xn_done, START + 2 * (g + 1))
            if routed(s):
                pe.wait_ge(silu_done, START + STEPS * g + s)
                for k in range(KT):
                    last = products(nc, ps_g[:], gu_hi[:, s % 2, 0, k], gu_lo[:, s % 2, 0, k], xn_hi[:, k], xn_lo[:, k], k == 0, k == KT - 1)
                last.then_inc(gate_done, 1)

        def up(g, s):
            if s > RSTEPS:
                pe.wait_ge(silu_done, START + STEPS * g + s)
            else:
                pe.wait_ge(stt_done, START + RSTEPS * g + s)
            if s == 0:
                pe.wait_ge(silu_done, START + STEPS * g)
            for k in range(KT):
                last = products(nc, ps_u[:], gu_hi[:, s % 2, 1, k], gu_lo[:, s % 2, 1, k], xn_hi[:, k], xn_lo[:, k], k == 0, k == KT - 1)
            last.then_inc(gu_done, 1)

        def bias(g):
            pe.wait_ge(y_done, START + 4 * g)
            pe.wait_ge(wT_done, START + g + 1)
            for k in range(KT):
                col = slice(k * P, (k + 1) * P)
                products(nc, ps_out[:, k], bd_hi[:, col], bd_lo[:, col], wT_hi[:], wT_lo[:], True, False, skip=True)

        def down(g, s):
            n = STEPS * g + s
            pe.wait_ge(hdlo_done, START + n + 1)
            pe.wait_ge(dnlo_done, START + n + 1)
            for k in range(KT):
                col = slice(k * P, (k + 1) * P)
                last = products(nc, ps_out[:, k], dn_hi[:, s % 2, col], dn_lo[:, s % 2, col], hd_hi[:, s % 2], hd_lo[:, s % 2], False,
                                s == STEPS - 1, skip=True)
            last.then_inc(down_done, 1)

        def turn_x2(q, a, after):
            pe.wait_ge(x_in, 16 * TJ * (q + 1))
            pe.wait_ge(*after)
            for kk in range(2):
                for j in range(TJ):
                    k = 2 * a + kk
                    last = nc.tensor.transpose(ps_m[:, kk, j * P:(j + 1) * P], x[:, j, k * P:(k + 1) * P], ident[:])
            last.then_inc(x2T_filled, 1)

        def turn_q(q, a, after):
            pe.wait_ge(xq_done, START + 4 * (q + 1))
            pe.wait_ge(*after)
            for kk in range(2):
                for j in range(TJ):
                    k = 2 * a + kk
                    last = nc.tensor.transpose(ps_m[:, kk, j * P:(j + 1) * P], xq[:, j, k * P:(k + 1) * P], ident[:])
            last.then_inc(q_filled, 1)

        def unit(q, u, after):
            hh, lb = u // KT, u % KT
            v = CHD * KT * q + u
            if u > 0:
                after = (prod_done, START + 4 * v)
            pe.wait_ge(kvlo_done, START + v + 1)
            pe.wait_ge(tlo_done, START + CHD * q + hh + 1)
            pe.wait_ge(*after)
            for half in range(2):
                bs = slice(half * B // 2, (half + 1) * B // 2)
                for m in range(lb + 1):
                    t = slice((lb - m) * P, (lb - m + 1) * P)
                    last = products(nc, m_units[:, bs, 0:PAIRS], t_hi[:, t], t_lo[:, t], kv_hi[:, m, bs], kv_lo[:, m, bs], m == 0, m == lb)
            last.then_inc(unit_done, 1)

        def turn_x3(q, a, after):
            pe.wait_ge(x3_done, START + q + 1)
            pe.wait_ge(*after)
            for jj in range(2):
                for k in range(KT):
                    j = 2 * a + jj
                    last = nc.tensor.transpose(ps_m[:, jj, k * P:(k + 1) * P], x3T[:, k, j * P:(j + 1) * P], ident[:])
            last.then_inc(nat_filled, 1)

        def turn_xn(q, a, after):
            pe.wait_ge(xnat_done, START + 4 * (q + 1))
            pe.wait_ge(*after)
            for kk in range(2):
                for j in range(TJ):
                    k = 2 * a + kk
                    last = nc.tensor.transpose(ps_m[:, kk, j * P:(j + 1) * P], xnat[:, j, k * P:(k + 1) * P], ident[:])
            last.then_inc(xnT_filled, 1)

        def logits(q):
            pe.wait_ge(xn_done, START + 2 * (q + 1))
            for j in range(TJ):
                tok = slice(j * P, (j + 1) * P)
                for k in range(KT):
                    last = products(nc, ps_m[:, 0, 8 * j:8 * j + 8], xn_hi[:, k, tok], xn_lo[:, k, tok], wr_hi[:, k], wr_lo[:, k],
                                    k == 0, k == KT - 1)
            last.then_inc(lg_filled, 1)

        def turn_w(g):
            pe.wait_ge(w_done, g + 1)
            for j in range(TJ):
                last = nc.tensor.transpose(ps_m[0:8, 0, j * P:(j + 1) * P], w[:, j], ident[:])
            last.then_inc(wT_filled, 1)

        def spread(g, a, after):
            pe.wait_ge(wT_done, START + g + 1)
            pe.wait_ge(*after)
            for e in range(2):
                nc.tensor.matmul(ps_m[:, e], sel[:, (2 * a + e) * P:(2 * a + e + 1) * P], wT_hi[:], start=True, stop=False)
                last = nc.tensor.matmul(ps_m[:, e], sel[:, (2 * a + e) * P:(2 * a + e + 1) * P], wT_lo[:], start=False, stop=True)
            last.then_inc(wb_filled, 1)

        for s in (gu_done, down_done, unit_done, q_filled, xnT_filled):
            pe.sem_inc(s, START)
        pe.wait_ge(setup_lo, 2)
        pe.wait_ge(setup_hi, 3)
        turn_x2(0, 0, (x2T_done, START))
        turn_x2(0, 1, (x2T_done, START + 1))
        turn_q(0, 0, (x2T_done, START + 2))
        turn_q(0, 1, (qe_done, START + 2))
        for u in range(CHD * KT):
            unit(0, u, (qe_done, START + 4))
        turn_x3(0, 0, (prod_done, START + 4 * CHD * KT))
        turn_x3(0, 1, (xnat_done, START + 2))
        turn_xn(0, 0, (xnat_done, START + 4))
        turn_xn(0, 1, (xn_done, START + 1))
        logits(0)

        def round_(g, q):
            for s in range(STEPS):
                units = UNITS.get(s, []) if q is not None else []
                gate(g, s)
                if s == 1:
                    spread(g, 0, (wT_done, START + g + 1))
                    if q is not None:
                        turn_x2(q, 0, (wb_done, START + 3 * g + 1))
                    bias(g)
                    if q is not None:
                        turn_x2(q, 1, (x2T_done, START + 2 * q + 1))
                if q is not None and s == 2:
                    turn_q(q, 0, (wb_done, START + 3 * g + 3))
                up(g, s)
                if s == 0:
                    turn_w(g)
                if s == 1:
                    spread(g, 1, (x2T_done, START + 2 * q + 2) if q is not None else (wb_done, START + 3 * g + 1))
                if q is not None and s == 2:
                    turn_q(q, 1, (qe_done, START + 4 * q + 2))
                if units and s > FIRST_UNIT_STEP:
                    unit(q, units[0], None)
                if q is not None and s == STEPS - 1:
                    turn_xn(q, 0, (xnat_done, START + 4 * q + 4))
                if s > 0:
                    down(g, s - 1)
                if s == 1:
                    spread(g, 2, (wb_done, START + 3 * g + 2))
                if units and s == FIRST_UNIT_STEP:
                    unit(q, units[0], (qe_done, START + 4 * q + 4))
                if len(units) > 1:
                    unit(q, units[1], None)
                if q is not None and s == 13:
                    turn_x3(q, 0, (prod_done, START + 4 * CHD * KT * (q + 1)))
                if q is not None and s == 14:
                    turn_x3(q, 1, (xnat_done, START + 4 * q + 2))
                if q is not None and s == STEPS - 1:
                    turn_xn(q, 1, (xn_done, START + 2 * q + 1))
            down(g, STEPS - 1)
            if q is not None:
                logits(q)

        with pe.Fori(0, NCH - 1) as g:
            round_(g, g + 1)
        round_(NCH - 1, None)

    st.close()


def expert_constants(np):
    own, other = np.meshgrid(np.arange(8), np.arange(8), indexing="ij")
    rep = lambda m: np.broadcast_to(m.astype(np.float32).reshape(1, 1, 64), (P, 4, 64)).reshape(P, 256)
    sel = np.zeros((8, NE * P), np.float32)
    for e in range(NE):
        sel[e, e * P:(e + 1) * P] = 1.0
    return {"sel": sel, "below": rep(other < own), "above": rep(other > own)}


def build(nc, dram):
    with ExitStack() as ctx:
        sb = lambda n, s, d=F32: ctx.enter_context(nc.sbuf_tensor(n, s, d))
        keep = {"vecs": sb("vecs", [P, V_COLS]), "gains": sb("gains", [P, 4]), "ident": sb("ident", [P, P]),
                "identb": sb("identb", [P, P], BF16), "wmean": sb("wmean", [P, 2])}
        attn = ctx.enter_context(ExitStack())
        at = lambda n, s, d=F32: attn.enter_context(nc.sbuf_tensor(n, s, d))
        keep.update({"at_hi": at("at_hi", [P, HEADS, CH], F32R), "at_lo": at("at_lo", [P, HEADS, CH], F32R),
                     "wo_hi": at("wo_hi", [P, KT, D], F32R), "wo_lo": at("wo_lo", [P, KT, D], F32R),
                     "w1q": at("w1q", [P, KT, HID], BF16), "w2q": at("w2q", [P, HT, D], BF16), "gam": at("gam", [P, D])})
        sc = ctx.enter_context(ExitStack())
        at = lambda n, s, d=F32: sc.enter_context(nc.sbuf_tensor(n, s, d))
        keep.update({"wg_hi": at("wg_hi", [P, KT, D], F32R), "wg_lo": at("wg_lo", [P, KT, D], F32R),
                     "wh_hi": at("wh_hi", [P, HEADS, P], F32R), "wh_lo": at("wh_lo", [P, HEADS, P], F32R),
                     "g_hi": at("g_hi", [P, HEADS, P], F32R), "g_lo": at("g_lo", [P, HEADS, P], F32R),
                     "mask": at("mask", [P, HEADS, CH])})
        setup_block(nc, ctx, dram, keep)
        scores_block(nc, ctx, dram, keep)
        sc.close()
        attn_block(nc, ctx, dram, keep)
        attn.close()
        experts_block(nc, ctx, dram, keep)


def decay_mask(np):
    gam = 1.0 - 2.0 ** (-5.0 - np.arange(HEADS))
    expo = (np.arange(S)[None, :] - np.arange(S)[:, None]).astype(np.float64)
    d = np.where(expo[None] <= 0, gam[:, None, None] ** np.minimum(expo[None], 0), 0.0)
    d = d / np.sqrt(d.sum(-1))[:, None, :] / np.sqrt(P)
    return np.ascontiguousarray(d.reshape(HEADS, S, 2, P).transpose(3, 0, 2, 1).reshape(P, HEADS, CH)).astype(np.float32)


def kernel(**inputs):
    import numpy as np
    import concourse.bacc as bacc
    from concourse import mybir as mb
    from concourse.bass_utils import run_bass_kernel_spmd

    a = {k: np.asarray(v) for k, v in inputs.items()}
    lay = np.ascontiguousarray
    ctx_t = a["ctx_2048"].reshape(B * S, D).T
    gains = [a["g_xattn"][0:1], a["g_xattn"][1:2], a["g_ffn"][0:1], a["g_ffn"][1:2], ]
    cols = lambda v: v.reshape(-1, P).T
    rows = lambda v: np.broadcast_to(v.reshape(1, -1), (P, v.size))
    vecs = np.concatenate([rows(g) for g in gains] + [
        cols(a["L0_xattn_gn_gamma"]), cols(a["L0_xattn_gn_beta"]), cols(a["L1_ffn_bgate"]), cols(a["L1_ffn_bup"]),
        cols(a["L1_ffn_bs_up"]), cols(a["L1_ffn_bs_down"]), rows(a["L1_ffn_bg"])], axis=1)
    ctx_g = a["ctx_2048"].reshape(B, NCH, S // NCH, D).transpose(1, 3, 0, 2).reshape(NCH, D, CH)
    padded = np.concatenate([np.zeros((S // CD, P), np.float32), a["L1_xattn_ssm_kernel"]], axis=1)
    toep = np.stack([padded[:, P - m:P - m + D] for m in range(P)], axis=1)
    tiles = lambda w, n: w.reshape(KT, P, n, P).transpose(2, 1, 0, 3).reshape(n, P, D)
    of = lambda w: np.concatenate([tiles(w[e], EH // P) for e in range(NE)])
    mgu = np.stack([of(a["L1_ffn_Wgate"]), of(a["L1_ffn_Wup"])], axis=2).reshape(RSTEPS, P, 2 * D)
    md = np.concatenate([a["L1_ffn_Wdown"].reshape(RSTEPS, P, D), a["L1_ffn_Ws_down"].reshape(SH // P, P, D)])
    bdown = np.concatenate([a["L1_ffn_bdown"], np.zeros((2, D), np.float32)])
    arrays = {
        "x": a["x"].reshape(B * S, D), "ctxT": ctx_t, "ctxG": ctx_g, "toep": toep,
        "skipD": rows(a["L1_xattn_D"]),
        "wh": a["L0_xattn_Wh"], "whT": a["L0_xattn_Wh"].transpose(0, 2, 1), "wg": a["L0_xattn_wg_w"],
        "wo": a["L0_xattn_wo_w"], "w1T": a["L0_ffn_w1"].T, "w2T": a["L0_ffn_w2"].T, "vecs": vecs,
        "gam": rows(a["L0_ffn_gamma"]), "ident": np.eye(P, dtype=np.float32), "mask": decay_mask(np),
        "mgu": mgu, "msu": tiles(a["L1_ffn_Ws_up"], SH // P), "md": md,
        "wroute": a["L1_ffn_Wg"].reshape(KT, P, 8).transpose(1, 0, 2), "bdown": bdown, **expert_constants(np),
    }
    arrays = {"in_" + n: lay(v) for n, v in arrays.items()}
    nc = bacc.Bacc("TRN2", target_bir_lowering=False, num_devices=1)
    dram = {n[3:]: nc.dram_tensor(n, v.shape, mb.dt.from_np(v.dtype), kind="ExternalInput").ap() for n, v in arrays.items()}
    dram["gates"] = nc.dram_tensor("gates", (NCH, P, KT, CH), mb.dt.float32, kind="Internal").ap()
    dram["vals"] = nc.dram_tensor("vals", (NCH, P, TJ, D), mb.dt.float32, kind="Internal").ap()
    dram["x2"] = nc.dram_tensor("x2", (B * S, D), mb.dt.float32, kind="Internal").ap()
    dram["out"] = nc.dram_tensor("out", (NCH, D, CH), mb.dt.float32, kind="ExternalOutput").ap()
    build(nc, dram)
    got = run_bass_kernel_spmd(nc, [arrays], core_ids=[0]).results[0]["out"]
    return lay(got.reshape(NCH, D, B, S // NCH).transpose(2, 0, 3, 1).reshape(B, S, D))
```

```python
from contextlib import ExitStack

import concourse.bass as bass
from concourse import mybir

F32 = mybir.dt.float32
F32R = mybir.dt.float32r
BF16 = mybir.dt.bfloat16
ACT = mybir.ActivationFunctionType
ALU = mybir.AluOpType
AX = mybir.AxisListType

P = 128
B, S, D = 16, 256, 512
KT = D // P
HEADS = 4
CH = 512
NCH = B * S // CH
TJ = CH // P
HID = 2048
HT = HID // P
START = 1
ROUND = 1.5 * 2.0 ** 23
LN_EPS, GN_EPS, RMS_EPS = 1e-5, 1e-3, 1e-6
QMAX = 127.0
NE, EH = 6, 256
SH = 512
CD = 8
CHD = 4
PAIRS = 36
EXT = 12
STEPS = (NE * EH + SH) // P
RSTEPS = NE * EH // P
V_GAIN, V_GAMMA, V_BETA, V_BG, V_BU, V_BSU, V_BSD, V_BGATE = 0, 4, 8, 12, 24, 36, 40, 44
V_COLS = 52


def f32(ap):
    return ap.bitcast(F32)


def products(nc, out, w_hi, w_lo, x_hi, x_lo, first, last, skip=False):
    nc.tensor.matmul(out, w_hi, x_hi, start=first, stop=False, skip_group_check=skip)
    nc.tensor.matmul(out, w_hi, x_lo, start=False, stop=False, skip_group_check=skip)
    return nc.tensor.matmul(out, w_lo, x_hi, start=False, stop=last, skip_group_check=skip)


def variance(nc, dve, stats, mom, var, eps, step, done):
    nc.vector.tensor_tensor(mom[:, 0], stats[:, :, 1], stats[:, :, 4], ALU.add).then_inc(step, 1)
    nc.vector.tensor_tensor(mom[:, 1], stats[:, :, 1], stats[:, :, 4], ALU.subtract).then_inc(step, 1)
    nc.vector.tensor_tensor(mom[:, 2], stats[:, :, 2], stats[:, :, 5], ALU.add).then_inc(step, 1)
    dve.wait_ge(step, done + 3)
    nc.vector.scalar_tensor_tensor(out=mom[:, 3], in0=mom[:, 1], scalar=0.25, in1=mom[:, 1], op0=ALU.mult,
                                   op1=ALU.mult).then_inc(step, 1)
    nc.vector.tensor_scalar(mom[:, 4], mom[:, 2], 1.0 / D, eps, ALU.mult, ALU.add).then_inc(step, 1)
    dve.wait_ge(step, done + 5)
    nc.vector.tensor_tensor(var, mom[:, 3], mom[:, 4], ALU.add).then_inc(step, 1)


def setup_block(nc, ctx, dram, keep):
    st = ctx.enter_context(ExitStack())
    sb = lambda n, s, d=F32: st.enter_context(nc.sbuf_tensor(n, s, d))
    sem = lambda n: ctx.enter_context(nc.semaphore(n))
    raw_wg = sb("raw_wg", [P, KT, D])
    raw_wh = sb("raw_wh", [P, HEADS, P])
    raw_wht = sb("raw_wht", [P, HEADS, P])
    wht_hi, wht_lo = sb("wht_hi", [P, HEADS, P], F32R), sb("wht_lo", [P, HEADS, P], F32R)
    ps_g = st.enter_context(nc.psum_tensor("ps_g", [P, 512], F32))
    vecs_in, ident_in, wh_in, wht_in, wg_in, hi_done, lo_done, g_done, ghi_done = (
        sem(n) for n in ("vecs_in", "ident_in", "wh_in", "wht_in", "wg_in", "hi_done", "lo_done", "g_done", "ghi_done"))
    cuts = [(raw_wht, wht_hi, wht_lo, wht_in), (raw_wh, keep["wh_hi"], keep["wh_lo"], wh_in),
            (raw_wg, keep["wg_hi"], keep["wg_lo"], wg_in)]
    block = st.enter_context(nc.Block())

    @block.sync
    def _(sp):
        sp.dma_start(raw_wht[:], dram["whT"].rearrange("h e d -> e h d")).then_inc(wht_in, 16)
        sp.dma_start(raw_wh[:], dram["wh"].rearrange("h d e -> d h e")).then_inc(wh_in, 16)
        sp.dma_start(raw_wg[:], dram["wg"].rearrange("(k p) n -> p k n", p=P)).then_inc(wg_in, 16)

    @block.scalar
    def _(act):
        act.dma_start(keep["vecs"][:], dram["vecs"]).then_inc(vecs_in, 16)
        act.dma_start(keep["ident"][:], dram["ident"]).then_inc(ident_in, 16)
        act.wait_ge(vecs_in, 16)
        nc.scalar.activation(keep["gains"][:], keep["vecs"][:, V_GAIN:V_GAIN + 4], ACT.Tanh)
        for raw, hi, lo, arrived in cuts:
            act.wait_ge(arrived, 16)
            nc.scalar.activation(hi[:], raw[:], ACT.Copy).then_inc(hi_done, 1)
        act.wait_ge(g_done, 1)
        nc.scalar.activation(keep["g_hi"][:], ps_g[:].rearrange("p (h d) -> p h d", h=HEADS), ACT.Copy).then_inc(ghi_done, 1)

    @block.gpsimd
    def _(pool):
        pool.wait_ge(ident_in, 16)
        nc.gpsimd.tensor_copy(keep["identb"][:], keep["ident"][:])

    @block.vector
    def _(dve):
        for n, (raw, hi, lo, arrived) in enumerate(cuts):
            dve.wait_ge(hi_done, n + 1)
            nc.vector.tensor_tensor(lo[:], raw[:], f32(hi[:]), ALU.subtract).then_inc(lo_done, 1)
        dve.wait_ge(ghi_done, 1)
        nc.vector.tensor_tensor(keep["g_lo"][:], ps_g[:].rearrange("p (h d) -> p h d", h=HEADS), f32(keep["g_hi"][:]), ALU.subtract)

    @block.tensor
    def _(pe):
        pe.wait_ge(lo_done, 1)
        for h in range(HEADS):
            last = products(nc, ps_g[:, h * P:(h + 1) * P], wht_hi[:, h], wht_lo[:, h], wht_hi[:, h], wht_lo[:, h], True, True)
        last.then_inc(g_done, 1)

    st.close()


def scores_block(nc, ctx, dram, keep):
    st = ctx.enter_context(ExitStack())
    sb = lambda n, s, d=F32: st.enter_context(nc.sbuf_tensor(n, s, d))
    sem = lambda n: ctx.enter_context(nc.semaphore(n))
    x = keep["stage"]
    xn = sb("xn", [P, TJ, D])
    xnT_hi, xnT_lo = sb("xnT_hi", [P, KT, CH], F32R), sb("xnT_lo", [P, KT, CH], F32R)
    c = sb("c", [P, KT, CH])
    c_hi, c_lo = sb("c_hi", [P, KT, CH], F32R), sb("c_lo", [P, KT, CH], F32R)
    q_hi, q_lo = sb("q_hi", [P, HEADS, CH], F32R), sb("q_lo", [P, HEADS, CH], F32R)
    gate = sb("gate", [P, KT, CH])
    val = sb("val", [P, TJ, D])
    raw = [sb("raw_w1", [P, HID]), sb("raw_w2", [P, HID])]
    zeros = sb("zeros", [P, CH], F32R)
    ones = sb("ones_f32", [P, P])
    stats = sb("stats", [P, TJ, 6])
    mom = sb("mom", [P, 5, TJ])
    ve, rstd, shift, mhalf = (sb(n, [P, TJ]) for n in ("ve", "rstd", "shift", "mhalf"))
    wpart, wsum, wrec = (sb(n, [P, 2]) for n in ("wpart", "wsum", "wrec"))
    rnd, unrnd = sb("rnd", [P, 1]), sb("unrnd", [P, 1])
    acc = st.enter_context(nc.psum_tensor("acc", [P, HEADS, CH], F32))
    bank = [st.enter_context(nc.psum_tensor(f"bank{n}", [P, CH], F32)) for n in range(4)]
    GATE, QUERY, VALUE, TURN = 0, 4, 8, 12
    HALF = NCH // 2
    names = ("x_in c_in stats_done mom_done rstd_done shift_done xn_done chi_done clo_done filled xhi_done qhi_done xnT_done "
             "val_done gate_done q_done scores_done consts_done val_out gate_out mask_done abs_done ahi_done const_in "
             "w1_in w2_in wohi_done wolo_done part_done sum_done mean_done scale_done scaled_done clip_done tern_done v0_in")
    (x_in, c_in, stats_done, mom_done, rstd_done, shift_done, xn_done, chi_done, clo_done, filled, xhi_done, qhi_done, xnT_done,
     val_done, gate_done, q_done, scores_done, consts_done, val_out, gate_out, mask_done, abs_done, ahi_done, const_in,
     w1_in, w2_in, wohi_done, wolo_done, part_done, sum_done, mean_done, scale_done, scaled_done, clip_done, tern_done, v0_in) = (
         sem("s_" + n) for n in names.split())
    w_in = [w1_in, w2_in]
    x_v = dram["x"].rearrange("(i j p) d -> i p j d", j=TJ, p=P)
    c_v = dram["ctxT"].rearrange("(k p) (i n) -> i p k n", p=P, n=CH)
    w_v = [dram["w1T"].rearrange("(i p) n -> i p n", p=P), dram["w2T"].rearrange("(i k p) n -> i p k n", k=KT, p=P)]
    w_out = [keep["w1q"], keep["w2q"][:].rearrange("p (i k) n -> p i (k n)", k=KT)]

    def filling(i, use):
        return 4 + 16 * i + use + 1

    block = st.enter_context(nc.Block())

    @block.sync
    def _(sp):
        def load_x(n):
            sp.wait_ge(xn_done, START + 4 * n)
            sp.dma_start(x[:], x_v[n]).then_inc(x_in, 16)

        def load_c(n):
            sp.wait_ge(clo_done, START + n)
            sp.dma_start(c[:], c_v[n]).then_inc(c_in, 16)

        def load_w_sum(i):
            for n in range(2):
                sp.wait_ge(part_done, START + 2 * i)
                sp.dma_start(raw[n][:].rearrange("p (k n) -> p k n", k=KT) if n else raw[n][:], w_v[n][i]).then_inc(w_in[n], 16)

        def load_w_round(i):
            for n in range(2):
                sp.wait_ge(tern_done, START + 2 * i)
                sp.dma_start(raw[n][:].rearrange("p (k n) -> p k n", k=KT) if n else raw[n][:], w_v[n][i]).then_inc(w_in[n], 16)

        def round_(i, part, load_weights, more_c, more_x):
            load_weights(part)
            if more_c:
                load_c(i + 1)
            sp.wait_ge(gate_done, 4 * (i + 1))
            sp.dma_start(dram["gates"][i], gate[:]).then_inc(gate_out, 16)
            if more_x:
                load_x(i + 2)
            sp.wait_ge(val_done, START + 4 * (i + 1))
            sp.dma_start(dram["vals"][i], val[:]).then_inc(val_out, 16)

        sp.sem_inc(gate_out, START)
        sp.sem_inc(val_out, START)
        load_x(0)
        load_c(0)
        load_x(1)
        sp.dma_start(raw[0][:].rearrange("p (k n) -> p k n", k=KT), dram["wo"].rearrange("(k p) n -> p k n", p=P)).then_inc(w1_in, 16)
        sp.dma_start(keep["mask"][:], dram["mask"]).then_inc(const_in, 16)
        sp.dma_start(keep["gam"][:], dram["gam"]).then_inc(const_in, 16)
        sp.wait_ge(wolo_done, 1)
        with sp.Fori(0, HALF) as i:
            round_(i, i, load_w_sum, True, True)
        sp.wait_ge(part_done, START + 2 * HALF)
        with sp.Fori(0, HALF - 2) as i:
            round_(i + HALF, i, load_w_round, True, True)
        round_(NCH - 2, HALF - 2, load_w_round, True, False)
        round_(NCH - 1, HALF - 1, load_w_round, False, False)
        sp.wait_ge(gate_out, START + 16 * NCH)
        sp.wait_ge(val_out, START + 16 * NCH)
        sp.wait_ge(xn_done, START + 4 * NCH)
        sp.dma_start(keep["stage"][:], dram["vals"][0]).then_inc(v0_in, 16)
        sp.wait_ge(v0_in, 16)

    @block.gpsimd
    def _(pool):
        for t, value in ((mhalf[:], -0.5), (f32(zeros[:]), 0.0), (ones[:], 1.0), (wsum[:], 0.0), (rnd[:], ROUND), (unrnd[:], -ROUND)):
            nc.gpsimd.memset(t, value).then_inc(consts_done, 1)
        pool.wait_ge(consts_done, 1)
        with pool.Fori(0, NCH) as i:
            pool.wait_ge(mom_done, 6 * i + 6)
            nc.gpsimd.tensor_tensor(rstd[:], ve[:], mhalf[:], ALU.pow).then_inc(rstd_done, 1)

    @block.scalar
    def _(act):
        def norm(n):
            act.wait_ge(shift_done, n + 1)
            for j in range(TJ):
                nc.scalar.activation(xn[:, j], x[:, j], ACT.Identity, bias=shift[:, j:j + 1],
                                     scale=rstd[:, j:j + 1]).then_inc(xn_done, 1)

        def cut_c(i):
            act.wait_ge(c_in, 16 * (i + 1))
            act.wait_ge(scores_done, START + HEADS * i)
            nc.scalar.activation(c_hi[:], c[:], ACT.Copy).then_inc(chi_done, 1)

        def cut_x(n):
            for k in range(KT):
                act.wait_ge(filled, 16 * n + k + 1)
                nc.scalar.activation(xnT_hi[:, k], bank[k][:], ACT.Copy).then_inc(xhi_done, 1)

        def cut_q(i):
            for h in range(HEADS):
                act.wait_ge(filled, filling(i, QUERY + h))
                nc.scalar.activation(q_hi[:, h], bank[h][:], ACT.Copy).then_inc(qhi_done, 1)

        def scale_w(part):
            for n in range(2):
                act.wait_ge(w_in[n], 16 * (part + 1 + HALF + (n == 0)))
                nc.scalar.activation(raw[n][:], raw[n][:], ACT.Identity, bias=rnd[:], scale=wrec[:, n:n + 1]).then_inc(scaled_done, 1)

        def ternary(part):
            for n in range(2):
                act.wait_ge(clip_done, 2 * part + n + 1)
                nc.scalar.activation(w_out[n][:, part], raw[n][:], ACT.Identity, bias=unrnd[:]).then_inc(tern_done, 1)

        for s in (xn_done, tern_done):
            act.sem_inc(s, START)
        act.wait_ge(consts_done, 6)
        norm(0)
        cut_x(0)
        act.wait_ge(w1_in, 16)
        nc.scalar.activation(keep["wo_hi"][:].rearrange("p k n -> p (k n)"), raw[0][:], ACT.Copy).then_inc(wohi_done, 1)

        def round_(i, n, part):
            cut_c(i)
            if n is not None:
                norm(n)
            cut_q(i)
            if part is not None:
                scale_w(part)
            if n is not None:
                cut_x(n)
            if part is not None:
                ternary(part)

        with act.Fori(0, HALF) as i:
            round_(i, i + 1, None)
        act.wait_ge(scale_done, 2)
        with act.Fori(0, HALF - 1) as i:
            round_(i + HALF, i + HALF + 1, i)
        round_(NCH - 1, None, HALF - 1)
        act.wait_ge(const_in, 32)

    @block.vector
    def _(dve):
        def norm_stats(n):
            dve.wait_ge(x_in, 16 * (n + 1))
            for j in range(TJ):
                nc.vector.bn_stats(stats[:, j], x[:, j]).then_inc(stats_done, 1)
            dve.wait_ge(stats_done, 4 * (n + 1))
            variance(nc, dve, stats, mom, ve[:], LN_EPS, mom_done, 6 * n)

        def norm_shift(n):
            dve.wait_ge(rstd_done, n + 1)
            nc.vector.scalar_tensor_tensor(out=shift[:], in0=mom[:, 0], scalar=-0.5, in1=rstd[:], op0=ALU.mult,
                                           op1=ALU.mult).then_inc(shift_done, 1)

        def cut_c(i):
            dve.wait_ge(chi_done, i + 1)
            nc.vector.tensor_tensor(c_lo[:], c[:], f32(c_hi[:]), ALU.subtract).then_inc(clo_done, 1)

        def cut_x(n):
            for k in range(KT):
                dve.wait_ge(xhi_done, 4 * n + k + 1)
                nc.vector.tensor_tensor(xnT_lo[:, k], bank[k][:], f32(xnT_hi[:, k]), ALU.subtract).then_inc(xnT_done, 1)

        def read_gate(i):
            dve.wait_ge(gate_out, START + 16 * i)
            for m in range(KT):
                dve.wait_ge(filled, filling(i, GATE + m))
                nc.vector.tensor_scalar(gate[:, m], bank[m][:], 0.0, None, ALU.max).then_inc(gate_done, 1)

        def cut_q(i):
            for h in range(HEADS):
                dve.wait_ge(qhi_done, 4 * i + h + 1)
                nc.vector.tensor_tensor(q_lo[:, h], bank[h][:], f32(q_hi[:, h]), ALU.subtract).then_inc(q_done, 1)

        def read_values(i):
            dve.wait_ge(val_out, START + 16 * i)
            for j in range(TJ):
                dve.wait_ge(filled, filling(i, VALUE + j))
                nc.vector.tensor_copy(val[:, j], bank[j][:]).then_inc(val_done, 1)

        def sum_w(part):
            for n in range(2):
                dve.wait_ge(w_in[n], 16 * (part + 1 + (n == 0)))
                nc.vector.tensor_reduce(wpart[:, n:n + 1], raw[n][:], AX.X, ALU.add, apply_absolute_value=True).then_inc(part_done, 1)
            dve.wait_ge(part_done, START + 2 * part + 2)
            dve.wait_ge(sum_done, START + part)
            nc.vector.tensor_tensor(wsum[:], wsum[:], wpart[:], ALU.add).then_inc(sum_done, 1)

        def clip_w(part):
            for n in range(2):
                dve.wait_ge(scaled_done, 2 * part + n + 1)
                nc.vector.tensor_scalar(raw[n][:], raw[n][:], ROUND + 1.0, ROUND - 1.0, ALU.min, ALU.max).then_inc(clip_done, 1)

        for s in (clo_done, q_done, val_done, part_done, sum_done):
            dve.sem_inc(s, START)
        dve.wait_ge(consts_done, 6)
        norm_stats(0)
        norm_shift(0)
        cut_x(0)
        dve.wait_ge(wohi_done, 1)
        nc.vector.tensor_tensor(keep["wo_lo"][:].rearrange("p k n -> p (k n)"), raw[0][:],
                                f32(keep["wo_hi"][:]).rearrange("p k n -> p (k n)"), ALU.subtract).then_inc(wolo_done, 1)

        def round_(i, n, weights, part):
            if n is not None:
                norm_stats(n)
            cut_c(i)
            if n is not None:
                norm_shift(n)
            read_gate(i)
            cut_q(i)
            read_values(i)
            if n is not None:
                cut_x(n)
            weights(part)

        with dve.Fori(0, HALF) as i:
            round_(i, i + 1, sum_w, i)
        dve.wait_ge(mean_done, 1)
        nc.vector.tensor_scalar(keep["wmean"][:], bank[0][:, 0:2], 1.0 / (D * HID), 1e-5, ALU.mult, ALU.max).then_inc(scale_done, 1)
        dve.wait_ge(scale_done, 1)
        nc.vector.reciprocal(wrec[:], keep["wmean"][:]).then_inc(scale_done, 1)
        with dve.Fori(0, HALF - 1) as i:
            round_(i + HALF, i + HALF + 1, clip_w, i)
        round_(NCH - 1, None, clip_w, HALF - 1)
        dve.wait_ge(gate_out, START + 16 * NCH)
        dve.wait_ge(val_out, START + 16 * NCH)
        dve.wait_ge(const_in, 32)
        for h in range(HEADS):
            dve.wait_ge(scores_done, START + HEADS * (NCH - 1) + h + 1)
            nc.vector.tensor_tensor(gate[:, h], acc[:, h], keep["mask"][:, h], ALU.mult).then_inc(mask_done, 1)
            dve.wait_ge(mask_done, h + 1)
            nc.vector.scalar_tensor_tensor(out=val[:, h], in0=gate[:, h], scalar=-1.0, in1=gate[:, h], op0=ALU.mult,
                                           op1=ALU.max).then_inc(abs_done, 1)
            dve.wait_ge(abs_done, h + 1)
            nc.vector.tensor_scalar(keep["at_hi"][:, h], val[:, h], 1.0, None, ALU.max).then_inc(ahi_done, 1)
            dve.wait_ge(ahi_done, h + 1)
            nc.vector.scalar_tensor_tensor(out=keep["at_lo"][:, h], in0=val[:, h], scalar=1.0, in1=f32(keep["at_hi"][:, h]),
                                           op0=ALU.max, op1=ALU.subtract)

    @block.tensor
    def _(pe):
        def turn(n, first=False):
            pe.wait_ge(xn_done, START + 4 * (n + 1))
            for k in range(KT):
                if not first:
                    pe.wait_ge(val_done, START + 4 * (n - 1) + k + 1)
                for j in range(TJ):
                    last = nc.tensor.transpose(bank[k][:, j * P:(j + 1) * P], xn[:, j, k * P:(k + 1) * P], keep["ident"][:])
                last.then_inc(filled, 1)

        pe.sem_inc(scores_done, START)
        pe.wait_ge(consts_done, 6)
        for h in range(HEADS):
            nc.tensor.matmul(acc[:, h], zeros[:, 0:P], zeros[:], start=True, stop=False, skip_group_check=True)
        turn(0, first=True)

        def round_(i, n):
            pe.wait_ge(xnT_done, 4 * (i + 1))
            for m in range(KT):
                for k in range(KT):
                    last = products(nc, bank[m][:], keep["wg_hi"][:, k, m * P:(m + 1) * P],
                                    keep["wg_lo"][:, k, m * P:(m + 1) * P], xnT_hi[:, k], xnT_lo[:, k], k == 0, k == KT - 1)
                last.then_inc(filled, 1)
            for h in range(HEADS):
                pe.wait_ge(gate_done, 4 * i + h + 1)
                last = products(nc, bank[h][:], keep["g_hi"][:, h], keep["g_lo"][:, h], xnT_hi[:, h], xnT_lo[:, h], True, True)
                last.then_inc(filled, 1)
            pe.wait_ge(clo_done, START + i + 1)
            for j in range(TJ):
                pe.wait_ge(q_done, START + 4 * i + j + 1)
                for h in range(HEADS):
                    last = products(nc, bank[j][:, h * P:(h + 1) * P], c_hi[:, h, j * P:(j + 1) * P],
                                    c_lo[:, h, j * P:(j + 1) * P], keep["wh_hi"][:, h], keep["wh_lo"][:, h], True, True)
                last.then_inc(filled, 1)
            if n is not None:
                turn(n)
            for h in range(HEADS):
                for b in range(2):
                    for t in range(2):
                        keys = slice(b * S + t * P, b * S + (t + 1) * P)
                        last = products(nc, acc[:, h, t * S:(t + 1) * S], c_hi[:, h, keys], c_lo[:, h, keys],
                                        q_hi[:, h, b * S:(b + 1) * S], q_lo[:, h, b * S:(b + 1) * S], False, False, skip=True)
                last.then_inc(scores_done, 1)

        with pe.Fori(0, HALF) as i:
            round_(i, i + 1)
        pe.wait_ge(sum_done, START + HALF)
        pe.wait_ge(xnT_done, 4 * (HALF + 1))
        nc.tensor.matmul(bank[0][:, 0:2], ones[:], wsum[:], start=True, stop=True).then_inc(mean_done, 1)
        pe.wait_ge(scale_done, 1)
        with pe.Fori(0, HALF - 1) as i:
            round_(i + HALF, i + HALF + 1)
        round_(NCH - 1, None)

    st.close()


def attn_block(nc, ctx, dram, keep):
    st = ctx.enter_context(ExitStack())
    sb = lambda n, s, d=F32: st.enter_context(nc.sbuf_tensor(n, s, d))
    sem = lambda n: ctx.enter_context(nc.semaphore("a_" + n))
    START = 2
    x = sb("ax", [P, TJ, D])
    v = keep["stage"][:].rearrange("p (a t) d -> p a t d", a=2)
    v_hi, v_lo = sb("av_hi", [P, 2, 2, D], F32R), sb("av_lo", [P, 2, 2, D], F32R)
    gate = sb("agate", [P, KT, CH])
    o = sb("ao", [P, TJ, D])
    og = sb("aog", [P, 2, CH])
    z = sb("az", [P, 2, CH])
    z_hi, z_lo = sb("az_hi", [P, KT, CH], F32R), sb("az_lo", [P, KT, CH], F32R)
    x1 = sb("ax1", [P, TJ, D])
    y = sb("ay", [P, TJ, D])
    yq = sb("ayq", [P, TJ, D], BF16)
    yqT = sb("ayqT", [P, KT, CH], BF16)
    h = sb("ah", [P, 2, HID])
    hq = sb("ahq", [P, 2, HID], BF16)
    hqT = sb("ahqT", [P, HT, P], BF16)
    x2 = sb("ax2", [P, TJ, D])
    x1_held = sb("ax1_held", [P, D])
    ostats, omom = sb("aostats", [P, 2, 6]), sb("aomom", [P, 5, 2])
    ove, orstd, oshift = (sb(n, [P, 2]) for n in ("aove", "aorstd", "aoshift"))
    stats, mom = sb("astats", [P, TJ, 6]), sb("amom", [P, 5, TJ])
    ve, rstd, sq, r2in, r2, scale, shift, amax, qrec, qscale, dq1 = (
        sb("a" + n, [P, TJ]) for n in "ve rstd sq r2in r2 scale shift amax qrec qscale dq1".split())
    hmax, hrec, hscale, dq2 = (sb("a" + n, [P, TJ]) for n in "hmax hrec hscale dq2".split())
    mhalf, rnd, dq2w = sb("amhalf", [P, TJ]), sb("arnd", [P, 1]), sb("adq2w", [P, 1])
    ps_o = st.enter_context(nc.psum_tensor("ps_o", [P, HEADS, 2, P], F32))
    ps_r = [st.enter_context(nc.psum_tensor(f"ps_r{n}", [P, CH], F32)) for n in range(2)]
    ps_t = st.enter_context(nc.psum_tensor("ps_t", [P, 2, 4, P], BF16))
    ps_h = [st.enter_context(nc.psum_tensor(f"ps_h{n}", [P, 512], F32)) for n in range(2)]
    ps_y = st.enter_context(nc.psum_tensor("ps_y", [P, D], F32))
    (v_in, gate_in, x_in, vhi_done, vlo_done, o_done, ostats_done, omom_done, orstd_done, oshift_done, on_done,
     oT_done, og_done, z_done, zhi_done, zlo_done, wo_done, x1_done, stats_done, mom_done, rstd_done, rms_step,
     r2_done, y_done, yg_done, amax_done, qs_done, round_done, yq_done, t_done, t_read, h_done, gelu_done,
     hmax_done, hs_done, hround_done, hq_done, mm2_done, x2_done, x2_out, consts_done, dq2w_done, shift_done, held_done) = (sem(n) for n in (
         "v_in gate_in x_in vhi_done vlo_done o_done ostats_done omom_done orstd_done oshift_done on_done "
         "oT_done og_done z_done zhi_done zlo_done wo_done x1_done stats_done mom_done rstd_done rms_step "
         "r2_done y_done yg_done amax_done qs_done round_done yq_done t_done t_read h_done gelu_done "
         "hmax_done hs_done hround_done hq_done mm2_done x2_done x2_out consts_done dq2w_done shift_done held_done").split())
    TU = 2 * TJ + 2
    x_v = dram["x"].rearrange("(c j p) d -> c p j d", j=TJ, p=P)
    x2_v = dram["x2"].rearrange("(c j p) d -> c j p d", j=TJ, p=P)

    def h_filling(c, j, f):
        return 2 + TU * c + 2 * j + f

    def y_filling(q, a):
        return TU * q + a

    block = st.enter_context(nc.Block())

    @block.sync
    def _(sp):
        def load_v(n):
            sp.wait_ge(vlo_done, START + n)
            sp.dma_start(keep["stage"][:], dram["vals"][n]).then_inc(v_in, 16)

        def load_gate(n):
            sp.wait_ge(z_done, START + 4 * n)
            sp.dma_start(gate[:], dram["gates"][n]).then_inc(gate_in, 16)

        def load_x(n):
            sp.wait_ge(x1_done, START + 4 * n)
            sp.dma_start(x[:], x_v[n]).then_inc(x_in, 16)

        def round_(c, q, ahead):
            if ahead:
                load_v(q + 1)
            for j in range(TJ):
                sp.wait_ge(x2_done, START + 4 * c + j + 1)
                sp.dma_start(x2_v[c, j], x2[:, j]).then_inc(x2_out, 16)
                if ahead and j == 1:
                    load_gate(q + 1)
            if ahead:
                load_x(q + 1)

        sp.sem_inc(x2_out, START)
        for n in range(2):
            if n == 0:
                sp.sem_inc(v_in, 16)
            else:
                load_v(n)
            load_gate(n)
            load_x(n)
        with sp.Fori(0, NCH - 2) as c:
            round_(c, c + 1, True)
        round_(NCH - 2, NCH - 1, False)
        round_(NCH - 1, None, False)
        sp.wait_ge(x2_out, START + 16 * TJ * NCH)

    @block.gpsimd
    def _(pool):
        def cut_v(q):
            pool.wait_ge(vhi_done, q + 1)
            nc.gpsimd.tensor_tensor(v_lo[:], v, f32(v_hi[:]), ALU.subtract).then_inc(vlo_done, 1)

        def group_pow(q, s):
            pool.wait_ge(omom_done, 12 * q + 6 * s + 6)
            nc.gpsimd.tensor_tensor(orstd[:], ove[:], mhalf[:, 0:2], ALU.pow).then_inc(orstd_done, 1)

        def cut_z(q, k):
            pool.wait_ge(zhi_done, 4 * q + k + 1)
            nc.gpsimd.tensor_tensor(z_lo[:, k], z[:, k % 2], f32(z_hi[:, k]), ALU.subtract).then_inc(zlo_done, 1)

        def layer_pow(q, a):
            pool.wait_ge(mom_done, 12 * q + 6 * a + 6)
            cols = slice(2 * a, 2 * a + 2)
            nc.gpsimd.tensor_tensor(rstd[:, cols], ve[:, cols], mhalf[:, cols], ALU.pow).then_inc(rstd_done, 1)
            pool.wait_ge(rms_step, 6 * q + 3 * a + 3)
            nc.gpsimd.tensor_tensor(r2[:, cols], r2in[:, cols], mhalf[:, cols], ALU.pow).then_inc(r2_done, 1)

        def times_gain(q, a):
            for j in (2 * a, 2 * a + 1):
                pool.wait_ge(y_done, 4 * q + j + 1)
                nc.gpsimd.tensor_tensor(y[:, j], y[:, j], keep["gam"][:], ALU.mult).then_inc(yg_done, 1)

        def attention(q, ahead):
            group_pow(q, 0)
            group_pow(q, 1)
            for k in range(KT):
                cut_z(q, k)
            if ahead:
                cut_v(q + 1)
            for a in range(2):
                layer_pow(q, a)
                times_gain(q, a)

        for s in (vlo_done, zlo_done):
            pool.sem_inc(s, START)
        nc.gpsimd.memset(mhalf[:], -0.5).then_inc(consts_done, 1)
        nc.gpsimd.memset(rnd[:], ROUND).then_inc(consts_done, 1)
        pool.wait_ge(consts_done, 1)
        cut_v(0)
        with pool.Fori(0, NCH - 1) as q:
            attention(q, True)
        attention(NCH - 1, False)

    @block.scalar
    def _(act):
        def cut_v(q):
            act.wait_ge(v_in, 16 * (q + 1))
            nc.scalar.activation(v_hi[:], v, ACT.Copy).then_inc(vhi_done, 1)

        def group_norm(q, s):
            act.wait_ge(oshift_done, 2 * q + s + 1)
            for b in range(2):
                nc.scalar.activation(o[:, 2 * b + s].rearrange("p (h e) -> p h e", e=P), ps_o[:, :, b], ACT.Identity,
                                     bias=oshift[:, b:b + 1], scale=orstd[:, b:b + 1]).then_inc(on_done, 1)

        def times_gamma(q, k):
            act.wait_ge(oT_done, 4 * q + k + 1)
            act.wait_ge(z_done, START + 4 * q + k - 1)
            nc.scalar.activation(og[:, k % 2], ps_r[k % 2][:], ACT.Identity, bias=keep["vecs"][:, V_BETA + k:V_BETA + k + 1],
                                 scale=keep["vecs"][:, V_GAMMA + k:V_GAMMA + k + 1]).then_inc(og_done, 1)

        def cut_z(q, k):
            act.wait_ge(z_done, START + 4 * q + k + 1)
            nc.scalar.activation(z_hi[:, k], z[:, k % 2], ACT.Copy).then_inc(zhi_done, 1)

        def layer_norm(q, a):
            act.wait_ge(shift_done, 4 * q + 2 * a + 2)
            act.wait_ge(yq_done, START + 4 * q)
            for j in (2 * a, 2 * a + 1):
                nc.scalar.activation(y[:, j], x1[:, j], ACT.Identity, bias=shift[:, j:j + 1], scale=scale[:, j:j + 1]).then_inc(y_done, 1)

        def round_y(q, a):
            act.wait_ge(qs_done, 10 * q + 5 * a + 5)
            for j in (2 * a, 2 * a + 1):
                nc.scalar.activation(y[:, j], y[:, j], ACT.Identity, bias=rnd[:], scale=qscale[:, j:j + 1]).then_inc(round_done, 1)

        def gelu(c, j, ns=range(4)):
            act.wait_ge(hq_done, START + 4 * c + j - 1)
            for n in ns:
                act.wait_ge(h_done, 16 * c + 4 * j + n + 1)
                nc.scalar.activation(h[:, j % 2, n * 512:(n + 1) * 512], ps_h[n % 2][:], ACT.Gelu,
                                     scale=dq1[:, j:j + 1]).then_inc(gelu_done, 1)

        def round_h(c, j):
            act.wait_ge(hs_done, 4 * (4 * c + j + 1))
            nc.scalar.activation(h[:, j % 2], h[:, j % 2], ACT.Identity, bias=rnd[:], scale=hscale[:, j:j + 1]).then_inc(hround_done, 1)

        def hold_x1(c):
            act.wait_ge(x2_done, START + 4 * c)
            nc.scalar.activation(x1_held[:], x1[:, TJ - 1], ACT.Copy).then_inc(held_done, 1)

        for s in (gelu_done, on_done):
            act.sem_inc(s, START)
        act.wait_ge(consts_done, 2)
        cut_v(0)
        group_norm(0, 0)
        group_norm(0, 1)
        times_gamma(0, 0)
        times_gamma(0, 1)
        cut_z(0, 0)
        times_gamma(0, 2)
        cut_z(0, 1)
        times_gamma(0, 3)
        cut_z(0, 2)
        cut_z(0, 3)
        cut_v(1)
        layer_norm(0, 0)
        round_y(0, 0)
        layer_norm(0, 1)
        gelu(0, 0)

        def round_(c, q, ahead):
            last = q is None
            gelu(c, 1, (0, 1))
            round_y(c, 1)
            round_h(c, 0)
            gelu(c, 1, (2, 3))
            if not last:
                group_norm(q, 0)
            gelu(c, 2)
            round_h(c, 1)
            if not last:
                group_norm(q, 1)
            hold_x1(c)
            if not last:
                times_gamma(q, 0)
                times_gamma(q, 1)
                cut_z(q, 0)
                times_gamma(q, 2)
                cut_z(q, 1)
            if ahead:
                cut_v(q + 1)
            gelu(c, 3, (0, 1))
            if not last:
                times_gamma(q, 3)
                cut_z(q, 2)
            round_h(c, 2)
            gelu(c, 3, (2, 3))
            if not last:
                cut_z(q, 3)
            round_h(c, 3)
            if not last:
                layer_norm(q, 0)
                round_y(q, 0)
                gelu(q, 0, (0, 1))
                layer_norm(q, 1)
                gelu(q, 0, (2, 3))

        with act.Fori(0, NCH - 2) as c:
            round_(c, c + 1, True)
        round_(NCH - 2, NCH - 1, False)
        round_(NCH - 1, None, False)

    @block.vector
    def _(dve):
        def group_stats(q, s):
            dve.wait_ge(o_done, 2 * q + s + 1)
            for b in range(2):
                nc.vector.bn_stats(ostats[:, b], ps_o[:, :, b]).then_inc(ostats_done, 1)
            dve.wait_ge(ostats_done, 4 * q + 2 * s + 2)
            variance(nc, dve, ostats, omom, ove[:], GN_EPS, omom_done, 12 * q + 6 * s)

        def group_shift(q, s):
            dve.wait_ge(orstd_done, 2 * q + s + 1)
            dve.wait_ge(on_done, START + 4 * q + 2 * s)
            nc.vector.scalar_tensor_tensor(out=oshift[:], in0=omom[:, 0], scalar=-0.5, in1=orstd[:], op0=ALU.mult,
                                           op1=ALU.mult).then_inc(oshift_done, 1)

        def gated(q, k):
            if k == 0:
                dve.wait_ge(gate_in, 16 * (q + 1))
            dve.wait_ge(og_done, 4 * q + k + 1)
            if k >= 2:
                dve.wait_ge(zlo_done, START + 4 * q + k - 1)
            nc.vector.tensor_tensor(z[:, k % 2], og[:, k % 2], gate[:, k], ALU.mult).then_inc(z_done, 1)

        def add_x(q, j, c=None):
            dve.wait_ge(wo_done, 4 * q + j + 1)
            if j == 0:
                dve.wait_ge(x_in, 16 * (q + 1))
            if c is not None and j < TJ - 1:
                dve.wait_ge(x2_done, START + 4 * c + j + 1)
            if c is not None and j == TJ - 1:
                dve.wait_ge(held_done, c + 1)
            nc.vector.scalar_tensor_tensor(out=x1[:, j], in0=ps_r[j % 2][:], scalar=keep["gains"][:, 0:1], in1=x[:, j],
                                           op0=ALU.mult, op1=ALU.add).then_inc(x1_done, 1)
            dve.wait_ge(x1_done, START + 4 * q + j + 1)
            nc.vector.bn_stats(stats[:, j], x1[:, j]).then_inc(stats_done, 1)

        def pair_variance(q, a):
            cols = slice(2 * a, 2 * a + 2)
            dve.wait_ge(stats_done, 4 * q + 2 * a + 2)
            variance(nc, dve, stats[:, cols], mom[:, :, cols], ve[:, cols], LN_EPS, mom_done, 12 * q + 6 * a)

        def pair_rms(q, a):
            cols = slice(2 * a, 2 * a + 2)
            n = 6 * q + 3 * a
            dve.wait_ge(rstd_done, 2 * q + a + 1)
            nc.vector.tensor_tensor(sq[:, cols], rstd[:, cols], rstd[:, cols], ALU.mult).then_inc(rms_step, 1)
            dve.wait_ge(rms_step, n + 1)
            nc.vector.scalar_tensor_tensor(out=r2in[:, cols], in0=ve[:, cols], scalar=LN_EPS, in1=sq[:, cols], op0=ALU.subtract,
                                           op1=ALU.mult).then_inc(rms_step, 1)
            dve.wait_ge(rms_step, n + 2)
            nc.vector.tensor_scalar(r2in[:, cols], r2in[:, cols], RMS_EPS, None, ALU.add).then_inc(rms_step, 1)

        def pair_shift(q, a):
            cols = slice(2 * a, 2 * a + 2)
            dve.wait_ge(r2_done, 2 * q + a + 1)
            nc.vector.tensor_tensor(scale[:, cols], rstd[:, cols], r2[:, cols], ALU.mult).then_inc(shift_done, 1)
            dve.wait_ge(shift_done, 4 * q + 2 * a + 1)
            nc.vector.scalar_tensor_tensor(out=shift[:, cols], in0=mom[:, 0, cols], scalar=-0.5, in1=scale[:, cols], op0=ALU.mult,
                                           op1=ALU.mult).then_inc(shift_done, 1)

        def pair_scale(q, a):
            cols = slice(2 * a, 2 * a + 2)
            n = 10 * q + 5 * a
            dve.wait_ge(yg_done, 4 * q + 2 * a + 2)
            nc.vector.tensor_reduce(amax[:, cols], y[:, cols], AX.X, ALU.max, apply_absolute_value=True).then_inc(amax_done, 1)
            dve.wait_ge(amax_done, 2 * q + a + 1)
            nc.vector.tensor_scalar(amax[:, cols], amax[:, cols], 1e-5, None, ALU.max).then_inc(qs_done, 1)
            dve.wait_ge(qs_done, n + 1)
            nc.vector.reciprocal(qrec[:, cols], amax[:, cols]).then_inc(qs_done, 1)
            nc.vector.tensor_scalar(dq1[:, cols], amax[:, cols], 1.0 / QMAX, keep["wmean"][:, 0:1], ALU.mult, ALU.mult).then_inc(qs_done, 2)
            dve.wait_ge(qs_done, n + 4)
            nc.vector.tensor_scalar(qscale[:, cols], qrec[:, cols], QMAX, None, ALU.mult).then_inc(qs_done, 1)

        def pair_bf16(q, a):
            for j in (2 * a, 2 * a + 1):
                dve.wait_ge(round_done, 4 * q + j + 1)
                nc.vector.tensor_scalar(yq[:, j], y[:, j], ROUND, None, ALU.subtract).then_inc(yq_done, 1)

        def read_yT(q, a):
            dve.wait_ge(t_done, y_filling(q, a) + 1)
            nc.vector.tensor_copy(yqT[:, :, 2 * a * P:(2 * a + 2) * P].rearrange("p k (j n) -> p j k n", n=P),
                                  ps_t[:]).then_inc(t_read, 1)

        def scale_h(c, j):
            col = slice(j, j + 1)
            dve.wait_ge(gelu_done, START + 16 * c + 4 * j + 4)
            nc.vector.tensor_reduce(hmax[:, col], h[:, j % 2], AX.X, ALU.max, apply_absolute_value=True).then_inc(hmax_done, 1)
            n = 4 * (4 * c + j)
            dve.wait_ge(hmax_done, 4 * c + j + 1)
            nc.vector.tensor_scalar(hmax[:, col], hmax[:, col], 1e-5, None, ALU.max).then_inc(hs_done, 1)
            dve.wait_ge(hs_done, n + 1)
            nc.vector.reciprocal(hrec[:, col], hmax[:, col]).then_inc(hs_done, 1)
            nc.vector.tensor_scalar(dq2[:, col], hmax[:, col], dq2w[:], None, ALU.mult).then_inc(hs_done, 1)
            dve.wait_ge(hs_done, n + 3)
            nc.vector.tensor_scalar(hscale[:, col], hrec[:, col], QMAX, None, ALU.mult).then_inc(hs_done, 1)

        def to_bf16(c, j):
            dve.wait_ge(hround_done, 4 * c + j + 1)
            nc.vector.tensor_scalar(hq[:, j % 2], h[:, j % 2], ROUND, None, ALU.subtract).then_inc(hq_done, 1)

        def read_hT(c, j, fs):
            for f in fs:
                dve.wait_ge(t_done, h_filling(c, j, f) + 1)
                if f == 0:
                    dve.wait_ge(mm2_done, START + 4 * c + j)
                nc.vector.tensor_copy(hqT[:, 8 * f:8 * f + 8], ps_t[:].rearrange("p a b n -> p (a b) n")).then_inc(t_read, 1)

        def residual(c, j):
            if j == 0:
                dve.wait_ge(x2_out, START + 16 * TJ * c)
            if j == TJ - 1:
                dve.wait_ge(held_done, c + 1)
            dve.wait_ge(mm2_done, START + 4 * c + j + 1)
            nc.vector.scalar_tensor_tensor(out=x2[:, j], in0=ps_y[:], scalar=dq2[:, j:j + 1],
                                           in1=x1[:, j] if j < TJ - 1 else x1_held[:], op0=ALU.mult,
                                           op1=ALU.add).then_inc(x2_done, 1)

        for s in (z_done, x1_done, hq_done, t_read, x2_done, yq_done):
            dve.sem_inc(s, START)
        nc.vector.tensor_scalar(dq2w[:], keep["wmean"][:, 1:2], keep["gains"][:, 2:3], 1.0 / QMAX, ALU.mult, ALU.mult).then_inc(dq2w_done, 1)
        dve.wait_ge(dq2w_done, 1)
        for s in range(2):
            group_stats(0, s)
            group_shift(0, s)
        for k in range(KT):
            gated(0, k)
        for a in range(2):
            add_x(0, 2 * a)
            add_x(0, 2 * a + 1)
            pair_variance(0, a)
            pair_rms(0, a)
            pair_shift(0, a)
            pair_scale(0, a)
            if a == 0:
                pair_bf16(0, 0)
                read_yT(0, 0)

        def round_(c, q):
            last = q is None
            scale_h(c, 0)
            pair_bf16(c, 1)
            to_bf16(c, 0)
            read_yT(c, 1)
            if not last:
                group_stats(q, 0)
                group_shift(q, 0)
            read_hT(c, 0, (0,))
            read_hT(c, 0, (1,))
            scale_h(c, 1)
            if not last:
                group_stats(q, 1)
                group_shift(q, 1)
            residual(c, 0)
            to_bf16(c, 1)
            if not last:
                gated(q, 0)
                gated(q, 1)
            read_hT(c, 1, (0,))
            if not last:
                gated(q, 2)
            read_hT(c, 1, (1,))
            scale_h(c, 2)
            if not last:
                gated(q, 3)
            to_bf16(c, 2)
            residual(c, 1)
            read_hT(c, 2, (0,))
            scale_h(c, 3)
            if not last:
                add_x(q, 0, c)
            read_hT(c, 2, (1,))
            if not last:
                add_x(q, 1, c)
                pair_variance(q, 0)
            to_bf16(c, 3)
            if not last:
                pair_rms(q, 0)
            residual(c, 2)
            if not last:
                pair_shift(q, 0)
                add_x(q, 2, c)
            read_hT(c, 3, (0,))
            if not last:
                pair_scale(q, 0)
            read_hT(c, 3, (1,))
            if not last:
                add_x(q, 3, c)
                pair_bf16(q, 0)
                pair_variance(q, 1)
                read_yT(q, 0)
                pair_rms(q, 1)
            residual(c, 3)
            if not last:
                pair_shift(q, 1)
                pair_scale(q, 1)

        with dve.Fori(0, NCH - 1) as c:
            round_(c, c + 1)
        round_(NCH - 1, None)

    @block.tensor
    def _(pe):
        def retention(q, s):
            if s == 0:
                pe.wait_ge(vlo_done, START + q + 1)
            pe.wait_ge(on_done, START + 4 * q + 2 * s)
            for h_ in range(HEADS):
                for t in range(2):
                    cols = slice(t * S + s * P, t * S + (s + 1) * P)
                    last = products(nc, ps_o[:, h_], keep["at_hi"][:, h_, cols], keep["at_lo"][:, h_, cols],
                                    v_hi[:, :, t, h_ * P:(h_ + 1) * P], v_lo[:, :, t, h_ * P:(h_ + 1) * P], t == 0, t == 1,
                                    skip=True)
            last.then_inc(o_done, 1)

        def turn_o(q, k):
            if k == 0:
                pe.wait_ge(on_done, START + 4 * q + 4)
            if k < 2:
                pe.wait_ge(x1_done, START + 4 * q)
            else:
                pe.wait_ge(og_done, 4 * q + k - 1)
            for j in range(TJ):
                last = nc.tensor.transpose(ps_r[k % 2][:, j * P:(j + 1) * P], o[:, j, k * P:(k + 1) * P], keep["ident"][:])
            last.then_inc(oT_done, 1)

        def project(q, j):
            if j == 0:
                pe.wait_ge(zlo_done, START + 4 * q + 4)
            if j < 2:
                pe.wait_ge(og_done, 4 * q + 3 + j)
            else:
                pe.wait_ge(x1_done, START + 4 * q + j - 1)
            for k in range(KT):
                last = products(nc, ps_r[j % 2][:], z_hi[:, k, j * P:(j + 1) * P], z_lo[:, k, j * P:(j + 1) * P],
                                keep["wo_hi"][:, k], keep["wo_lo"][:, k], k == 0, k == KT - 1)
            last.then_inc(wo_done, 1)

        def turn_y(q, a):
            pe.wait_ge(yq_done, START + 4 * q + 2 * a + 2)
            pe.wait_ge(t_read, START + y_filling(q, a))
            for j in range(2):
                for k in range(KT):
                    last = nc.tensor.transpose(ps_t[:, j, k], yq[:, 2 * a + j, k * P:(k + 1) * P], keep["identb"][:])
            last.then_inc(t_done, 1)

        def mm1(c, j, ready, ns=range(4)):
            pe.wait_ge(t_read, START + ready)
            for n in ns:
                pe.wait_ge(gelu_done, START + 16 * c + 4 * j + n - 1)
                for k in range(KT):
                    last = nc.tensor.matmul(ps_h[n % 2][:], yqT[:, k, j * P:(j + 1) * P], keep["w1q"][:, k, n * 512:(n + 1) * 512],
                                            start=(k == 0), stop=(k == KT - 1))
                last.then_inc(h_done, 1)

        def turn_h(c, j, f):
            pe.wait_ge(hq_done, START + 4 * c + j + 1)
            pe.wait_ge(t_read, START + h_filling(c, j, f))
            for m in range(8):
                last = nc.tensor.transpose(ps_t[:, m // 4, m % 4], hq[:, j % 2, (8 * f + m) * P:(8 * f + m + 1) * P], keep["identb"][:])
            last.then_inc(t_done, 1)

        def mm2(c, j):
            pe.wait_ge(x2_done, START + 4 * c + j)
            for f in range(2):
                pe.wait_ge(t_read, START + h_filling(c, j, f) + 1)
                for k in range(8 * f, 8 * f + 8):
                    last = nc.tensor.matmul(ps_y[:], hqT[:, k], keep["w2q"][:, k], start=(k == 0), stop=(k == HT - 1))
            last.then_inc(mm2_done, 1)

        pe.sem_inc(mm2_done, START)
        retention(0, 0)
        retention(0, 1)
        for k in range(KT):
            turn_o(0, k)
        for j in range(TJ):
            project(0, j)
        turn_y(0, 0)
        mm1(0, 0, 1)

        def round_(c, q):
            last = q is None
            before = h_filling(c, 0, 0)
            mm1(c, 1, y_filling(c, 0) + 1)
            if not last:
                retention(q, 0)
            turn_y(c, 1)
            turn_h(c, 0, 0)
            mm1(c, 2, before, (0, 1))
            turn_h(c, 0, 1)
            if not last:
                retention(q, 1)
            mm1(c, 2, before, (2, 3))
            mm2(c, 0)
            if not last:
                turn_o(q, 0)
                turn_o(q, 1)
            turn_h(c, 1, 0)
            if not last:
                turn_o(q, 2)
            turn_h(c, 1, 1)
            if not last:
                turn_o(q, 3)
            mm1(c, 3, before)
            mm2(c, 1)
            turn_h(c, 2, 0)
            if not last:
                project(q, 0)
            turn_h(c, 2, 1)
            if not last:
                project(q, 1)
            mm2(c, 2)
            if not last:
                project(q, 2)
            turn_h(c, 3, 0)
            if not last:
                project(q, 3)
            turn_h(c, 3, 1)
            mm2(c, 3)
            if not last:
                turn_y(q, 0)
                mm1(q, 0, y_filling(q, 0) + 1)

        with pe.Fori(0, NCH - 1) as c:
            round_(c, c + 1)
        round_(NCH - 1, None)

    st.close()


def experts_block(nc, ctx, dram, keep):
    st = ctx.enter_context(ExitStack())
    sb = lambda n, s, d=F32: st.enter_context(nc.sbuf_tensor("e_" + n, s, d))
    ps = lambda n, s: st.enter_context(nc.psum_tensor("e_" + n, s, F32))
    sem = lambda n: ctx.enter_context(nc.semaphore("e_" + n))
    START = 2
    gu_raw, gu_hi, gu_lo = sb("gu_raw", [P, 2, 2, KT, P]), sb("gu_hi", [P, 2, 2, KT, P], F32R), sb("gu_lo", [P, 2, 2, KT, P], F32R)
    dn_raw, dn_hi, dn_lo = sb("dn_raw", [P, 2, D]), sb("dn_hi", [P, 2, D], F32R), sb("dn_lo", [P, 2, D], F32R)
    x = sb("x", [P, TJ, D])
    xq = sb("xq", [P, TJ, D])
    x2T = sb("x2T", [P, KT, CH])
    qe = sb("qe", [P, KT * B * CHD, EXT])
    c = sb("c", [P, KT, CH])
    ke = sb("ke", [P, KT * B, EXT])
    kv_raw = sb("kv_raw", [P, 2, B, PAIRS])
    kv_hi, kv_lo = sb("kv_hi", [P, KT, B, PAIRS], F32R), sb("kv_lo", [P, KT, B, PAIRS], F32R)
    t_raw, t_hi, t_lo = sb("t_raw", [P, D]), sb("t_hi", [P, D], F32R), sb("t_lo", [P, D], F32R)
    ZW, ZROW = 160, 20
    zp = sb("zp", [P, B, ZW])
    skip = sb("skip", [P, NCH * CHD])
    x3T = sb("x3T", [P, KT, CH])
    xnat = sb("xnat", [P, TJ, D])
    xn_hi, xn_lo = sb("xn_hi", [P, KT, CH], F32R), sb("xn_lo", [P, KT, CH], F32R)
    wb = sb("wb", [P, NE, CH])
    wT_hi, wT_lo = sb("wT_hi", [8, CH], F32R), sb("wT_lo", [8, CH], F32R)
    sg, sgw, hd = sb("sg", [P, CH]), sb("sgw", [P, CH]), sb("hd", [P, CH])
    lgT = sgw[0:8]
    hd_hi, hd_lo = sb("hd_hi", [P, 2, CH], F32R), sb("hd_lo", [P, 2, CH], F32R)
    y = sb("y", [P, KT, CH])
    bd_raw, bd_hi, bd_lo = hd[0:8], sb("bd_hi", [8, D], F32R), sb("bd_lo", [8, D], F32R)
    sel_raw, sel = y[0:8, 0:2].rearrange("p k n -> p (k n)")[:, 0:NE * P], sb("sel", [8, NE * P], F32R)
    wr_raw, wr_hi, wr_lo = xnat[:, 0:KT, 0:8], sb("wr_hi", [P, KT, 8], F32R), sb("wr_lo", [P, KT, 8], F32R)
    lg, lx, rank, keepw, ew, w = (sb(n, [P, TJ, 8]) for n in "lg lx rank keepw ew w".split())
    ge, gt, below, above = (sb(n, [P, 4 * 64]) for n in "ge gt below above".split())
    lmax, wsum, wrec = (sb(n, [P, TJ]) for n in "lmax wsum wrec".split())
    stats, mom = sb("stats", [P, TJ, 6]), sb("mom", [P, 5, TJ])
    ve, rstd, shift, mhalf = (sb(n, [P, TJ]) for n in "ve rstd shift mhalf".split())
    pstats, pmom = sb("pstats", [P, 2, 6]), sb("pmom", [P, 5, 2])
    pve, prstd, pshift = (sb(n, [P, 2]) for n in "pve prstd pshift".split())
    gb = sb("gb", [P, KT])

    ps_out = ps("ps_out", [P, KT, CH])
    ps_g, ps_u, ps_m = ps("ps_g", [P, CH]), ps("ps_u", [P, CH]), ps("ps_m", [P, 2, CH])
    first = [ps_m[:], ps_out[:, 0:2]]

    names = ("const_in const_done setup_hi setup_lo gb_done guhi_done gulo_done dnhi_done dnlo_done gate_done gu_done "
             "silu_done sgw_done stt_done hdhi_done hdlo_done down_done y_copied y_done y_out x_in c_in t_in "
             "stats_done mom_done rstd_done shift_done xq_done x2T_filled x2T_done q_filled qe_done ke_done kvraw_done "
             "kvhi_done kvlo_done td_done thi_done tlo_done unit_done prod_done red_done x3_done nat_filled pstats_done "
             "pmom_done prstd_done pshift_done xnat_done xnT_filled xnhi_done xn_done lgT_filled lgT_done lg_filled lg_done rt exp_done w_done "
             "wT_filled wThi_done wT_done wb_filled wb_done")
    (const_in, const_done, setup_hi, setup_lo, gb_done, guhi_done, gulo_done, dnhi_done, dnlo_done, gate_done, gu_done,
     silu_done, sgw_done, stt_done, hdhi_done, hdlo_done, down_done, y_copied, y_done, y_out, x_in, c_in, t_in,
     stats_done, mom_done, rstd_done, shift_done, xq_done, x2T_filled, x2T_done, q_filled, qe_done, ke_done, kvraw_done,
     kvhi_done, kvlo_done, td_done, thi_done, tlo_done, unit_done, prod_done, red_done, x3_done, nat_filled, pstats_done,
     pmom_done, prstd_done, pshift_done, xnat_done, xnT_filled, xnhi_done, xn_done, lgT_filled, lgT_done, lg_filled, lg_done, rt, exp_done, w_done,
     wT_filled, wThi_done, wT_done, wb_filled, wb_done) = (sem(n) for n in names.split())
    gu_in, dn_in = ([sem(n + "0"), sem(n + "1")] for n in ("gu_in", "dn_in"))
    RT = 15

    def view(t, offset, *dims):
        return bass.AP(t[:].tensor, t[:].offset + offset, [list(t[:].ap[0])] + [list(d) for d in dims])

    FIRST_UNIT_STEP = 2
    UNITS = {FIRST_UNIT_STEP: [0]}
    u = 1
    for s in range(3, 13):
        UNITS[s] = list(range(u, u + (2 if s % 2 else 1)))
        u += len(UNITS[s])
    assert u == CHD * KT
    T_STEPS = (3, 5, 8)
    routed = lambda s: s < RSTEPS
    block = st.enter_context(nc.Block())

    @block.sync
    def _(sp):
        def load_gu(g, s):
            n = STEPS * g + s
            s %= STEPS
            sp.wait_ge(gulo_done, START + n - 1)
            if routed(s):
                sp.dma_start(gu_raw[:, s % 2].rearrange("p a k n -> p (a k n)"), dram["mgu"][s]).then_inc(gu_in[s % 2], 16)
            else:
                sp.dma_start(gu_raw[:, s % 2, 1].rearrange("p k n -> p (k n)"), dram["msu"][s - RSTEPS]).then_inc(gu_in[s % 2], 16)

        def load_dn(g, s):
            n = STEPS * g + s
            s %= STEPS
            sp.wait_ge(dnlo_done, START + n - 1)
            sp.dma_start(dn_raw[:, s % 2], dram["md"][s]).then_inc(dn_in[s % 2], 16)

        def load_x(q):
            sp.wait_ge(xq_done, START + 4 * q)
            sp.wait_ge(x2T_done, START + 2 * q)
            for j in range(TJ):
                sp.dma_start(x[:, j],
                             dram["x2"].rearrange("(j b g r) d -> g j b r d", j=TJ, b=4, g=NCH)[q, j]).then_inc(x_in, 16)

        def load_c(q):
            sp.wait_ge(ke_done, START + 2 * CHD * q)
            sp.dma_start(c[:], dram["ctxG"].rearrange("g (k p) n -> g p k n", p=P)[q]).then_inc(c_in, 16)

        def load_t(q, hh):
            sp.wait_ge(tlo_done, START + CHD * q + hh)
            sp.dma_start(t_raw[:], dram["toep"][CHD * q + hh]).then_inc(t_in, 16)

        def store(g):
            sp.wait_ge(y_done, START + 4 * g + 4)
            sp.dma_start(dram["out"].rearrange("g (k p) n -> g p k n", p=P)[g], y[:]).then_inc(y_out, 16)

        sp.sem_inc(y_out, START)
        load_x(0)
        load_c(0)
        load_t(0, 0)
        for t, name in ((bd_raw, "bdown"), (sel_raw, "sel"), (wr_raw, "wroute"), (below[:], "below"), (above[:], "above"),
                        (skip[:], "skipD")):
            sp.dma_start(t, dram[name]).then_inc(const_in, 16)
        load_gu(0, 0)
        load_dn(0, 0)
        load_gu(0, 1)
        for hh in range(1, CHD):
            load_t(0, hh)
        load_x(1)
        load_c(1)
        load_t(1, 0)

        def round_(g, q, ahead):
            for s in range(STEPS):
                if q is not None or s < STEPS - 2:
                    load_gu(g, s + 2)
                if q is not None or s < STEPS - 1:
                    load_dn(g, s + 1)
                if q is not None and s in T_STEPS:
                    load_t(q, T_STEPS.index(s) + 1)
                if ahead and s == 2:
                    load_x(q + 1)
                if ahead and s == 11:
                    load_c(q + 1)
                    load_t(q + 1, 0)
            store(g)

        with sp.Fori(0, NCH - 2) as g:
            round_(g, g + 1, True)
        round_(NCH - 2, NCH - 1, False)
        round_(NCH - 1, None, False)
        sp.wait_ge(y_out, START + 16 * NCH)

    @block.gpsimd
    def _(pool):
        def cut_gu(g, s):
            n = STEPS * g + s
            s %= STEPS
            pool.wait_ge(guhi_done, n + 1)
            a = slice(0 if routed(s) else 1, 2)
            nc.gpsimd.tensor_tensor(gu_lo[:, s % 2, a], gu_raw[:, s % 2, a], f32(gu_hi[:, s % 2, a]), ALU.subtract).then_inc(gulo_done, 1)

        def cut_dn(g, s):
            n = STEPS * g + s
            pool.wait_ge(dnhi_done, n + 1)
            nc.gpsimd.tensor_tensor(dn_lo[:, s % 2], dn_raw[:, s % 2], f32(dn_hi[:, s % 2]), ALU.subtract).then_inc(dnlo_done, 1)

        def weigh(g, s):
            if not routed(s):
                return
            pool.wait_ge(silu_done, START + STEPS * g + s + 1)
            pool.wait_ge(wb_done, START + 3 * g + s // 4 + 1)
            pool.wait_ge(stt_done, START + RSTEPS * g + s)
            nc.gpsimd.tensor_tensor(sgw[:], sg[:], wb[:, s // 2], ALU.mult).then_inc(sgw_done, 1)

        def pairs(q, u):
            v = CHD * KT * q + u
            m = u % KT
            pool.wait_ge(ke_done, START + 2 * (CHD * q + u // KT + 1))
            pool.wait_ge(kvlo_done, START + v - 1)
            out = kv_raw[:, u % 2]
            nc.gpsimd.tensor_tensor(out[:, :, 0:32].rearrange("p b (d i) -> p b d i", i=CD),
                                    view(ke, m * B * EXT, (EXT, B), (0, 4), (1, CD)),
                                    view(ke, m * B * EXT, (EXT, B), (1, 4), (1, CD)), ALU.mult).then_inc(kvraw_done, 1)
            nc.gpsimd.tensor_tensor(out[:, :, 32:36], ke[:, m * B:(m + 1) * B, 0:4], ke[:, m * B:(m + 1) * B, 4:8],
                                    ALU.mult).then_inc(kvraw_done, 1)

        def conv_pow(q):
            pool.wait_ge(mom_done, 6 * q + 6)
            nc.gpsimd.tensor_tensor(rstd[:], ve[:], mhalf[:], ALU.pow).then_inc(rstd_done, 1)

        def nat_pow(q, a):
            pool.wait_ge(pmom_done, 12 * q + 6 * a + 6)
            nc.gpsimd.tensor_tensor(prstd[:], pve[:], mhalf[:, 0:2], ALU.pow).then_inc(prstd_done, 1)

        for s in (gulo_done, dnlo_done, sgw_done, kvraw_done):
            pool.sem_inc(s, START)
        nc.gpsimd.memset(mhalf[:], -0.5).then_inc(const_done, 1)
        pool.wait_ge(const_done, 1)
        conv_pow(0)
        pairs(0, 0)
        pairs(0, 1)
        for u in range(CHD * KT):
            if u + 2 < CHD * KT:
                pairs(0, u + 2)
        nat_pow(0, 0)
        nat_pow(0, 1)
        cut_gu(0, 0)

        def round_(g, q):
            for s in range(STEPS):
                units = UNITS.get(s, []) if q is not None else []
                if q is not None or s < STEPS - 1:
                    cut_gu(g, s + 1)
                cut_dn(g, s)
                weigh(g, s)
                if q is not None and s == 0:
                    conv_pow(q)
                if q is not None and s in (1, 2):
                    pairs(q, s - 1)
                for u in units:
                    if u + 2 < CHD * KT:
                        pairs(q, u + 2)
                if q is not None and s in (13, 14):
                    nat_pow(q, s - 13)

        with pool.Fori(0, NCH - 1) as g:
            round_(g, g + 1)
        round_(NCH - 1, None)

    @block.scalar
    def _(act):
        vecs = keep["vecs"]

        def cut_gu(g, s):
            n = STEPS * g + s
            act.wait_ge(gu_in[s % 2], 16 * (STEPS // 2 * g + s // 2 + 1))
            s %= STEPS
            act.wait_ge(gu_done, START + n - 1)
            a = slice(0 if routed(s) else 1, 2)
            nc.scalar.activation(gu_hi[:, s % 2, a], gu_raw[:, s % 2, a], ACT.Copy).then_inc(guhi_done, 1)

        def cut_dn(g, s):
            n = STEPS * g + s
            act.wait_ge(dn_in[s % 2], 16 * (STEPS // 2 * g + s // 2 + 1))
            act.wait_ge(down_done, START + n - 1)
            nc.scalar.activation(dn_hi[:, s % 2], dn_raw[:, s % 2], ACT.Copy).then_inc(dnhi_done, 1)

        def silu(g, s):
            n = STEPS * g + s
            if routed(s):
                act.wait_ge(gate_done, RSTEPS * g + s + 1)
                act.wait_ge(sgw_done, START + RSTEPS * g + s)
                nc.scalar.activation(sg[:], ps_g[:], ACT.Silu, bias=vecs[:, V_BG + s:V_BG + s + 1]).then_inc(silu_done, 1)
            else:
                act.wait_ge(gu_done, START + n + 1)
                act.wait_ge(hdlo_done, START + n)
                nc.scalar.activation(hd[:], ps_u[:], ACT.Silu,
                                     bias=vecs[:, V_BSU + s - RSTEPS:V_BSU + s - RSTEPS + 1]).then_inc(silu_done, 1)

        def cut_hd(g, s):
            n = STEPS * g + s
            if routed(s):
                act.wait_ge(stt_done, START + RSTEPS * g + s + 1)
            else:
                act.wait_ge(silu_done, START + n + 1)
            act.wait_ge(down_done, START + n - 1)
            nc.scalar.activation(hd_hi[:, s % 2], hd[:], ACT.Copy).then_inc(hdhi_done, 1)

        def norm_x(q):
            act.wait_ge(shift_done, q + 1)
            act.wait_ge(q_filled, START + 2 * q)
            for j in range(TJ):
                nc.scalar.activation(xq[:, j], x[:, j], ACT.Identity, bias=shift[:, j:j + 1], scale=rstd[:, j:j + 1]).then_inc(xq_done, 1)

        def read_x2T(q, a):
            act.wait_ge(x2T_filled, 2 * q + a + 1)
            act.wait_ge(x3_done, START + q)
            nc.scalar.activation(x2T[:, 2 * a:2 * a + 2], ps_m[:], ACT.Copy).then_inc(x2T_done, 1)

        def read_q(q, a):
            act.wait_ge(q_filled, START + 2 * q + a + 1)
            act.wait_ge(prod_done, START + 4 * CHD * KT * q)
            half = B * CHD * 2
            src = ps_m[:].rearrange("p a (n i) -> p (a n) i", i=CD)
            nc.scalar.activation(qe[:, half * a:half * (a + 1), 0:CD], src, ACT.Copy).then_inc(qe_done, 1)
            nc.scalar.activation(qe[:, half * a:half * (a + 1), CD:EXT], src[:, :, 0:EXT - CD], ACT.Copy).then_inc(qe_done, 1)

        def keys(q, hh):
            n = CHD * q + hh
            act.wait_ge(c_in, 16 * (q + 1))
            act.wait_ge(kvraw_done, START + 2 * KT * n)
            src = c[:].rearrange("p k (b n) -> p (k b) n", b=B)
            nc.scalar.activation(ke[:, :, 0:CD], src[:, :, hh * CD:(hh + 1) * CD], ACT.Copy).then_inc(ke_done, 1)
            nc.scalar.activation(ke[:, :, CD:EXT], src[:, :, hh * CD:hh * CD + EXT - CD], ACT.Copy).then_inc(ke_done, 1)

        def cut_t(q, hh):
            n = CHD * q + hh
            act.wait_ge(td_done, n + 1)
            act.wait_ge(unit_done, START + KT * n)
            nc.scalar.activation(t_hi[:], t_raw[:], ACT.Copy).then_inc(thi_done, 1)

        def cut_kv(q, u):
            v = CHD * KT * q + u
            act.wait_ge(kvraw_done, START + 2 * (v + 1))
            act.wait_ge(unit_done, START + v - u % KT)
            nc.scalar.activation(kv_hi[:, u % KT], kv_raw[:, u % 2], ACT.Copy).then_inc(kvhi_done, 1)

        def unit(q, u):
            if u % KT == 2 and u // KT < CHD - 1:
                keys(q, u // KT + 1)
            if u + 1 < CHD * KT:
                if (u + 1) % KT == 0:
                    cut_t(q, (u + 1) // KT)
                cut_kv(q, u + 1)

        def norm_nat(q, a):
            act.wait_ge(pshift_done, 2 * q + a + 1)
            act.wait_ge(xnT_filled, START + 2 * q)
            for j in range(2):
                nc.scalar.activation(xnat[:, 2 * a + j], ps_m[:, j], ACT.Identity, bias=pshift[:, j:j + 1],
                                     scale=prstd[:, j:j + 1]).then_inc(xnat_done, 1)

        def cut_xn(q, a):
            act.wait_ge(xnT_filled, START + 2 * q + a + 1)
            nc.scalar.activation(xn_hi[:, 2 * a:2 * a + 2], ps_m[:], ACT.Copy).then_inc(xnhi_done, 1)

        def read_lgT(q):
            act.wait_ge(lgT_filled, q + 1)
            nc.scalar.activation(lgT, ps_m[0:8, 0], ACT.Copy).then_inc(lgT_done, 1)

        def exp(q):
            act.wait_ge(rt, RT * q + 9)
            nc.scalar.activation(ew[:], lx[:], ACT.Exp).then_inc(exp_done, 1)

        def cut_wT(g):
            act.wait_ge(wT_filled, g + 1)
            nc.scalar.activation(wT_hi[:], ps_m[0:8, 0], ACT.Copy).then_inc(wThi_done, 1)

        def read_wb(g, a):
            act.wait_ge(wb_filled, 3 * g + a + 1)
            act.wait_ge(sgw_done, START + RSTEPS * g)
            nc.scalar.activation(wb[:, 2 * a:2 * a + 2], ps_m[:], ACT.Copy).then_inc(wb_done, 1)

        def copy_x3(g):
            act.wait_ge(x3_done, START + g + 1)
            act.wait_ge(y_out, START + 16 * g)
            for k in range(KT):
                nc.scalar.activation(y[:, k], x3T[:, k], ACT.Identity, bias=gb[:, k:k + 1]).then_inc(y_copied, 1)

        for s in (silu_done, xq_done, x2T_done, ke_done, qe_done, xnat_done, wb_done, y_copied):
            act.sem_inc(s, START)
        norm_x(0)
        read_x2T(0, 0)
        read_x2T(0, 1)
        keys(0, 0)
        cut_t(0, 0)
        read_q(0, 0)
        read_q(0, 1)
        cut_kv(0, 0)
        act.wait_ge(const_in, 16 * 6)
        nc.scalar.activation(bd_hi[:], bd_raw, ACT.Copy).then_inc(setup_hi, 1)
        nc.scalar.activation(wr_hi[:], wr_raw, ACT.Copy).then_inc(setup_hi, 1)
        nc.scalar.activation(sel[:], sel_raw, ACT.Copy).then_inc(setup_hi, 1)
        for u in range(CHD * KT):
            unit(0, u)
        act.wait_ge(gb_done, 1)
        act.wait_ge(setup_lo, 2)
        norm_nat(0, 0)
        norm_nat(0, 1)
        cut_gu(0, 0)
        cut_xn(0, 0)
        cut_xn(0, 1)
        read_lgT(0)
        exp(0)

        def round_(g, q):
            for s in range(STEPS):
                units = UNITS.get(s, []) if q is not None else []
                if q is not None or s < STEPS - 1:
                    cut_gu(g, s + 1)
                cut_dn(g, s)
                silu(g, s)
                if s == 0:
                    cut_wT(g)
                    read_wb(g, 0)
                    if q is not None:
                        read_x2T(q, 0)
                if s == 1:
                    read_wb(g, 1)
                    if q is not None:
                        norm_x(q)
                if q is not None and s == 2:
                    read_q(q, 0)
                    read_q(q, 1)
                    cut_kv(q, 0)
                if units and s > FIRST_UNIT_STEP:
                    unit(q, units[0])
                if q is not None and s == STEPS - 1:
                    cut_xn(q, 0)
                cut_hd(g, s)
                if units and s == FIRST_UNIT_STEP:
                    unit(q, units[0])
                if len(units) > 1:
                    unit(q, units[1])
                if s == 0:
                    copy_x3(g)
                    if q is not None:
                        read_x2T(q, 1)
                if s == 1:
                    read_wb(g, 2)
                    if q is not None:
                        keys(q, 0)
                        cut_t(q, 0)
                if q is not None and s in (13, 14):
                    norm_nat(q, s - 13)
                if q is not None and s == STEPS - 1:
                    cut_xn(q, 1)
                    read_lgT(q)
                    exp(q)

        with act.Fori(0, NCH - 1) as g:
            round_(g, g + 1)
        round_(NCH - 1, None)

    @block.vector
    def _(dve):
        vecs = keep["vecs"]

        def gated(g, s):
            if not routed(s):
                return
            n = STEPS * g + s
            dve.wait_ge(gu_done, START + n + 1)
            dve.wait_ge(sgw_done, START + RSTEPS * g + s + 1)
            dve.wait_ge(hdlo_done, START + n)
            nc.vector.scalar_tensor_tensor(out=hd[:], in0=ps_u[:], scalar=vecs[:, V_BU + s:V_BU + s + 1], in1=sgw[:], op0=ALU.add,
                                           op1=ALU.mult).then_inc(stt_done, 1)

        def cut_hd(g, s):
            dve.wait_ge(hdhi_done, STEPS * g + s + 1)
            nc.vector.tensor_tensor(hd_lo[:, s % 2], hd[:], f32(hd_hi[:, s % 2]), ALU.subtract).then_inc(hdlo_done, 1)

        def norm_stats(q):
            dve.wait_ge(x_in, 16 * TJ * (q + 1))
            for j in range(TJ):
                nc.vector.bn_stats(stats[:, j], x[:, j]).then_inc(stats_done, 1)
            dve.wait_ge(stats_done, 4 * (q + 1))
            variance(nc, dve, stats, mom, ve[:], LN_EPS, mom_done, 6 * q)

        def norm_shift(q):
            dve.wait_ge(rstd_done, q + 1)
            nc.vector.scalar_tensor_tensor(out=shift[:], in0=mom[:, 0], scalar=-0.5, in1=rstd[:], op0=ALU.mult,
                                           op1=ALU.mult).then_inc(shift_done, 1)

        def add_skip(q, hh):
            n = CHD * q + hh
            dve.wait_ge(t_in, 16 * (n + 1))
            nc.vector.scalar_tensor_tensor(out=t_raw[:, 0:P], in0=keep["ident"][:], scalar=skip[:, bass.ds(n, 1)], in1=t_raw[:, 0:P],
                                           op0=ALU.mult, op1=ALU.add).then_inc(td_done, 1)

        def cut_t(q, hh):
            dve.wait_ge(thi_done, CHD * q + hh + 1)
            nc.vector.tensor_tensor(t_lo[:], t_raw[:], f32(t_hi[:]), ALU.subtract).then_inc(tlo_done, 1)

        def cut_kv(q, u):
            dve.wait_ge(kvhi_done, CHD * KT * q + u + 1)
            nc.vector.tensor_tensor(kv_lo[:, u % KT], kv_raw[:, u % 2], f32(kv_hi[:, u % KT]), ALU.subtract).then_inc(kvlo_done, 1)

        def unit(q, u, src=ps_m[:]):
            hh, lb = u // KT, u % KT
            v = CHD * KT * q + u
            if u + 1 < CHD * KT:
                if (u + 1) % KT == 0:
                    add_skip(q, hh + 1)
                    cut_t(q, hh + 1)
                cut_kv(q, u + 1)
            if u == 0:
                dve.wait_ge(qe_done, START + 4 * (q + 1))
                dve.wait_ge(y_copied, START + 4 * q)
            dve.wait_ge(red_done, START + v)
            dve.wait_ge(unit_done, START + v + 1)
            qo = (lb * B * CHD + hh) * EXT
            qv = lambda off, *dims: view(qe, qo + off, (CHD * EXT, B), *dims)
            yv = lambda off, *dims: bass.AP(src.tensor, src.offset + off, [list(src.ap[0]), [64, B]] + [list(d) for d in dims])
            zv = lambda off, *dims: view(zp, off, (ZW, B), *dims)
            nc.vector.tensor_tensor(zv(68, (21, 4), (1, 8)), yv(0, (8, 4), (1, 8)), qv(0, (1, 4), (1, 8)), ALU.mult).then_inc(prod_done, 1)
            nc.vector.tensor_tensor(zv(152, (4, 2), (1, 4)), yv(32, (0, 2), (1, 4)), qv(4, (4, 2), (1, 4)), ALU.mult).then_inc(prod_done, 1)
            nc.vector.tensor_tensor(zv(2 * ZROW + 8, (-ZROW, 3), (1, 8)), yv(8, (8, 3), (1, 8)), qv(0, (0, 3), (1, 8)),
                                    ALU.mult).then_inc(prod_done, 1)
            nc.vector.tensor_tensor(zv(2 * ZROW + 5, (-ZROW, 3), (1, 3)), yv(8 + 5, (8, 3), (1, 3)), qv(5, (0, 3), (1, 3)),
                                    ALU.mult).then_inc(prod_done, 1)
            dve.wait_ge(prod_done, START + 4 * (v + 1))
            nc.vector.tensor_reduce(x3T[:, lb].rearrange("p (b n) -> p b n", b=B)[:, :, hh * CD:(hh + 1) * CD],
                                    zv(5, (1, 8), (21, 8)), AX.X, ALU.add).then_inc(red_done, 1)

        def add_x2(q):
            dve.wait_ge(red_done, START + CHD * KT * (q + 1))
            dve.wait_ge(x2T_done, START + 2 * (q + 1))
            nc.vector.scalar_tensor_tensor(out=x3T[:], in0=x3T[:], scalar=keep["gains"][:, 1:2], in1=x2T[:], op0=ALU.mult,
                                           op1=ALU.add).then_inc(x3_done, 1)

        def nat_stats(q, a):
            dve.wait_ge(nat_filled, 2 * q + a + 1)
            for j in range(2):
                nc.vector.bn_stats(pstats[:, j], ps_m[:, j]).then_inc(pstats_done, 1)
            dve.wait_ge(pstats_done, 4 * q + 2 * a + 2)
            variance(nc, dve, pstats, pmom, pve[:], LN_EPS, pmom_done, 12 * q + 6 * a)
            dve.wait_ge(prstd_done, 2 * q + a + 1)
            dve.wait_ge(xnat_done, START + 4 * q + 2 * a)
            nc.vector.scalar_tensor_tensor(out=pshift[:], in0=pmom[:, 0], scalar=-0.5, in1=prstd[:], op0=ALU.mult,
                                           op1=ALU.mult).then_inc(pshift_done, 1)

        def cut_xn(q, a):
            dve.wait_ge(xnhi_done, 2 * q + a + 1)
            nc.vector.tensor_tensor(xn_lo[:, 2 * a:2 * a + 2], ps_m[:], f32(xn_hi[:, 2 * a:2 * a + 2]), ALU.subtract).then_inc(xn_done, 1)

        def route(q):
            r0 = RT * q
            n8 = lambda t: t[:].rearrange("p (j i e) -> p j i e", i=8, e=8)
            other, own = view(lg, 0, (8, TJ), (0, 8), (1, 8)), view(lg, 0, (8, TJ), (1, 8), (0, 8))
            row = lambda t: view(t, 0, (1, TJ), (0, 8))
            dve.wait_ge(lg_filled, q + 1)
            nc.vector.tensor_tensor(lg[:], ps_m[:, 1, 0:TJ * 8].rearrange("p (j e) -> p j e", e=8), view(vecs, V_BGATE, (0, TJ), (1, 8)),
                                    ALU.add).then_inc(lg_done, 1)
            dve.wait_ge(lg_done, START + q + 1)
            nc.vector.tensor_tensor(n8(ge), other, own, ALU.is_ge).then_inc(rt, 1)
            nc.vector.tensor_tensor(n8(gt), other, own, ALU.is_gt).then_inc(rt, 1)
            nc.vector.tensor_reduce(lmax[:], lg[:], AX.X, ALU.max).then_inc(rt, 1)
            dve.wait_ge(rt, r0 + 3)
            nc.vector.tensor_tensor(ge[:], ge[:], below[:], ALU.mult).then_inc(rt, 1)
            nc.vector.tensor_tensor(gt[:], gt[:], above[:], ALU.mult).then_inc(rt, 1)
            nc.vector.tensor_tensor(lx[:], lg[:], row(lmax), ALU.subtract).then_inc(rt, 4)
            dve.wait_ge(rt, r0 + 9)
            nc.vector.tensor_tensor(ge[:], ge[:], gt[:], ALU.add).then_inc(rt, 1)
            dve.wait_ge(rt, r0 + 10)
            nc.vector.tensor_reduce(rank[:], n8(ge), AX.X, ALU.add).then_inc(rt, 1)
            dve.wait_ge(rt, r0 + 11)
            nc.vector.tensor_scalar(keepw[:], rank[:], float(NE) - 0.5, None, ALU.is_lt).then_inc(rt, 1)
            dve.wait_ge(rt, r0 + 12)
            dve.wait_ge(exp_done, q + 1)
            nc.vector.tensor_tensor(ew[:], ew[:], keepw[:], ALU.mult).then_inc(rt, 1)
            dve.wait_ge(rt, r0 + 13)
            nc.vector.tensor_reduce(wsum[:], ew[:], AX.X, ALU.add).then_inc(rt, 1)
            dve.wait_ge(rt, r0 + 14)
            nc.vector.reciprocal(wrec[:], wsum[:]).then_inc(rt, 1)
            dve.wait_ge(rt, r0 + 15)
            nc.vector.tensor_tensor(w[:], ew[:], row(wrec), ALU.mult).then_inc(w_done, 1)

        def cut_wT(g):
            dve.wait_ge(wThi_done, g + 1)
            nc.vector.tensor_tensor(wT_lo[:], ps_m[0:8, 0], f32(wT_hi[:]), ALU.subtract).then_inc(wT_done, 1)

        def finish(g):
            dve.wait_ge(down_done, START + STEPS * (g + 1))
            dve.wait_ge(y_copied, START + 4 * (g + 1))
            for k in range(KT):
                nc.vector.scalar_tensor_tensor(out=y[:, k], in0=ps_out[:, k], scalar=keep["gains"][:, 3:4], in1=y[:, k], op0=ALU.mult,
                                               op1=ALU.add).then_inc(y_done, 1)

        for s in (hdlo_done, stt_done, kvlo_done, tlo_done, prod_done, red_done, x3_done, xn_done, lg_done, wT_done, y_done):
            dve.sem_inc(s, START)
        norm_stats(0)
        norm_shift(0)
        dve.wait_ge(const_in, 16 * 6)
        add_skip(0, 0)
        cut_t(0, 0)
        cut_kv(0, 0)
        nc.vector.tensor_scalar(gb[:], vecs[:, V_BSD:V_BSD + KT], keep["gains"][:, 3:4], None, ALU.mult).then_inc(gb_done, 1)
        dve.wait_ge(setup_hi, 2)
        nc.vector.tensor_tensor(bd_lo[:], bd_raw, f32(bd_hi[:]), ALU.subtract).then_inc(setup_lo, 1)
        nc.vector.tensor_tensor(wr_lo[:], wr_raw, f32(wr_hi[:]), ALU.subtract).then_inc(setup_lo, 1)
        for u in range(CHD * KT):
            unit(0, u, first[u % 2])
        add_x2(0)
        nat_stats(0, 0)
        nat_stats(0, 1)
        cut_xn(0, 0)
        cut_xn(0, 1)
        route(0)

        def round_(g, q):
            for s in range(STEPS):
                units = UNITS.get(s, []) if q is not None else []
                if q is not None and s == 13:
                    add_x2(q)
                if s == 0:
                    cut_wT(g)
                    if q is not None:
                        norm_stats(q)
                gated(g, s)
                if q is not None and s == 0:
                    norm_shift(q)
                if q is not None and s == 2:
                    cut_kv(q, 0)
                if units and s > FIRST_UNIT_STEP:
                    unit(q, units[0])
                if q is not None and s == STEPS - 1:
                    cut_xn(q, 0)
                cut_hd(g, s)
                if q is not None and s == 1:
                    add_skip(q, 0)
                    cut_t(q, 0)
                if units and s == FIRST_UNIT_STEP:
                    unit(q, units[0])
                if len(units) > 1:
                    unit(q, units[1])
                if q is not None and s in (13, 14):
                    nat_stats(q, s - 13)
                if q is not None and s == STEPS - 1:
                    cut_xn(q, 1)
            finish(g)
            if q is not None:
                route(q)

        with dve.Fori(0, NCH - 1) as g:
            round_(g, g + 1)
        round_(NCH - 1, None)

    @block.tensor
    def _(pe):
        ident = keep["ident"]

        def gate(g, s):
            pe.wait_ge(gulo_done, START + STEPS * g + s + 1)
            if s == 0:
                pe.wait_ge(xn_done, START + 2 * (g + 1))
            if routed(s):
                pe.wait_ge(silu_done, START + STEPS * g + s)
                for k in range(KT):
                    last = products(nc, ps_g[:], gu_hi[:, s % 2, 0, k], gu_lo[:, s % 2, 0, k], xn_hi[:, k], xn_lo[:, k], k == 0, k == KT - 1)
                last.then_inc(gate_done, 1)

        def up(g, s):
            if s > RSTEPS:
                pe.wait_ge(silu_done, START + STEPS * g + s)
            else:
                pe.wait_ge(stt_done, START + RSTEPS * g + s)
            if s == 0:
                pe.wait_ge(silu_done, START + STEPS * g)
            for k in range(KT):
                last = products(nc, ps_u[:], gu_hi[:, s % 2, 1, k], gu_lo[:, s % 2, 1, k], xn_hi[:, k], xn_lo[:, k], k == 0, k == KT - 1)
            last.then_inc(gu_done, 1)

        def bias(g):
            pe.wait_ge(y_done, START + 4 * g)
            pe.wait_ge(wT_done, START + g + 1)
            for k in range(KT):
                col = slice(k * P, (k + 1) * P)
                products(nc, ps_out[:, k], bd_hi[:, col], bd_lo[:, col], wT_hi[:], wT_lo[:], True, False, skip=True)

        def down(g, s):
            n = STEPS * g + s
            pe.wait_ge(hdlo_done, START + n + 1)
            pe.wait_ge(dnlo_done, START + n + 1)
            for k in range(KT):
                col = slice(k * P, (k + 1) * P)
                last = products(nc, ps_out[:, k], dn_hi[:, s % 2, col], dn_lo[:, s % 2, col], hd_hi[:, s % 2], hd_lo[:, s % 2], False,
                                s == STEPS - 1, skip=True)
            last.then_inc(down_done, 1)

        def turn_x2(q, a, after):
            pe.wait_ge(x_in, 16 * TJ * (q + 1))
            pe.wait_ge(*after)
            for kk in range(2):
                for j in range(TJ):
                    k = 2 * a + kk
                    last = nc.tensor.transpose(ps_m[:, kk, j * P:(j + 1) * P], x[:, j, k * P:(k + 1) * P], ident[:])
            last.then_inc(x2T_filled, 1)

        def turn_q(q, a, after):
            pe.wait_ge(xq_done, START + 4 * (q + 1))
            pe.wait_ge(*after)
            for kk in range(2):
                for j in range(TJ):
                    k = 2 * a + kk
                    last = nc.tensor.transpose(ps_m[:, kk, j * P:(j + 1) * P], xq[:, j, k * P:(k + 1) * P], ident[:])
            last.then_inc(q_filled, 1)

        def unit(q, u, after, out=ps_m[:]):
            hh, lb = u // KT, u % KT
            v = CHD * KT * q + u
            if u > 0 and after is None:
                after = (prod_done, START + 4 * v)
            units = out.rearrange("p a (b n) -> p (a b) n", n=64)
            pe.wait_ge(kvlo_done, START + v + 1)
            pe.wait_ge(tlo_done, START + CHD * q + hh + 1)
            pe.wait_ge(*after)
            for half in range(2):
                bs = slice(half * B // 2, (half + 1) * B // 2)
                for m in range(lb + 1):
                    t = slice((lb - m) * P, (lb - m + 1) * P)
                    last = products(nc, units[:, bs, 0:PAIRS], t_hi[:, t], t_lo[:, t], kv_hi[:, m, bs], kv_lo[:, m, bs], m == 0, m == lb)
            last.then_inc(unit_done, 1)

        def turn_x3(q, a, after):
            pe.wait_ge(x3_done, START + q + 1)
            pe.wait_ge(*after)
            for jj in range(2):
                for k in range(KT):
                    j = 2 * a + jj
                    last = nc.tensor.transpose(ps_m[:, jj, k * P:(k + 1) * P], x3T[:, k, j * P:(j + 1) * P], ident[:])
            last.then_inc(nat_filled, 1)

        def turn_xn(q, a, after):
            pe.wait_ge(xnat_done, START + 4 * (q + 1))
            pe.wait_ge(*after)
            for kk in range(2):
                for j in range(TJ):
                    k = 2 * a + kk
                    last = nc.tensor.transpose(ps_m[:, kk, j * P:(j + 1) * P], xnat[:, j, k * P:(k + 1) * P], ident[:])
            last.then_inc(xnT_filled, 1)

        def logits(q):
            pe.wait_ge(xn_done, START + 2 * (q + 1))
            for k in range(KT):
                last = products(nc, ps_m[0:8, 0], wr_hi[:, k], wr_lo[:, k], xn_hi[:, k], xn_lo[:, k], k == 0, k == KT - 1)
            last.then_inc(lgT_filled, 1)
            pe.wait_ge(lgT_done, q + 1)
            for j in range(TJ):
                last = nc.tensor.matmul(ps_m[:, 1, 8 * j:8 * j + 8], lgT[:, j * P:(j + 1) * P], ident[0:8, 0:8], start=True, stop=True)
            last.then_inc(lg_filled, 1)

        def turn_w(g):
            pe.wait_ge(w_done, g + 1)
            for j in range(TJ):
                last = nc.tensor.transpose(ps_m[0:8, 0, j * P:(j + 1) * P], w[:, j], ident[:])
            last.then_inc(wT_filled, 1)

        def spread(g, a, after):
            pe.wait_ge(wT_done, START + g + 1)
            pe.wait_ge(*after)
            for e in range(2):
                nc.tensor.matmul(ps_m[:, e], sel[:, (2 * a + e) * P:(2 * a + e + 1) * P], wT_hi[:], start=True, stop=False)
                last = nc.tensor.matmul(ps_m[:, e], sel[:, (2 * a + e) * P:(2 * a + e + 1) * P], wT_lo[:], start=False, stop=True)
            last.then_inc(wb_filled, 1)

        for s in (gu_done, down_done, unit_done, q_filled, xnT_filled):
            pe.sem_inc(s, START)
        turn_x2(0, 0, (x2T_done, START))
        turn_x2(0, 1, (x2T_done, START + 1))
        turn_q(0, 0, (x2T_done, START + 2))
        turn_q(0, 1, (qe_done, START + 2))
        for u in range(CHD * KT):
            unit(0, u, (qe_done, START + 4) if u == 0 else (prod_done, START + 4 * (u - 1)), first[u % 2])
        pe.wait_ge(setup_lo, 2)
        pe.wait_ge(setup_hi, 3)
        turn_x3(0, 0, (prod_done, START + 4 * CHD * KT))
        turn_x3(0, 1, (xnat_done, START + 2))
        turn_xn(0, 0, (xnat_done, START + 4))
        turn_xn(0, 1, (xn_done, START + 1))
        logits(0)

        def round_(g, q):
            for s in range(STEPS):
                units = UNITS.get(s, []) if q is not None else []
                gate(g, s)
                if s == 1:
                    spread(g, 0, (wT_done, START + g + 1))
                    if q is not None:
                        turn_x2(q, 0, (wb_done, START + 3 * g + 1))
                    bias(g)
                    if q is not None:
                        turn_x2(q, 1, (x2T_done, START + 2 * q + 1))
                if q is not None and s == 2:
                    turn_q(q, 0, (wb_done, START + 3 * g + 3))
                up(g, s)
                if s == 0:
                    turn_w(g)
                if s == 1:
                    spread(g, 1, (x2T_done, START + 2 * q + 2) if q is not None else (wb_done, START + 3 * g + 1))
                if q is not None and s == 2:
                    turn_q(q, 1, (qe_done, START + 4 * q + 2))
                if units and s > FIRST_UNIT_STEP:
                    unit(q, units[0], None)
                if q is not None and s == 14:
                    turn_x3(q, 1, (xnat_done, START + 4 * q + 2))
                if q is not None and s == STEPS - 1:
                    turn_xn(q, 0, (xnat_done, START + 4 * q + 4))
                if s > 0:
                    down(g, s - 1)
                if s == 1:
                    spread(g, 2, (wb_done, START + 3 * g + 2))
                if units and s == FIRST_UNIT_STEP:
                    unit(q, units[0], (qe_done, START + 4 * q + 4))
                if len(units) > 1:
                    unit(q, units[1], None)
                if q is not None and s == 13:
                    turn_x3(q, 0, (prod_done, START + 4 * CHD * KT * (q + 1)))
                if q is not None and s == STEPS - 1:
                    turn_xn(q, 1, (xn_done, START + 2 * q + 1))
            down(g, STEPS - 1)
            if q is not None:
                logits(q)

        with pe.Fori(0, NCH - 1) as g:
            round_(g, g + 1)
        round_(NCH - 1, None)

    st.close()


def expert_constants(np):
    own, other = np.meshgrid(np.arange(8), np.arange(8), indexing="ij")
    rep = lambda m: np.broadcast_to(m.astype(np.float32).reshape(1, 1, 64), (P, 4, 64)).reshape(P, 256)
    sel = np.zeros((8, NE * P), np.float32)
    for e in range(NE):
        sel[e, e * P:(e + 1) * P] = 1.0
    return {"sel": sel, "below": rep(other < own), "above": rep(other > own)}


def build(nc, dram):
    with ExitStack() as ctx:
        sb = lambda n, s, d=F32: ctx.enter_context(nc.sbuf_tensor(n, s, d))
        keep = {"vecs": sb("vecs", [P, V_COLS]), "gains": sb("gains", [P, 4]), "ident": sb("ident", [P, P]),
                "identb": sb("identb", [P, P], BF16), "wmean": sb("wmean", [P, 2])}
        attn = ctx.enter_context(ExitStack())
        at = lambda n, s, d=F32: attn.enter_context(nc.sbuf_tensor(n, s, d))
        keep.update({"at_hi": at("at_hi", [P, HEADS, CH], F32R), "at_lo": at("at_lo", [P, HEADS, CH], F32R),
                     "wo_hi": at("wo_hi", [P, KT, D], F32R), "wo_lo": at("wo_lo", [P, KT, D], F32R),
                     "w1q": at("w1q", [P, KT, HID], BF16), "w2q": at("w2q", [P, HT, D], BF16), "gam": at("gam", [P, D]),
                     "stage": at("stage", [P, TJ, D])})
        sc = ctx.enter_context(ExitStack())
        at = lambda n, s, d=F32: sc.enter_context(nc.sbuf_tensor(n, s, d))
        keep.update({"wg_hi": at("wg_hi", [P, KT, D], F32R), "wg_lo": at("wg_lo", [P, KT, D], F32R),
                     "wh_hi": at("wh_hi", [P, HEADS, P], F32R), "wh_lo": at("wh_lo", [P, HEADS, P], F32R),
                     "g_hi": at("g_hi", [P, HEADS, P], F32R), "g_lo": at("g_lo", [P, HEADS, P], F32R),
                     "mask": at("mask", [P, HEADS, CH])})
        setup_block(nc, ctx, dram, keep)
        scores_block(nc, ctx, dram, keep)
        sc.close()
        attn_block(nc, ctx, dram, keep)
        attn.close()
        experts_block(nc, ctx, dram, keep)


def decay_mask(np):
    gam = 1.0 - 2.0 ** (-5.0 - np.arange(HEADS))
    expo = (np.arange(S)[None, :] - np.arange(S)[:, None]).astype(np.float64)
    d = np.where(expo[None] <= 0, gam[:, None, None] ** np.minimum(expo[None], 0), 0.0)
    d = d / np.sqrt(d.sum(-1))[:, None, :] / np.sqrt(P)
    return np.ascontiguousarray(d.reshape(HEADS, S, 2, P).transpose(3, 0, 2, 1).reshape(P, HEADS, CH)).astype(np.float32)


def kernel(**inputs):
    import numpy as np
    import concourse.bacc as bacc
    from concourse import mybir as mb
    from concourse.bass_utils import run_bass_kernel_spmd

    a = {k: np.asarray(v) for k, v in inputs.items()}
    lay = np.ascontiguousarray
    ctx_t = a["ctx_2048"].reshape(B * S, D).T
    gains = [a["g_xattn"][0:1], a["g_xattn"][1:2], a["g_ffn"][0:1], a["g_ffn"][1:2], ]
    cols = lambda v: v.reshape(-1, P).T
    rows = lambda v: np.broadcast_to(v.reshape(1, -1), (P, v.size))
    vecs = np.concatenate([rows(g) for g in gains] + [
        cols(a["L0_xattn_gn_gamma"]), cols(a["L0_xattn_gn_beta"]), cols(a["L1_ffn_bgate"]), cols(a["L1_ffn_bup"]),
        cols(a["L1_ffn_bs_up"]), cols(a["L1_ffn_bs_down"]), rows(a["L1_ffn_bg"])], axis=1)
    ctx_g = a["ctx_2048"].reshape(B, NCH, S // NCH, D).transpose(1, 3, 0, 2).reshape(NCH, D, CH)
    padded = np.concatenate([np.zeros((S // CD, P), np.float32), a["L1_xattn_ssm_kernel"]], axis=1)
    toep = np.stack([padded[:, P - m:P - m + D] for m in range(P)], axis=1)
    tiles = lambda w, n: w.reshape(KT, P, n, P).transpose(2, 1, 0, 3).reshape(n, P, D)
    of = lambda w: np.concatenate([tiles(w[e], EH // P) for e in range(NE)])
    mgu = np.stack([of(a["L1_ffn_Wgate"]), of(a["L1_ffn_Wup"])], axis=2).reshape(RSTEPS, P, 2 * D)
    md = np.concatenate([a["L1_ffn_Wdown"].reshape(RSTEPS, P, D), a["L1_ffn_Ws_down"].reshape(SH // P, P, D)])
    bdown = np.concatenate([a["L1_ffn_bdown"], np.zeros((2, D), np.float32)])
    arrays = {
        "x": a["x"].reshape(B * S, D), "ctxT": ctx_t, "ctxG": ctx_g, "toep": toep,
        "skipD": rows(a["L1_xattn_D"]),
        "wh": a["L0_xattn_Wh"], "whT": a["L0_xattn_Wh"].transpose(0, 2, 1), "wg": a["L0_xattn_wg_w"],
        "wo": a["L0_xattn_wo_w"], "w1T": a["L0_ffn_w1"].T, "w2T": a["L0_ffn_w2"].T, "vecs": vecs,
        "gam": rows(a["L0_ffn_gamma"]), "ident": np.eye(P, dtype=np.float32), "mask": decay_mask(np),
        "mgu": mgu, "msu": tiles(a["L1_ffn_Ws_up"], SH // P), "md": md,
        "wroute": a["L1_ffn_Wg"].reshape(KT, P, 8).transpose(1, 0, 2), "bdown": bdown, **expert_constants(np),
    }
    arrays = {"in_" + n: lay(v) for n, v in arrays.items()}
    nc = bacc.Bacc("TRN2", target_bir_lowering=False, num_devices=1)
    dram = {n[3:]: nc.dram_tensor(n, v.shape, mb.dt.from_np(v.dtype), kind="ExternalInput").ap() for n, v in arrays.items()}
    dram["gates"] = nc.dram_tensor("gates", (NCH, P, KT, CH), mb.dt.float32, kind="Internal").ap()
    dram["vals"] = nc.dram_tensor("vals", (NCH, P, TJ, D), mb.dt.float32, kind="Internal").ap()
    dram["x2"] = nc.dram_tensor("x2", (B * S, D), mb.dt.float32, kind="Internal").ap()
    dram["out"] = nc.dram_tensor("out", (NCH, D, CH), mb.dt.float32, kind="ExternalOutput").ap()
    build(nc, dram)
    got = run_bass_kernel_spmd(nc, [arrays], core_ids=[0]).results[0]["out"]
    return lay(got.reshape(NCH, D, B, S // NCH).transpose(2, 0, 3, 1).reshape(B, S, D))
```
